# Optimizing a Trainium2 kernel written in Bass

```python
import numpy as np
import jax
import jax.numpy as jnp

def _softmax(x, axis=-1):
    return jax.nn.softmax(x, axis=axis)

def _gelu(x):
    return jax.nn.gelu(x, approximate=True)

def _silu(x):
    return jax.nn.silu(x)

def _sigmoid(x):
    return jax.nn.sigmoid(x)

def _layernorm(x, axis=-1, eps=1e-05):
    m = jnp.mean(x, axis=axis, keepdims=True)
    v = jnp.var(x, axis=axis, keepdims=True)
    return (x - m) / jnp.sqrt(v + eps)

def _scatter_add(tgt, idx, src, axis=0):
    return tgt.at[idx].add(src)

def _segment_sum(src, seg, n):
    return jax.ops.segment_sum(src, seg, n)
kernel_name = 'mk_seq_preln_d1_jaxref_r4_5066b4'

def setup_inputs(seed: int=0):
    np.random.seed(seed)
    _w = jnp.asarray

    def _L0_attn_setup():
        import jax, jax.numpy as jnp
        import numpy as np
        D_MODEL = 512
        D_INNER = 512
        D_XB = 128
        D_STATE = 32
        DT_RANK = 128
        D_FF = 1408
        BATCH = 2
        SEQ = 256
        EPS = 1e-05

        def _rmsnorm(x, w):
            var = jnp.mean(jnp.square(x), axis=-1, keepdims=True)
            return x * jax.lax.rsqrt(var + EPS) * w

        def _selective_scan(x, dt, A, B, C):
            b, l, g, p = x.shape
            n = A.shape[-1]

            def step(h, inp):
                x_t, dt_t, B_t, C_t = inp
                dA = jnp.exp(dt_t[..., None] * A)
                h = dA * h + (dt_t * x_t)[..., None] * B_t[:, :, None, :]
                y = jnp.einsum('bgpn,bgn->bgp', h, C_t)
                return (h, y)
            h0 = jnp.zeros((b, g, p, n), x.dtype)
            xs = tuple((jnp.moveaxis(a, 1, 0) for a in (x, dt, B, C)))
            _, ys = jax.lax.scan(step, h0, xs)
            return jnp.moveaxis(ys, 0, 1)

        def _mamba(u, in_proj_w, dt_proj_w, dt_proj_b, A_log, D_param, out_proj_w):
            b, l, _ = u.shape
            zxbcdt = u @ in_proj_w.T
            splits = np.cumsum([D_INNER, D_XB, D_XB, D_INNER]).tolist()
            z, x, Bc, Cc, dt_raw = jnp.split(zxbcdt, splits, axis=-1)
            dt = jax.nn.softplus(dt_raw @ dt_proj_w.T + dt_proj_b)
            g = D_INNER // D_STATE
            g_kv = D_XB // D_STATE
            rep = g // g_kv
            x = jnp.repeat(x.reshape(b, l, g_kv, D_STATE), rep, axis=2)
            Bm = jnp.repeat(Bc.reshape(b, l, g_kv, D_STATE), rep, axis=2)
            Cm = Cc.reshape(b, l, g, D_STATE)
            A = -jnp.exp(A_log).reshape(g, D_STATE, D_STATE)
            dt = dt.reshape(b, l, g, D_STATE)
            y = _selective_scan(x, dt, A, Bm, Cm).reshape(b, l, D_INNER)
            y = y + x.reshape(b, l, D_INNER) * D_param
            y = y * jax.nn.silu(z)
            return y @ out_proj_w.T

        def _forward(hidden_states, in_proj_w, dt_proj_w, dt_proj_b, A_log, D_param, out_proj_w, gate_w, up_w, down_w, norm1_w, norm2_w):
            h = hidden_states + _mamba(_rmsnorm(hidden_states, norm1_w), in_proj_w, dt_proj_w, dt_proj_b, A_log, D_param, out_proj_w)
            xn = _rmsnorm(h, norm2_w)
            mlp = jax.nn.silu(xn @ gate_w.T) * (xn @ up_w.T) @ down_w.T
            return h + mlp
        key = jax.random.key(seed)
        ks = jax.random.split(key, 8)
        s = lambda k, shape, scale=0.02: jax.random.normal(k, shape, jnp.float32) * scale
        proj_dim = 2 * D_INNER + 2 * D_XB + DT_RANK
        return {'hidden_states': jax.random.normal(ks[0], (BATCH, SEQ, D_MODEL), jnp.float32), 'in_proj_w': s(ks[1], (proj_dim, D_MODEL)), 'dt_proj_w': s(ks[2], (D_INNER, DT_RANK)), 'dt_proj_b': jnp.full((D_INNER,), -4.6, jnp.float32), 'A_log': jnp.log(jnp.tile(jnp.arange(1, D_STATE + 1, dtype=jnp.float32), (D_INNER, 1))), 'D_param': jnp.ones((D_INNER,), jnp.float32), 'out_proj_w': s(ks[3], (D_MODEL, D_INNER)), 'gate_w': s(ks[4], (D_FF, D_MODEL)), 'up_w': s(ks[5], (D_FF, D_MODEL)), 'down_w': s(ks[6], (D_MODEL, D_FF)), 'norm1_w': jnp.ones((D_MODEL,), jnp.float32), 'norm2_w': jnp.ones((D_MODEL,), jnp.float32)}
    _L0_attn_in = _L0_attn_setup()

    def _L0_ffn_setup():
        import jax, jax.numpy as jnp
        import numpy as np
        N_HEAD = 16
        N_EMBD = 512
        R = 8
        HEAD_DIM = N_EMBD // N_HEAD
        D_STD = HEAD_DIM - R
        THRESHOLD = 0.1
        B, T = (4, 256)
        key = jax.random.key(seed)
        k1, k2, k3, k4, k5 = jax.random.split(key, 5)
        fused_dim = 2 * N_HEAD * D_STD + N_EMBD + 2 * N_HEAD * R
        x = jax.random.normal(k1, (B, T, N_EMBD), dtype=jnp.float32)
        Wa = jax.random.normal(k2, (N_EMBD, fused_dim), dtype=jnp.float32) * 0.02
        Wp = jax.random.normal(k3, (N_EMBD, N_EMBD), dtype=jnp.float32) * 0.02
        w_std = jax.random.uniform(k4, (N_HEAD,), dtype=jnp.float32, minval=0.3, maxval=0.7)
        w_rec = jax.random.uniform(k5, (N_HEAD,), dtype=jnp.float32)
        return {'x': x, 'Wa': Wa, 'Wp': Wp, 'w_std': w_std, 'w_rec': w_rec}
    _L0_ffn_in = _L0_ffn_setup()
    _d = {'L0_attn_hidden_states': _L0_attn_in['hidden_states'], 'L0_attn_in_proj_w': _L0_attn_in['in_proj_w'], 'L0_attn_dt_proj_w': _L0_attn_in['dt_proj_w'], 'L0_attn_dt_proj_b': _L0_attn_in['dt_proj_b'], 'L0_attn_A_log': _L0_attn_in['A_log'], 'L0_attn_D_param': _L0_attn_in['D_param'], 'L0_attn_out_proj_w': _L0_attn_in['out_proj_w'], 'L0_attn_gate_w': _L0_attn_in['gate_w'], 'L0_attn_up_w': _L0_attn_in['up_w'], 'L0_attn_down_w': _L0_attn_in['down_w'], 'L0_attn_norm1_w': _L0_attn_in['norm1_w'], 'L0_attn_norm2_w': _L0_attn_in['norm2_w'], 'L0_ffn_Wa': _L0_ffn_in['Wa'], 'L0_ffn_Wp': _L0_ffn_in['Wp'], 'L0_ffn_w_std': _L0_ffn_in['w_std'], 'L0_ffn_w_rec': _L0_ffn_in['w_rec']}
    _x0 = _d['L0_attn_hidden_states']
    _d['L0_attn_hidden_states'] = jax.random.normal(jax.random.fold_in(jax.random.key(seed), 1), (4, 1024, 512), dtype=_x0.dtype)
    del _x0
    return _d

def reference(L0_attn_hidden_states, L0_attn_in_proj_w, L0_attn_dt_proj_w, L0_attn_dt_proj_b, L0_attn_A_log, L0_attn_D_param, L0_attn_out_proj_w, L0_attn_gate_w, L0_attn_up_w, L0_attn_down_w, L0_attn_norm1_w, L0_attn_norm2_w, L0_ffn_Wa, L0_ffn_Wp, L0_ffn_w_std, L0_ffn_w_rec):

    def _L0_attn_ref(hidden_states, in_proj_w, dt_proj_w, dt_proj_b, A_log, D_param, out_proj_w, gate_w, up_w, down_w, norm1_w, norm2_w):
        import jax, jax.numpy as jnp
        import numpy as np
        D_MODEL = 512
        D_INNER = 512
        D_XB = 128
        D_STATE = 32
        DT_RANK = 128
        D_FF = 1408
        BATCH = 2
        SEQ = 256
        EPS = 1e-05

        def _rmsnorm(x, w):
            var = jnp.mean(jnp.square(x), axis=-1, keepdims=True)
            return x * jax.lax.rsqrt(var + EPS) * w

        def _selective_scan(x, dt, A, B, C):
            b, l, g, p = x.shape
            n = A.shape[-1]

            def step(h, inp):
                x_t, dt_t, B_t, C_t = inp
                dA = jnp.exp(dt_t[..., None] * A)
                h = dA * h + (dt_t * x_t)[..., None] * B_t[:, :, None, :]
                y = jnp.einsum('bgpn,bgn->bgp', h, C_t)
                return (h, y)
            h0 = jnp.zeros((b, g, p, n), x.dtype)
            xs = tuple((jnp.moveaxis(a, 1, 0) for a in (x, dt, B, C)))
            _, ys = jax.lax.scan(step, h0, xs)
            return jnp.moveaxis(ys, 0, 1)

        def _mamba(u, in_proj_w, dt_proj_w, dt_proj_b, A_log, D_param, out_proj_w):
            b, l, _ = u.shape
            zxbcdt = u @ in_proj_w.T
            splits = np.cumsum([D_INNER, D_XB, D_XB, D_INNER]).tolist()
            z, x, Bc, Cc, dt_raw = jnp.split(zxbcdt, splits, axis=-1)
            dt = jax.nn.softplus(dt_raw @ dt_proj_w.T + dt_proj_b)
            g = D_INNER // D_STATE
            g_kv = D_XB // D_STATE
            rep = g // g_kv
            x = jnp.repeat(x.reshape(b, l, g_kv, D_STATE), rep, axis=2)
            Bm = jnp.repeat(Bc.reshape(b, l, g_kv, D_STATE), rep, axis=2)
            Cm = Cc.reshape(b, l, g, D_STATE)
            A = -jnp.exp(A_log).reshape(g, D_STATE, D_STATE)
            dt = dt.reshape(b, l, g, D_STATE)
            y = _selective_scan(x, dt, A, Bm, Cm).reshape(b, l, D_INNER)
            y = y + x.reshape(b, l, D_INNER) * D_param
            y = y * jax.nn.silu(z)
            return y @ out_proj_w.T

        def _forward(hidden_states, in_proj_w, dt_proj_w, dt_proj_b, A_log, D_param, out_proj_w, gate_w, up_w, down_w, norm1_w, norm2_w):
            h = hidden_states + _mamba(_rmsnorm(hidden_states, norm1_w), in_proj_w, dt_proj_w, dt_proj_b, A_log, D_param, out_proj_w)
            xn = _rmsnorm(h, norm2_w)
            mlp = jax.nn.silu(xn @ gate_w.T) * (xn @ up_w.T) @ down_w.T
            return h + mlp
        return _forward(hidden_states, in_proj_w, dt_proj_w, dt_proj_b, A_log, D_param, out_proj_w, gate_w, up_w, down_w, norm1_w, norm2_w)

    def _L0_ffn_ref(x, Wa, Wp, w_std, w_rec):
        import jax, jax.numpy as jnp
        import numpy as np
        N_HEAD = 16
        N_EMBD = 512
        R = 8
        HEAD_DIM = N_EMBD // N_HEAD
        D_STD = HEAD_DIM - R
        THRESHOLD = 0.1
        B, T = (4, 256)
        Bx, Tx, C = x.shape
        H, D, Ds, r = (N_HEAD, HEAD_DIM, D_STD, R)
        s_std = jnp.sqrt(jnp.clip(w_std, 1e-08, None))
        s_rec = jnp.sqrt(jnp.clip(w_rec, 1e-08, None))
        col_scale = jnp.concatenate([jnp.repeat(s_std, Ds), jnp.repeat(s_std, Ds), jnp.ones((C,), dtype=x.dtype), jnp.repeat(s_rec, r), jnp.repeat(s_rec, r)])
        Wb = Wa * col_scale[None, :]
        fused = x @ Wb
        q_std_end = H * Ds
        k_std_end = q_std_end + H * Ds
        v_end = k_std_end + C
        q_low_end = v_end + H * r

        def heads(t, d):
            return t.reshape(Bx, Tx, H, d).transpose(0, 2, 1, 3)
        Q_std = heads(fused[..., :q_std_end], Ds)
        K_std = heads(fused[..., q_std_end:k_std_end], Ds)
        V = heads(fused[..., k_std_end:v_end], D)
        Q_low = heads(fused[..., v_end:q_low_end], r)
        K_low = heads(fused[..., q_low_end:], r)
        use_ra = (w_rec > THRESHOLD)[None, :, None, None]
        q_tail = jnp.where(use_ra, K_low, Q_low)
        k_tail = jnp.where(use_ra, Q_low, K_low)
        Qf = jnp.concatenate([Q_std, q_tail], axis=-1)
        Kf = jnp.concatenate([K_std, k_tail], axis=-1)
        scale = 1.0 / jnp.sqrt(jnp.asarray(D, dtype=x.dtype))
        scores = jnp.einsum('bhtd,bhsd->bhts', Qf, Kf) * scale
        causal = jnp.tril(jnp.ones((Tx, Tx), dtype=bool))
        scores = jnp.where(causal[None, None], scores, jnp.finfo(scores.dtype).min)
        attn = jax.nn.softmax(scores, axis=-1)
        out = jnp.einsum('bhts,bhsd->bhtd', attn, V)
        y = out.transpose(0, 2, 1, 3).reshape(Bx, Tx, C)
        return y @ Wp
    x = L0_attn_hidden_states
    x = x + _L0_attn_ref(_layernorm(x, axis=-1), L0_attn_in_proj_w, L0_attn_dt_proj_w, L0_attn_dt_proj_b, L0_attn_A_log, L0_attn_D_param, L0_attn_out_proj_w, L0_attn_gate_w, L0_attn_up_w, L0_attn_down_w, L0_attn_norm1_w, L0_attn_norm2_w)
    x = x + _L0_ffn_ref(_layernorm(x, axis=-1), L0_ffn_Wa, L0_ffn_Wp, L0_ffn_w_std, L0_ffn_w_rec)
    return x

_drawn_inputs = setup_inputs


def setup_inputs(seed=0):
    import zlib

    import numpy as np

    out = dict(_drawn_inputs(seed))
    spreads = {'L0_attn_dt_proj_b': (-4.599999904632568, 0.6),
     'L0_attn_D_param': (1.0, 0.6),
     'L0_attn_norm1_w': (1.0, 0.6),
     'L0_attn_norm2_w': (1.0, 0.6)}
    factors = {'L0_attn_dt_proj_w': 8.0,
     'L0_attn_A_log': 8.0,
     'L0_ffn_Wa': 6.525,
     'L0_ffn_Wp': 6.49,
     'L0_ffn_w_std': 8.0,
     'L0_ffn_w_rec': 8.0}
    for name, (base, spread) in spreads.items():
        noise = np.random.default_rng([zlib.crc32(name.encode()), seed]).standard_normal(out[name].shape)
        drawn = base * np.exp(spread * noise) if base else spread * noise
        out[name] = jnp.asarray(drawn.astype(out[name].dtype))
    for name, factor in factors.items():
        out[name] = (out[name] * factor).astype(out[name].dtype)
    return out
```

```python
from contextlib import ExitStack

import concourse.bass as bass
from concourse import mybir

F32 = mybir.dt.float32
F32R = mybir.dt.float32r
BF16 = mybir.dt.bfloat16
ALU = mybir.AluOpType
ACT = mybir.ActivationFunctionType
AX_X = mybir.AxisListType.X

P = 128
EPS = 1e-5
BATCH, SEQ, DM = 4, 1024, 512
NC = DM // P
STATE = 32
REP = 4
FF = 1408
NF = FF // P
TT = 512
NT = BATCH * SEQ // TT
NS = TT // P
UP = SEQ // TT
HEADS, HD = 16, 32


def rolled(eng, first, period, total, emit, tail=0):
    n = (total - first - tail) // period
    for v in range(first):
        emit(0, v)
    with eng.Fori(0, n) as j:
        for v in range(first, first + period):
            emit(j, v)
    for v in range(first + n * period, total):
        emit(0, v)


def split_weight(nc, dve, ready, n, head, tail, full):
    nc.vector.tensor_copy(head, full).then_inc(ready, 1)
    dve.wait_ge(ready, n + 1)
    nc.vector.tensor_tensor(tail, full, head.bitcast(F32), ALU.subtract).then_inc(ready, 1)


def products3(nc, out, w_head, w_tail, x_head, x_tail, first, last):
    nc.tensor.matmul(out, w_head, x_head, start=first, stop=False)
    nc.tensor.matmul(out, w_head, x_tail, start=False, stop=False)
    return nc.tensor.matmul(out, w_tail, x_head, start=False, stop=last)


def stage1(nc, d, persist):
    ident, mean_all, rstd_all = persist["ident"], persist["mean_all"], persist["rstd_all"]
    x_v = d["x"].rearrange("(b u s p) c -> b u p s c", b=BATCH, u=UP, p=P)
    ORDER = [10, 4, 5, 6, 7, 8, 9, None, None, None, None, 0, 1, 2, 3]
    NOUT = len(ORDER)
    USES = [sum(1 for k in range(NOUT) if k % 4 == b) for b in range(4)]

    with ExitStack() as ctx:
        sb = lambda name, shape, dt=F32: ctx.enter_context(nc.sbuf_tensor("s1_" + name, shape, dt))
        ps = lambda name, shape, dt=F32: ctx.enter_context(nc.psum_tensor("s1_" + name, shape, dt))
        sem = lambda name: ctx.enter_context(nc.semaphore("s1_" + name))
        w_head = sb("in_w_head", [P, NC, FF], F32R)
        w_tail = sb("in_w_tail", [P, NC, FF], F32R)
        dtw_head = sb("dt_w_head", [P, DM], F32R)
        dtw_tail = sb("dt_w_tail", [P, DM], F32R)
        norm1 = sb("norm1", [P, NC])
        dt_bias = sb("dt_bias", [P, NC])
        xb = sb("x_rows", [P, 2, NS, DM])
        uh = sb("u_rows", [P, NS, DM])
        u_head = sb("u_head", [P, NC, TT], F32R)
        u_tail = sb("u_tail", [P, NC, TT], F32R)
        stats = sb("stats", [P, NS, 6])
        mom = sb("moments", [P, NS, 2])
        var_eps = sb("var_eps", [P, NS])
        std1 = sb("std1", [P, NS])
        rstd1 = sb("rstd1", [P, NS])
        ms2 = sb("ms2", [P, NS])
        std2 = sb("std2", [P, NS])
        rstd2 = sb("rstd2", [P, NS])
        scale12 = sb("scale12", [P, NS])
        dtr_head = sb("dt_raw_head", [P, TT], F32R)
        dtr_tail = sb("dt_raw_tail", [P, TT], F32R)
        x_ch = sb("x_channels", [P, TT])
        x_rep = sb("x_repeated", [P, NC, TT])
        bcz = sb("bcz", [P, 9, TT])
        mag = sb("magnitude", [P, NC, TT])
        pos = sb("positive", [P, NC, TT])
        one_e = sb("one_plus_e", [P, NC, TT])
        log_w = sb("log_w", [P, NC, TT])
        inv_w = sb("inv_w", [P, NC, TT])
        parts = sb("parts", [P, 4, NC * TT])
        w_full = parts[:, :, :].rearrange("p a n -> p (a n)")[:, 0:NC * FF].rearrange("p (c m) -> p c m", c=NC)
        dtw_full = parts[:, 3, NC * TT - DM:NC * TT]
        u_ps = ps("u_ps", [P, NC, TT])
        o_ps = ps("o_ps", [P, 4, TT])

        w_loaded, w_ready = sem("w_loaded"), sem("w_ready")
        sp_passed, dve_passed = sem("sp_passed"), sem("dve_passed")
        x_loaded = [sem("x_loaded0"), sem("x_loaded1")]
        stats_done, mom_done, var_done, std1_done, rstd1_done = (
            sem("stats"), sem("moments"), sem("var_eps"), sem("std1"), sem("rstd1"))
        sq_done, ms_done, std2_done, rstd2_done, scale_done = (
            sem("sq"), sem("ms"), sem("std2"), sem("rstd2"), sem("scale"))
        normed = sem("normed")
        transposed = sem("transposed")
        head_done, tail_done = sem("u_head"), sem("u_tail")
        out_ready = sem("out_ready")
        o_free = [sem(f"o_free{b}") for b in range(4)]
        dtr_head_done = sem("dt_raw_head")
        x_repeated = sem("x_repeated")
        stored = [sem("stored_bc"), sem("stored_z"), sem("stored_parts"), sem("stored_x")]
        e_done, ln_masked, one_e_done, ln_done, inv_done = (
            sem("e"), sem("ln_masked"), sem("one_e"), sem("ln"), sem("inv"))
        err_done, corr_done, log1p_done, dt_done, dtx_done = (
            sem("err"), sem("corr"), sem("log1p"), sem("dt"), sem("dtx"))
        ph_done, parts_done = sem("part_heads"), sem("parts")

        by_dve, by_act = (2, 4, 6, 11, 13), (3, 5, 12, 14)

        def freed(k, t):
            return USES[k % 4] * t + k // 4 + 2

        with nc.Block() as block:
            @block.sync
            def _(sp):
                sp.dma_start(w_full, d["in_w"].rearrange("(c p) m -> p c m", p=P)).then_inc(w_loaded, 16)
                sp.dma_start(dtw_full, d["dt_w"]).then_inc(w_loaded, 16)
                sp.dma_start(norm1[:, :], d["norm1"]).then_inc(w_loaded, 16)
                sp.dma_start(dt_bias[:, :], d["dt_b"]).then_inc(w_loaded, 16)
                for u in range(2):
                    sp.dma_start(xb[:, u], x_v[0, u]).then_inc(x_loaded[u], 16)

                def step(j, v):
                    t, b, u = 2 * j + v, j + v // 2, v % 2
                    if not (isinstance(t, int) and t >= NT - 2):
                        sp.wait_ge(normed, t + 1)
                        sp.dma_start(xb[:, u], x_v[b + 1, u]).then_inc(x_loaded[u], 16)
                    tok = slice(u * TT, (u + 1) * TT)
                    sp.wait_ge(o_free[1], freed(1, t))
                    sp.wait_ge(dtx_done, t + 1)
                    for g in range(NC):
                        for r in range(REP):
                            sp.dma_start(x_rep[STATE * r:STATE * (r + 1), g, :],
                                         x_ch[STATE * g:STATE * (g + 1), :]).then_inc(x_repeated, 16)
                    sp.dma_start(d["x_s"][b, :, tok], x_ch[:, :]).then_inc(stored[3], 16)
                    for k in range(3, 7):
                        sp.wait_ge(o_free[k % 4], freed(k, t))
                        if k % 4 == 3:
                            sp.sem_inc(sp_passed, 1)
                    sp.dma_start(d["B_s"][b, :, tok], bcz[:, 0, :]).then_inc(stored[0], 16)
                    sp.dma_start(d["C_s"][b, :, :, tok].rearrange("k p t -> p k t"),
                                 bcz[:, 1:5, :]).then_inc(stored[0], 16)
                    for k in range(11, 15):
                        sp.wait_ge(o_free[k % 4], freed(k, t))
                        if k % 4 == 3:
                            sp.sem_inc(sp_passed, 1)
                    sp.dma_start(d["z_s"][b, :, :, tok].rearrange("k p t -> p k t"),
                                 bcz[:, 5:9, :]).then_inc(stored[1], 16)
                    sp.wait_ge(parts_done, t + 1)
                    for n, name in enumerate(("dt_s", "dtx_s")):
                        for part in range(2):
                            for half in range(2):
                                rows = slice(64 * part, 64 * part + 64)
                                src = parts[64 * half:64 * half + 64, 2 * n + part, :]
                                sp.dma_start(d[name][b, :, half, rows, tok].rearrange("k c t -> c k t"),
                                             src.rearrange("c (k t) -> c k t", k=NC)).then_inc(stored[2], 16)

                rolled(sp, 0, 2, NT, step, tail=2)
                sp.wait_ge(stored[3], 16 * NT)
                sp.wait_ge(stored[0], 32 * NT)
                sp.wait_ge(stored[1], 16 * NT)
                sp.wait_ge(stored[2], 128 * NT)

            @block.vector
            def _(dve):
                dve.sem_inc(tail_done, 1)
                dve.wait_ge(w_loaded, 64)
                for c in range(NC):
                    last = nc.vector.tensor_scalar(w_full[:, c, :], w_full[:, c, :], norm1[:, c:c + 1], None, ALU.mult)
                last.then_inc(w_ready, 1)
                dve.wait_ge(w_ready, 1)
                split_weight(nc, dve, w_ready, 1, w_head[:, :, :], w_tail[:, :, :], w_full)
                split_weight(nc, dve, w_ready, 3, dtw_head[:, :], dtw_tail[:, :], dtw_full)

                def norm(j, v):
                    t, u = 2 * j + v, v % 2
                    dve.wait_ge(x_loaded[u], 16 * (j + v // 2 + 1))
                    for s in range(NS):
                        last = nc.vector.bn_stats(stats[:, s, :], xb[:, u, s, :])
                    last.then_inc(stats_done, 1)
                    dve.wait_ge(stats_done, t + 1)
                    dve.sem_inc(dve_passed, 1)
                    for s in range(NS):
                        last = nc.vector.bn_aggr(mom[:, s, :], stats[:, s, :])
                    last.then_inc(mom_done, 1)
                    dve.wait_ge(mom_done, t + 1)
                    nc.vector.tensor_copy(mean_all[:, bass.ds(NS * t, NS)], mom[:, :, 0])
                    nc.vector.tensor_scalar(var_eps[:, :], mom[:, :, 1], EPS, None, ALU.add).then_inc(var_done, 1)
                    dve.wait_ge(std1_done, t + 1)
                    nc.vector.reciprocal(rstd1[:, :], std1[:, :]).then_inc(rstd1_done, 1)
                    dve.wait_ge(rstd1_done, t + 1)
                    nc.vector.tensor_copy(rstd_all[:, bass.ds(NS * t, NS)], rstd1[:, :])
                    nc.vector.tensor_tensor(ms2[:, :], rstd1[:, :], rstd1[:, :], ALU.mult).then_inc(sq_done, 1)
                    dve.wait_ge(sq_done, 2 * t + 1)
                    nc.vector.tensor_tensor(ms2[:, :], ms2[:, :], mom[:, :, 1], ALU.mult).then_inc(sq_done, 1)
                    dve.wait_ge(sq_done, 2 * t + 2)
                    nc.vector.tensor_scalar(ms2[:, :], ms2[:, :], EPS, None, ALU.add).then_inc(ms_done, 1)
                    dve.wait_ge(std2_done, t + 1)
                    nc.vector.reciprocal(rstd2[:, :], std2[:, :]).then_inc(rstd2_done, 1)
                    dve.wait_ge(rstd2_done, t + 1)
                    nc.vector.tensor_tensor(scale12[:, :], rstd1[:, :], rstd2[:, :], ALU.mult).then_inc(scale_done, 1)
                    dve.wait_ge(scale_done, t + 1)
                    if not (isinstance(t, int) and t == 0):
                        dve.wait_ge(transposed, NC * t)
                    for s in range(NS):
                        last = nc.vector.tensor_scalar(uh[:, s, :], xb[:, u, s, :], mom[:, s, 0:1], scale12[:, s:s + 1],
                                                       ALU.subtract, ALU.mult)
                    last.then_inc(normed, 1)

                def tails(j, v):
                    t = 2 * j + v
                    for c in range(NC):
                        dve.wait_ge(head_done, NC * t + c + 1)
                        nc.vector.tensor_tensor(u_tail[:, c, :], u_ps[:, c, :], u_head[:, c, :].bitcast(F32),
                                                ALU.subtract).then_inc(tail_done, 1)

                def finish(j, v):
                    t = 2 * j + v
                    dve.wait_ge(dtx_done, t + 2)
                    if not (isinstance(t, int) and t == 0):
                        dve.wait_ge(stored[2], 128 * t)
                    flat = lambda buf: buf[:, :, :].rearrange("p k t -> p (k t)")
                    nc.vector.tensor_copy(parts[:, 0, :].bitcast(F32R), flat(log_w))
                    nc.vector.tensor_copy(parts[:, 2, :].bitcast(F32R), flat(inv_w)).then_inc(ph_done, 1)
                    dve.wait_ge(ph_done, t + 1)
                    nc.vector.tensor_tensor(parts[:, 1, :].bitcast(F32R), flat(log_w), parts[:, 0, :], ALU.subtract)
                    nc.vector.tensor_tensor(parts[:, 3, :].bitcast(F32R), flat(inv_w), parts[:, 2, :],
                                            ALU.subtract).then_inc(parts_done, 1)

                def copies(j, v):
                    t = 2 * j + v
                    dve.wait_ge(dtr_head_done, t + 1)
                    nc.vector.tensor_tensor(dtr_tail[:, :], o_ps[:, 0, :], dtr_head[:, :].bitcast(F32),
                                            ALU.subtract).then_inc(o_free[0], 1)
                    for k in by_dve:
                        if k == 11:
                            if not (isinstance(t, int) and t == 0):
                                finish(j, v - 1)
                            dve.wait_ge(e_done, t + 1)
                            nc.vector.tensor_scalar(one_e[:, :, :], mag[:, :, :], 1.0, None, ALU.add).then_inc(one_e_done, 1)
                        dve.wait_ge(out_ready, NOUT * t + k + 1)
                        if not (isinstance(t, int) and t == 0):
                            if k == 2:
                                dve.wait_ge(stored[0], 32 * t)
                            if k == 11:
                                dve.wait_ge(stored[1], 16 * t)
                        slot = k - 2 if k < 7 else k - 6
                        nc.vector.tensor_copy(bcz[:, slot, :], o_ps[:, k % 4, :]).then_inc(o_free[k % 4], 1)
                    dve.wait_ge(ln_done, t + 1)
                    nc.vector.scalar_tensor_tensor(log_w[:, :, :], one_e[:, :, :], 1.0, log_w[:, :, :],
                                                   ALU.is_gt, ALU.mult).then_inc(ln_masked, 1)
                    nc.vector.scalar_tensor_tensor(one_e[:, :, :], one_e[:, :, :], 1.0, mag[:, :, :],
                                                   ALU.subtract, ALU.subtract).then_inc(err_done, 1)

                def step(j, v):
                    tails(j, v)
                    if not (isinstance(j, int) and v == NT - 1):
                        norm(j, v + 1)
                    copies(j, v)

                norm(0, 0)
                rolled(dve, 1, 2, NT, step, tail=1)
                finish(0, NT - 1)

            @block.scalar
            def _(act):
                act.sem_inc(o_free[1], 1)
                act.sem_inc(o_free[0], 1)
                act.sem_inc(o_free[2], 1)
                act.sem_inc(o_free[3], 1)

                def roots(t):
                    act.wait_ge(var_done, t + 1)
                    nc.scalar.activation(std1[:, :], var_eps[:, :], ACT.Sqrt).then_inc(std1_done, 1)
                    act.wait_ge(ms_done, t + 1)
                    nc.scalar.activation(std2[:, :], ms2[:, :], ACT.Sqrt).then_inc(std2_done, 1)

                def step(j, v):
                    t = 2 * j + v
                    first = isinstance(t, int) and t == 0
                    if not first:
                        act.wait_ge(out_ready, NOUT * t)
                    for c in range(NC):
                        act.wait_ge(transposed, NC * t + c + 1)
                        nc.scalar.activation(u_head[:, c, :], u_ps[:, c, :], ACT.Copy).then_inc(head_done, 1)
                    if not (isinstance(t, int) and t == NT - 1):
                        roots(t + 1)
                    act.wait_ge(out_ready, NOUT * t + 1)
                    nc.scalar.activation(dtr_head[:, :], o_ps[:, 0, :], ACT.Copy).then_inc(dtr_head_done, 1)
                    act.wait_ge(out_ready, NOUT * t + 2)
                    if not first:
                        act.wait_ge(stored[3], 16 * t)
                        act.wait_ge(x_repeated, 256 * t)
                    nc.scalar.activation(x_ch[:, :], o_ps[:, 1, :], ACT.Copy).then_inc(o_free[1], 1)
                    for k in range(3, NOUT):
                        if k in by_act:
                            act.wait_ge(out_ready, NOUT * t + k + 1)
                            if not first:
                                if k == 3:
                                    act.wait_ge(stored[0], 32 * t)
                                if k == 12:
                                    act.wait_ge(stored[1], 16 * t)
                            slot = k - 2 if k < 7 else k - 6
                            nc.scalar.activation(bcz[:, slot, :], o_ps[:, k % 4, :], ACT.Copy).then_inc(o_free[k % 4], 1)
                        if k == 7 and not first:
                            act.wait_ge(dtx_done, t + 1)
                        if 7 <= k < 11:
                            c = k - 7
                            act.wait_ge(out_ready, NOUT * t + k + 1)
                            nc.scalar.activation(mag[:, c, :], o_ps[:, k % 4, :], ACT.Abs, bias=dt_bias[:, c:c + 1])
                            nc.scalar.activation(pos[:, c, :], o_ps[:, k % 4, :], ACT.Relu,
                                                 bias=dt_bias[:, c:c + 1]).then_inc(o_free[k % 4], 1)
                        if k == 10:
                            act.wait_ge(o_free[2], freed(10, t))
                            nc.scalar.activation(mag[:, :, :], mag[:, :, :], ACT.Exp, scale=-1.0).then_inc(e_done, 1)
                            act.wait_ge(one_e_done, t + 1)
                            if not first:
                                act.wait_ge(parts_done, t)
                            nc.scalar.activation(log_w[:, :, :], one_e[:, :, :], ACT.Ln).then_inc(ln_done, 1)
                            act.wait_ge(ln_masked, t + 1)
                            nc.scalar.activation(inv_w[:, :, :], log_w[:, :, :], ACT.Exp, scale=-1.0).then_inc(inv_done, 1)

                roots(0)
                rolled(act, 1, 2, NT, step, tail=1)

            @block.gpsimd
            def _(pool):
                pool.sem_inc(dtx_done, 1)

                def step(j, v):
                    t = 2 * j + v
                    pool.wait_ge(err_done, t + 1)
                    pool.wait_ge(inv_done, t + 1)
                    nc.gpsimd.tensor_tensor(inv_w[:, :, :], inv_w[:, :, :], one_e[:, :, :], ALU.mult).then_inc(corr_done, 1)
                    pool.wait_ge(corr_done, t + 1)
                    nc.gpsimd.tensor_tensor(log_w[:, :, :], log_w[:, :, :], inv_w[:, :, :], ALU.subtract).then_inc(log1p_done, 1)
                    pool.wait_ge(log1p_done, t + 1)
                    pool.wait_ge(o_free[2], freed(10, t))
                    nc.gpsimd.tensor_tensor(log_w[:, :, :], log_w[:, :, :], pos[:, :, :], ALU.add).then_inc(dt_done, 1)
                    pool.wait_ge(dt_done, t + 1)
                    pool.wait_ge(x_repeated, 256 * (t + 1))
                    nc.gpsimd.tensor_tensor(inv_w[:, :, :], log_w[:, :, :], x_rep[:, :, :], ALU.mult).then_inc(dtx_done, 1)

                rolled(pool, 1, 2, NT, step)

            @block.tensor
            def _(pe):
                def step(j, v):
                    t = 2 * j + v
                    first = isinstance(t, int) and t == 0
                    pe.wait_ge(normed, t + 1)
                    pe.wait_ge(tail_done, NC * t + 1)
                    for c in range(NC):
                        for s in range(NS):
                            last = nc.tensor.transpose(u_ps[:, c, P * s:P * (s + 1)], uh[:, s, P * c:P * (c + 1)], ident[:, :])
                        last.then_inc(transposed, 1)
                    if first:
                        pe.wait_ge(w_ready, 5)
                    for k, m in enumerate(ORDER):
                        uses = USES[k % 4] * t + k // 4
                        pe.wait_ge(o_free[k % 4], uses + 1)
                        out = o_ps[:, k % 4, :]
                        if m is None:
                            rows = slice(P * (k - 7), P * (k - 6))
                            last = products3(nc, out, dtw_head[:, rows], dtw_tail[:, rows], dtr_head[:, :], dtr_tail[:, :],
                                             True, True)
                        else:
                            rows = slice(P * m, P * (m + 1))
                            for c in range(NC):
                                if k == 0:
                                    pe.wait_ge(tail_done, NC * t + c + 2)
                                last = products3(nc, out, w_head[:, c, rows], w_tail[:, c, rows], u_head[:, c, :],
                                                 u_tail[:, c, :], c == 0, c == NC - 1)
                        last.then_inc(out_ready, 1)

                pe.wait_ge(persist["ident_ready"], 2)
                rolled(pe, 1, 2, NT, step)
    return None


def stage2(nc, d, persist):
    ITS = BATCH * NC
    TILES = P // 4
    with ExitStack() as ctx:
        sb = lambda name, shape, dt=F32: ctx.enter_context(nc.sbuf_tensor("s2_" + name, shape, dt))
        ps = lambda name, shape, dt=F32: ctx.enter_context(nc.psum_tensor("s2_" + name, shape, dt))
        sem = lambda name: ctx.enter_context(nc.semaphore("s2_" + name))
        dt_in = sb("dt_in", [P, 2, 2, SEQ], F32R)
        dtx_in = sb("dtx_in", [P, 2, 2, SEQ], F32R)
        B_in = sb("B_in", [P, 2, SEQ])
        C_in = sb("C_in", [P, 2, REP, SEQ])
        x_in = sb("x_in", [P, 2, SEQ])
        y_sb = sb("y_sb", [P, 2, SEQ])
        negA = sb("negA", [P, ITS * TILES])
        D_all = sb("D_all", [P, ITS])
        A_cur = sb("A_cur", [P, 2, TILES])
        D_cur = sb("D_cur", [P, 2, 1])
        decay = sb("decay", [P, 2, SEQ])
        h = sb("h", [P, 2, SEQ])
        hc = sb("hc", [P, 2, SEQ])
        ones = sb("ones", [P, 16 * 128])
        spread = sb("spread", [P, 16, P], F32R)
        gather = sb("gather", [P, 8, STATE])
        dt_ps = ps("dt_ps", [P, 2, 512])
        dtx_ps = ps("dtx_ps", [P, 2, SEQ])
        y_ps = ps("y_ps", [P, SEQ])

        loaded = [sem("loaded0"), sem("loaded1")]
        const_loaded, A_ready, made = sem("const_loaded"), sem("A_ready"), sem("made")
        A_copied = sem("A_copied")
        dt_ready, exp_done = sem("dt_ready"), sem("exp_done")
        dtx_ready, b_done = sem("dtx_ready"), sem("b_done")
        scanned, multiplied, summed = sem("scanned"), sem("multiplied"), sem("summed")
        y_out = sem("y_out")
        y_stored = [sem("y_stored0"), sem("y_stored1")]
        DMAS = 14

        with nc.Block() as block:
            @block.sync
            def _(sp):
                for b in range(BATCH):
                    sp.dma_start(negA[:, P * b:P * (b + 1)], d["A_log"]).then_inc(const_loaded, 16)
                    sp.dma_start(D_all[:, NC * b:NC * (b + 1)], d["D"]).then_inc(const_loaded, 16)

                def load(it, u):
                    flat = lambda name: d[name].rearrange("b k h r t -> (b k) r h t")
                    inc = lambda ins: ins.then_inc(loaded[u], 16)
                    inc(sp.dma_start(dt_in[:, u].bitcast(F32), flat("dt_s")[it]))
                    inc(sp.dma_start(dtx_in[:, u].bitcast(F32), flat("dtx_s")[it]))
                    for n in range(4):
                        rows = slice(STATE * n, STATE * (n + 1))
                        inc(sp.dma_start(B_in[rows, u], d["B_s"].rearrange("b (g n) t -> (b g) n t", n=STATE)[it]))
                        inc(sp.dma_start(C_in[rows, u], d["C_s"].rearrange("b k (r n) t -> (b k) n r t", n=STATE)[it]))
                        inc(sp.dma_start(x_in[rows, u], d["x_s"].rearrange("b (g n) t -> (b g) n t", n=STATE)[it]))

                def store(it, u):
                    sp.dma_start(d["y_s"].rearrange("b k p t -> (b k) p t")[it], y_sb[:, u]).then_inc(y_stored[u], 16)

                def step(j, v):
                    it, u = 2 * j + v, v % 2
                    if not (isinstance(j, int) and j == 0 and v < 2):
                        sp.wait_ge(y_out, it + 1)
                        store(it - 2, u)
                    load(it, u)

                assert DMAS == 2 + 3 * 4
                rolled(sp, 2, 2, ITS, step)
                for it in (ITS - 2, ITS - 1):
                    sp.wait_ge(y_out, it + 3)
                    store(it, it % 2)
                for u in range(2):
                    sp.wait_ge(y_stored[u], 16 * (ITS // 2))

            @block.gpsimd
            def _(pool):
                pool.sem_inc(multiplied, 2)
                nc.gpsimd.memset(ones[:, :], 0.0).then_inc(made, 1)
                pat = ones[:, :].rearrange("p (q j n) -> p q j n", q=16, j=4)
                pool.wait_ge(made, 1)
                for n in range(2):
                    nc.gpsimd.affine_select(out=pat, in_=pat, compare_op=ALU.not_equal, fill=1.0, base=-64 * n,
                                            pattern=[[-4, 16], [-1, 4], [0, STATE]], channel_multiplier=1).then_inc(made, 1)
                    pool.wait_ge(made, n + 2)
                nc.gpsimd.tensor_copy(spread[:, :, :].rearrange("p q m -> p (q m)"), ones[:, :]).then_inc(made, 1)
                nc.gpsimd.memset(gather[:, :, :], 1.0).then_inc(made, 1)
                pool.wait_ge(made, 5)
                nc.gpsimd.affine_select(out=gather[:, :, :], in_=gather[:, :, :], compare_op=ALU.is_ge, fill=0.0, base=0,
                                        pattern=[[P, 8], [-STATE, STATE]], channel_multiplier=1).then_inc(made, 1)
                pool.wait_ge(made, 6)
                nc.gpsimd.affine_select(out=gather[:, :, :], in_=gather[:, :, :], compare_op=ALU.is_ge, fill=0.0,
                                        base=STATE - 1, pattern=[[-P, 8], [STATE, STATE]],
                                        channel_multiplier=-1).then_inc(made, 1)

                def step(j, v):
                    w, u = 2 * TILES * j + v, (v // TILES) % 2
                    r = v % 4
                    if v % TILES == 0:
                        pool.wait_ge(loaded[u], 16 * DMAS * (j + v // (2 * TILES) + 1))
                    pool.wait_ge(scanned, w + 3)
                    pool.wait_ge(summed, w + 1)
                    nc.gpsimd.tensor_tensor(hc[:, v % 2], h[:, v % 2], C_in[:, u, r], ALU.mult).then_inc(multiplied, 1)

                rolled(pool, 0, 2 * TILES, ITS * TILES, step)

            @block.scalar
            def _(act):
                act.sem_inc(exp_done, 2)
                act.wait_ge(const_loaded, 32 * BATCH)
                nc.scalar.activation(negA[:, :], negA[:, :], ACT.Exp).then_inc(A_ready, 1)
                act.wait_ge(A_ready, 1)
                nc.scalar.mul(negA[:, :], negA[:, :], -1.0).then_inc(A_ready, 1)

                def step(j, v):
                    w, u = 2 * TILES * j + v, (v // TILES) % 2
                    if v % TILES == 0:
                        act.wait_ge(A_copied, 2 * j + v // TILES + 1)
                    act.wait_ge(scanned, w + 1)
                    for k in range(2):
                        act.wait_ge(dt_ready, 2 * w + k + 1)
                        nc.scalar.activation(decay[:, v % 2, 512 * k:512 * (k + 1)], dt_ps[:, k], ACT.Exp,
                                             scale=A_cur[:, u, v % TILES:v % TILES + 1]).then_inc(exp_done, 1)

                rolled(act, 0, 2 * TILES, ITS * TILES, step)

            @block.vector
            def _(dve):
                dve.sem_inc(scanned, 2)
                dve.sem_inc(y_out, 2)
                dve.wait_ge(A_ready, 2)

                def evac(it, u, n):
                    dve.wait_ge(A_copied, it + 1)
                    dve.wait_ge(summed, TILES * (it + 1) + 2)
                    if not (isinstance(n, int) and n == 0):
                        dve.wait_ge(y_stored[u], 16 * n)
                    nc.vector.scalar_tensor_tensor(y_sb[:, u], x_in[:, u], D_cur[:, u], y_ps[:, :],
                                                   ALU.mult, ALU.add).then_inc(y_out, 1)

                def step(j, v):
                    w, it, u = 2 * TILES * j + v, 2 * j + v // TILES, (v // TILES) % 2
                    if v % TILES == 0:
                        dve.wait_ge(loaded[u], 16 * DMAS * (j + v // (2 * TILES) + 1))
                        nc.vector.tensor_copy(D_cur[:, u], D_all[:, bass.ds(it, 1)])
                        nc.vector.tensor_copy(A_cur[:, u], negA[:, bass.ds(TILES * it, TILES)]).then_inc(A_copied, 1)
                    dve.wait_ge(dtx_ready, w + 1)
                    nc.vector.tensor_tensor(dtx_ps[:, v % 2], dtx_ps[:, v % 2], B_in[:, u], ALU.mult).then_inc(b_done, 1)
                    dve.wait_ge(b_done, w + 1)
                    dve.wait_ge(exp_done, 2 * w + 4)
                    dve.wait_ge(multiplied, w + 1)
                    nc.vector.tensor_tensor_scan(h[:, v % 2], decay[:, v % 2], dtx_ps[:, v % 2], 0.0,
                                                 ALU.mult, ALU.add).then_inc(scanned, 1)
                    if v >= TILES and v % TILES == 2:
                        vb = v // TILES - 1
                        evac(2 * j + vb, vb % 2, j + vb // 2)

                rolled(dve, 3, 2 * TILES, ITS * TILES, step)
                evac(ITS - 1, 1, ITS // 2 - 1)

            @block.tensor
            def _(pe):
                pe.sem_inc(summed, 2)
                LAG = 3

                def spread_tile(j, v):
                    w, u = 2 * TILES * j + v, (v // TILES) % 2
                    q, r = (v % TILES) // 4, v % 4
                    half, sel = r // 2, (r % 2) * 8 + q
                    if v % TILES == 0:
                        pe.wait_ge(loaded[u], 16 * DMAS * (j + v // (2 * TILES) + 1))
                    for k in range(2):
                        pe.wait_ge(exp_done, 2 * w + k + 1)
                        nc.tensor.matmul(dt_ps[:, k], spread[:, sel], dt_in[:, u, half, 512 * k:512 * (k + 1)],
                                         start=True, stop=True).then_inc(dt_ready, 1)
                    pe.wait_ge(scanned, w + 1)
                    for k in range(2):
                        last = nc.tensor.matmul(dtx_ps[:, v % 2, 512 * k:512 * (k + 1)], spread[:, sel],
                                                dtx_in[:, u, half, 512 * k:512 * (k + 1)], start=True, stop=True)
                    last.then_inc(dtx_ready, 1)

                def sum_tile(j, v):
                    w = 2 * TILES * j + v
                    q, r = (v % TILES) // 4, v % 4
                    if v % TILES == 0:
                        pe.wait_ge(y_out, 2 * j + v // TILES + 2)
                    pe.wait_ge(multiplied, w + 3)
                    for k in range(2):
                        last = nc.tensor.matmul(y_ps[STATE * r:STATE * (r + 1), 512 * k:512 * (k + 1)], gather[:, q],
                                                hc[:, v % 2, 512 * k:512 * (k + 1)], start=(q == 0), stop=(q == 7))
                    last.then_inc(summed, 1)

                def step(j, v):
                    spread_tile(j, v)
                    if not (isinstance(j, int) and j == 0 and v < LAG):
                        sum_tile(j, v - LAG)

                pe.wait_ge(made, 7)
                rolled(pe, LAG, 2 * TILES, ITS * TILES, step)
                for v in range(ITS * TILES - LAG, ITS * TILES):
                    sum_tile(0, v)


def stage3(nc, d, persist):
    ident, mean_all, rstd_all = persist["ident"], persist["mean_all"], persist["rstd_all"]
    rows_v = lambda name: d[name].rearrange("(b u s p) c -> b u p s c", b=BATCH, u=UP, p=P)
    with ExitStack() as ctx:
        sb = lambda name, shape, dt=F32: ctx.enter_context(nc.sbuf_tensor("s3_" + name, shape, dt))
        ps = lambda name, shape, dt=F32: ctx.enter_context(nc.psum_tensor("s3_" + name, shape, dt))
        sem = lambda name: ctx.enter_context(nc.semaphore("s3_" + name))
        out_head, out_tail = (sb(n, [P, NC, DM], F32R) for n in ("out_head", "out_tail"))
        gate_head, gate_tail = (sb(n, [P, NC, FF], F32R) for n in ("gate_head", "gate_tail"))
        up_head, up_tail = (sb(n, [P, NC, FF], F32R) for n in ("up_head", "up_tail"))
        down_head, down_tail = (sb(n, [P, NF, DM], F32R) for n in ("down_head", "down_tail"))
        norm2 = sb("norm2", [P, NC])
        work = sb("work", [P, 3, NC * TT])
        Y, Z, X = (work[:, n, :].rearrange("p (k t) -> p k t", k=NC) for n in range(3))
        a_head = sb("a_head", [P, NC, TT], F32R)
        a_tail = sb("a_tail", [P, NC, TT], F32R)
        sg = sb("silu_gate", [P, TT])
        gu = sb("gate_up", [P, TT])
        gu_head = sb("gu_head", [P, 2, TT], F32R)
        gu_tail = sb("gu_tail", [P, 2, TT], F32R)
        sumsq = sb("sumsq", [P, NS])
        msq = sb("msq", [P, NS])
        std = sb("std", [P, NS])
        rstd = sb("rstd", [P, NS])
        mean_cur = sb("mean_cur", [P, NS])
        rstd_cur = sb("rstd_cur", [P, NS])
        gu_ps = ps("gu_ps", [P, 4, TT])
        acc_ps = ps("acc_ps", [P, NC, TT])

        w_loaded = [sem(f"w_loaded{n}") for n in range(4)]
        w_head_done, w_tail_done, cur_done = sem("w_head"), sem("w_tail"), sem("cur")
        norm_loaded = sem("norm_loaded")
        sp_passed = sem("sp_passed")
        yz_loaded, x_loaded, x1_stored = sem("yz_loaded"), sem("x_loaded"), sem("x1_stored")
        silu_z, gated, a_head_y, a_tail_y = sem("silu_z"), sem("gated"), sem("a_head_y"), sem("a_tail_y")
        o_ready, u0_done, h_done, xh_done = sem("o_ready"), sem("u0"), sem("h"), sem("xh")
        sq_done, msq_done, std_done, rstd_done, hn_done = (
            sem("sq"), sem("msq"), sem("std"), sem("rstd"), sem("hn"))
        transposed, a_head_x, a_tail_x = sem("transposed"), sem("a_head_x"), sem("a_tail_x")
        gu_ready = sem("gu_ready")
        sg_done, gu_done, guh_done, gut_done = sem("sg"), sem("gu"), sem("gu_head"), sem("gu_tail")
        down_done = sem("down")
        x1_done = sem("x1")

        weights = [(d["out_w"], out_head, out_tail, NC, DM, False), (d["gate_w"], gate_head, gate_tail, NC, FF, True),
                   (d["up_w"], up_head, up_tail, NC, FF, True), (d["down_w"], down_head, down_tail, NF, DM, False)]
        SLOT = FF
        flat = work[:, :, :].rearrange("p a n -> p (a n)")
        pieces = []
        for src, head, tail, blocks, cols, scaled in weights:
            per = max(1, SLOT // cols)
            for c in range(0, blocks, per):
                n = min(per, blocks - c)
                slot = len(pieces) % 4
                pieces.append((src.rearrange("(c p) m -> p c m", p=P)[:, c:c + n, :],
                               flat[:, slot * SLOT:slot * SLOT + n * cols].rearrange("p (c m) -> p c m", c=n),
                               head[:, c:c + n, :], tail[:, c:c + n, :], norm2[:, c:c + 1] if scaled else 1.0))
        first_gate = 2
        assert NC * DM <= 2 * SLOT

        with nc.Block() as block:
            @block.sync
            def _(sp):
                sp.dma_start(norm2[:, :], d["norm2"]).then_inc(norm_loaded, 16)
                for n, (src, slot, _, _, _) in enumerate(pieces):
                    if n >= 4:
                        sp.wait_ge(w_tail_done, n - 3)
                    sp.dma_start(slot, src).then_inc(w_loaded[n % 4], 16)
                sp.wait_ge(w_tail_done, len(pieces))

                def step(j, v):
                    t, b, u = 2 * j + v, j + v // 2, v % 2
                    first = isinstance(t, int) and t == 0
                    tok = slice(u * TT, (u + 1) * TT)
                    if not first:
                        sp.wait_ge(hn_done, NS * t)
                        sp.wait_ge(xh_done, t)
                        sp.wait_ge(transposed, NC * t)
                    sp.dma_start(Y, d["y_s"][b, :, :, tok].rearrange("k p t -> p k t")).then_inc(yz_loaded, 16)
                    sp.dma_start(Z, d["z_s"][b, :, :, tok].rearrange("k p t -> p k t")).then_inc(yz_loaded, 16)
                    if not first:
                        sp.wait_ge(x1_done, t)
                        sp.sem_inc(sp_passed, 1)
                        sp.dma_start(rows_v("x1_s")[j + (v - 1) // 2, (v - 1) % 2], X).then_inc(x1_stored, 16)
                        sp.wait_ge(x1_stored, 16 * t)
                    sp.dma_start(X, rows_v("x")[b, u]).then_inc(x_loaded, 16)

                rolled(sp, 1, 2, NT, step)
                sp.wait_ge(x1_done, NT)
                sp.dma_start(rows_v("x1_s")[BATCH - 1, UP - 1], X).then_inc(x1_stored, 16)
                sp.wait_ge(x1_stored, 16 * NT)

            @block.scalar
            def _(act):
                act.wait_ge(norm_loaded, 16)
                for n, (_, slot, head, _, scale) in enumerate(pieces):
                    act.wait_ge(w_loaded[n % 4], 16 * (n // 4 + 1))
                    nc.scalar.activation(head, slot, ACT.Copy, scale=scale).then_inc(w_head_done, 1)

                def step(j, v):
                    t = 2 * j + v
                    first = isinstance(t, int) and t == 0
                    act.wait_ge(yz_loaded, 32 * (t + 1))
                    nc.scalar.activation(Z, Z, ACT.Silu).then_inc(silu_z, 1)
                    act.wait_ge(gated, t + 1)
                    if not first:
                        act.wait_ge(gu_ready, 2 * NF * t)
                    nc.scalar.activation(a_head[:, :, :], Y, ACT.Copy).then_inc(a_head_y, 1)
                    for s in range(NS):
                        act.wait_ge(h_done, NS * t + s + 1)
                        last = nc.scalar.activation(Z[:, s, :], Y[:, s, :], ACT.Square, accum_out=sumsq[:, s:s + 1])
                    last.then_inc(sq_done, 1)
                    act.wait_ge(msq_done, t + 1)
                    nc.scalar.activation(std[:, :], msq[:, :], ACT.Sqrt).then_inc(std_done, 1)
                    act.wait_ge(rstd_done, t + 1)
                    for s in range(NS):
                        nc.scalar.activation(Z[:, s, :], Y[:, s, :], ACT.Copy, scale=rstd[:, s:s + 1]).then_inc(hn_done, 1)
                    act.wait_ge(o_ready, NS * (t + 1))
                    for c in range(NC):
                        act.wait_ge(transposed, NC * t + c + 1)
                        nc.scalar.activation(a_head[:, c, :], acc_ps[:, c, :], ACT.Copy).then_inc(a_head_x, 1)
                    for f in range(NF):
                        n = NF * t + f
                        act.wait_ge(gu_ready, 2 * n + 1)
                        if not (first and f == 0):
                            act.wait_ge(gu_done, n)
                        nc.scalar.activation(sg[:, :], gu_ps[:, 2 * f % 4, :], ACT.Silu).then_inc(sg_done, 1)
                        act.wait_ge(gu_done, n + 1)
                        if not (first and f < 2):
                            act.wait_ge(down_done, n - 1)
                        nc.scalar.activation(gu_head[:, f % 2, :], gu[:, :], ACT.Copy).then_inc(guh_done, 1)

                rolled(act, 1, 2, NT, step)

            @block.vector
            def _(dve):
                for n, (_, slot, head, tail, scale) in enumerate(pieces):
                    dve.wait_ge(w_head_done, n + 1)
                    nc.vector.scalar_tensor_tensor(tail, slot, scale, head.bitcast(F32), ALU.mult,
                                                   ALU.subtract).then_inc(w_tail_done, 1)

                def step(j, v):
                    t = 2 * j + v
                    first = isinstance(t, int) and t == 0
                    dve.wait_ge(silu_z, t + 1)
                    nc.vector.tensor_tensor(Y, Y, Z, ALU.mult).then_inc(gated, 1)
                    dve.wait_ge(a_head_y, t + 1)
                    nc.vector.tensor_tensor(a_tail[:, :, :], Y, a_head[:, :, :].bitcast(F32), ALU.subtract).then_inc(a_tail_y, 1)
                    dve.wait_ge(x_loaded, 16 * (t + 1))
                    dve.wait_ge(a_tail_y, t + 1)
                    nc.vector.tensor_copy(mean_cur[:, :], mean_all[:, bass.ds(NS * t, NS)])
                    nc.vector.tensor_copy(rstd_cur[:, :], rstd_all[:, bass.ds(NS * t, NS)]).then_inc(cur_done, 1)
                    dve.wait_ge(cur_done, t + 1)
                    for s in range(NS):
                        last = nc.vector.tensor_scalar(Y[:, s, :], X[:, s, :], mean_cur[:, s:s + 1], rstd_cur[:, s:s + 1],
                                                       ALU.subtract, ALU.mult)
                    last.then_inc(u0_done, 1)
                    dve.wait_ge(u0_done, t + 1)
                    for s in range(NS):
                        dve.wait_ge(o_ready, NS * t + s + 1)
                        nc.vector.tensor_tensor(Y[:, s, :], Y[:, s, :], gu_ps[:, s, :], ALU.add).then_inc(h_done, 1)
                    dve.wait_ge(h_done, NS * (t + 1))
                    dve.wait_ge(sq_done, t + 1)
                    nc.vector.tensor_scalar(msq[:, :], sumsq[:, :], 1.0 / DM, EPS, ALU.mult, ALU.add).then_inc(msq_done, 1)
                    nc.vector.tensor_tensor(X, X, Y, ALU.add).then_inc(xh_done, 1)
                    dve.wait_ge(std_done, t + 1)
                    nc.vector.reciprocal(rstd[:, :], std[:, :]).then_inc(rstd_done, 1)
                    for c in range(NC):
                        dve.wait_ge(a_head_x, NC * t + c + 1)
                        nc.vector.tensor_tensor(a_tail[:, c, :], acc_ps[:, c, :], a_head[:, c, :].bitcast(F32),
                                                ALU.subtract).then_inc(a_tail_x, 1)
                    for f in range(NF):
                        n = NF * t + f
                        dve.wait_ge(sg_done, n + 1)
                        dve.wait_ge(gu_ready, 2 * n + 2)
                        if not (first and f == 0):
                            dve.wait_ge(gut_done, n)
                        nc.vector.tensor_tensor(gu[:, :], sg[:, :], gu_ps[:, (2 * f + 1) % 4, :], ALU.mult).then_inc(gu_done, 1)
                        dve.wait_ge(guh_done, n + 1)
                        nc.vector.tensor_tensor(gu_tail[:, f % 2, :], gu[:, :], gu_head[:, f % 2, :].bitcast(F32),
                                                ALU.subtract).then_inc(gut_done, 1)
                    dve.wait_ge(down_done, NF * (t + 1))
                    dve.wait_ge(xh_done, t + 1)
                    nc.vector.tensor_tensor(X, X, acc_ps[:, :, :], ALU.add).then_inc(x1_done, 1)

                rolled(dve, 1, 2, NT, step)

            @block.tensor
            def _(pe):
                def step(j, v):
                    t = 2 * j + v
                    first = isinstance(t, int) and t == 0
                    if first:
                        pe.wait_ge(w_tail_done, first_gate)
                    pe.wait_ge(a_tail_y, t + 1)
                    if not first:
                        pe.wait_ge(gut_done, NF * t)
                    for s in range(NS):
                        for c in range(NC):
                            cols = slice(P * s, P * (s + 1))
                            last = products3(nc, gu_ps[:, s, :], a_head[:, c, cols], a_tail[:, c, cols], out_head[:, c, :],
                                             out_tail[:, c, :], c == 0, c == NC - 1)
                        last.then_inc(o_ready, 1)
                    if not first:
                        pe.wait_ge(x1_done, t)
                    pe.wait_ge(hn_done, NS * (t + 1))
                    for c in range(NC):
                        for s in range(NS):
                            last = nc.tensor.transpose(acc_ps[:, c, P * s:P * (s + 1)], Z[:, s, P * c:P * (c + 1)], ident[:, :])
                        last.then_inc(transposed, 1)
                    if first:
                        pe.wait_ge(w_tail_done, len(pieces))

                    def down(f):
                        pe.wait_ge(gut_done, NF * t + f + 1)
                        if f == 0:
                            pe.wait_ge(a_tail_x, NC * (t + 1))
                        for s in range(NS):
                            cols = slice(P * s, P * (s + 1))
                            last = products3(nc, acc_ps[:, s, :], gu_head[:, f % 2, cols], gu_tail[:, f % 2, cols],
                                             down_head[:, f, :], down_tail[:, f, :], f == 0, f == NF - 1)
                        last.then_inc(down_done, 1)

                    for f in range(NF):
                        n = NF * t + f
                        if not (first and f < 2):
                            pe.wait_ge(gu_done, n - 1)
                        if f < 2:
                            pe.wait_ge(h_done, NS * (t + 1))
                        rows = slice(P * f, P * (f + 1))
                        for k, (head, tail) in enumerate(((gate_head, gate_tail), (up_head, up_tail))):
                            for c in range(NC):
                                if f == 0 and k == 0:
                                    pe.wait_ge(a_tail_x, NC * t + c + 1)
                                last = products3(nc, gu_ps[:, (2 * f + k) % 4, :], head[:, c, rows], tail[:, c, rows],
                                                 a_head[:, c, :], a_tail[:, c, :], c == 0, c == NC - 1)
                            last.then_inc(gu_ready, 1)
                        if f:
                            down(f - 1)
                    down(NF - 1)

                rolled(pe, 1, 2, NT, step)


def stage4(nc, d, persist):
    ident = persist["ident"]
    RA = 8
    STD = HD - RA
    rows_v = lambda name: d[name].rearrange("(b u s p) c -> b u p s c", b=BATCH, u=UP, p=P)
    with ExitStack() as ctx:
        sb = lambda name, shape, dt=F32: ctx.enter_context(nc.sbuf_tensor("s4_" + name, shape, dt))
        ps = lambda name, shape, dt=F32: ctx.enter_context(nc.psum_tensor("s4_" + name, shape, dt))
        sem = lambda name: ctx.enter_context(nc.semaphore("s4_" + name))
        q_w, k_w, v_w = (sb(n, [P, NC, DM]) for n in ("q_w", "k_w", "v_w"))
        heads = [sb(n, [P, NC, DM], F32R) for n in ("q_head", "k_head", "v_head")]
        tails = [sb(n, [P, NC, DM], F32R) for n in ("q_tail", "k_tail", "v_tail")]
        w_sr = sb("w_sr", [P, 2, HEADS])
        s_sr = sb("s_sr", [P, 2, HEADS])
        q_sr = sb("q_sr", [P, 2, HEADS])
        use_ra = sb("use_ra", [P, 2, HEADS])
        mix = sb("mix", [P, 4, HEADS, RA])
        xb = sb("x_rows", [P, 2, NS, DM])
        uh = sb("u_rows", [P, NS, DM])
        stats = sb("stats", [P, NS, 6])
        mom = sb("moments", [P, NS, 2])
        var_eps = sb("var_eps", [P, NS])
        std = sb("std", [P, NS])
        rstd = sb("rstd", [P, NS])
        u_head = sb("u_head", [P, NC, TT], F32R)
        u_tail = sb("u_tail", [P, NC, TT], F32R)
        qk = sb("qk", [P, 4, NC, TT])
        v_rows = sb("v_rows", [P, NS, DM])
        u_ps = ps("u_ps", [P, NC, TT])
        o_ps = ps("o_ps", [P, 4, TT])

        w_loaded, s_ready, mixed, scaled = sem("w_loaded"), sem("s_ready"), sem("mixed"), sem("scaled")
        w_head_done, w_tail_done = sem("w_head"), sem("w_tail")
        dve_passed = sem("dve_passed")
        x_loaded = [sem("x_loaded0"), sem("x_loaded1")]
        stats_done, mom_done, var_done, std_done, rstd_done, normed = (
            sem("stats"), sem("moments"), sem("var_eps"), sem("std"), sem("rstd"), sem("normed"))
        transposed, head_done, tail_done = sem("transposed"), sem("u_head"), sem("u_tail")
        out_ready = sem("out_ready")
        copied, split = sem("copied"), sem("split")
        qk_stored, v_stored = sem("qk_stored"), sem("v_stored")
        NOUT = 12

        with nc.Block() as block:
            @block.sync
            def _(sp):
                for buf, name in ((q_w, "wq"), (k_w, "wk"), (v_w, "wv")):
                    sp.dma_start(buf[:, :, :], d[name].rearrange("(c p) m -> p c m", p=P)).then_inc(w_loaded, 16)
                for n, name in enumerate(("w_std", "w_rec")):
                    sp.dma_start(w_sr[:, n, :], d[name].partition_broadcast(P)).then_inc(w_loaded, 16)
                for u in range(2):
                    sp.dma_start(xb[:, u], rows_v("x1_s")[0, u]).then_inc(x_loaded[u], 16)

                def step(j, v):
                    t, b, u = 2 * j + v, j + v // 2, v % 2
                    tok = slice(u * TT, (u + 1) * TT)
                    if not (isinstance(t, int) and t >= NT - 2):
                        sp.wait_ge(normed, t + 1)
                        sp.dma_start(xb[:, u], rows_v("x1_s")[b + 1, u]).then_inc(x_loaded[u], 16)
                    sp.wait_ge(split, 10 * t + 8)
                    for n, name in enumerate(("q_s", "q_s", "k_s", "k_s")):
                        sp.dma_start(d[name][b, :, n % 2, :, tok].rearrange("k p t -> p k t"), qk[:, n]).then_inc(qk_stored, 16)
                    sp.wait_ge(split, 10 * t + 10)
                    sp.wait_ge(copied, 10 * t + 10)
                    sp.dma_start(rows_v("v_s")[b, u], v_rows[:, :, :]).then_inc(v_stored, 16)

                rolled(sp, 0, 2, NT, step, tail=2)
                sp.wait_ge(qk_stored, 64 * NT)
                sp.wait_ge(v_stored, 16 * NT)

            @block.scalar
            def _(act):
                act.wait_ge(s_ready, 1)
                nc.scalar.activation(s_sr[:, :, :], w_sr[:, :, :], ACT.Sqrt).then_inc(s_ready, 1)

                def root(t):
                    act.wait_ge(var_done, t + 1)
                    nc.scalar.activation(std[:, :], var_eps[:, :], ACT.Sqrt).then_inc(std_done, 1)

                for n, buf in enumerate((q_w, k_w, v_w)):
                    act.wait_ge(scaled, min(n + 1, 2))
                    nc.scalar.activation(heads[n][:, :, :], buf[:, :, :], ACT.Copy).then_inc(w_head_done, 1)

                def step(j, v):
                    t = 2 * j + v
                    first = isinstance(t, int) and t == 0
                    if not first:
                        act.wait_ge(out_ready, NOUT * t)
                    for c in range(NC):
                        act.wait_ge(transposed, NC * t + c + 1)
                        nc.scalar.activation(u_head[:, c, :], u_ps[:, c, :], ACT.Copy).then_inc(head_done, 1)
                    if not (isinstance(t, int) and t == NT - 1):
                        root(t + 1)
                    for k in range(8):
                        act.wait_ge(out_ready, NOUT * t + k + 1)
                        if not first and k == 0:
                            act.wait_ge(qk_stored, 64 * t)
                        nc.scalar.activation(qk[:, 2 * (k // 4), k % 4, :].bitcast(F32R), o_ps[:, k % 4, :],
                                             ACT.Copy).then_inc(copied, 1)
                    for k in (8, 10):
                        act.wait_ge(out_ready, NOUT * t + k + 1)
                        if not first and k == 8:
                            act.wait_ge(v_stored, 16 * t)
                        nc.scalar.activation(v_rows[:, k - 8, :], o_ps[:, k % 4, :], ACT.Copy).then_inc(copied, 1)

                root(0)
                rolled(act, 1, 2, NT, step, tail=1)

            @block.vector
            def _(dve):
                dve.wait_ge(w_loaded, 80)
                nc.vector.tensor_scalar(use_ra[:, 0], w_sr[:, 1], 0.1, None, ALU.is_gt).then_inc(mixed, 1)
                dve.wait_ge(mixed, 1)
                nc.vector.tensor_scalar(use_ra[:, 1], use_ra[:, 0], -1.0, 1.0, ALU.mult, ALU.add).then_inc(mixed, 1)
                nc.vector.tensor_scalar(w_sr[:, :, :], w_sr[:, :, :], 1e-8, None, ALU.max).then_inc(s_ready, 1)
                dve.wait_ge(mixed, 2)
                per_head = lambda buf, n: buf[:, n, :].unsqueeze(2).broadcast_to([P, HEADS, RA])
                for c in range(NC):
                    tail_of = lambda buf: buf[:, c, :].rearrange("p (h e) -> p h e", h=HEADS)[:, :, STD:HD]
                    q_t, k_t = tail_of(q_w), tail_of(k_w)
                    if c:
                        dve.wait_ge(mixed, 2 + 2 * c)
                    nc.vector.tensor_tensor(mix[:, 0], k_t, per_head(use_ra, 0), ALU.mult)
                    nc.vector.tensor_tensor(mix[:, 1], q_t, per_head(use_ra, 1), ALU.mult)
                    nc.vector.tensor_tensor(mix[:, 2], q_t, per_head(use_ra, 0), ALU.mult)
                    nc.vector.tensor_tensor(mix[:, 3], k_t, per_head(use_ra, 1), ALU.mult).then_inc(mixed, 1)
                    dve.wait_ge(mixed, 3 + 2 * c)
                    nc.vector.tensor_tensor(q_t, mix[:, 0], mix[:, 1], ALU.add)
                    nc.vector.tensor_tensor(k_t, mix[:, 2], mix[:, 3], ALU.add).then_inc(mixed, 1)
                dve.wait_ge(s_ready, 2)
                nc.vector.tensor_scalar(q_sr[:, :, :], s_sr[:, :, :], float(HD) ** -0.5, None, ALU.mult).then_inc(s_ready, 1)
                dve.wait_ge(s_ready, 3)
                dve.wait_ge(mixed, 2 + 2 * NC)
                for buf, scale in ((q_w, q_sr), (k_w, s_sr)):
                    for c in range(NC):
                        w = buf[:, c, :].rearrange("p (h e) -> p h e", h=HEADS)
                        nc.vector.tensor_tensor(w[:, :, 0:STD], w[:, :, 0:STD],
                                                scale[:, 0].unsqueeze(2).broadcast_to([P, HEADS, STD]), ALU.mult)
                        last = nc.vector.tensor_tensor(w[:, :, STD:HD], w[:, :, STD:HD], per_head(scale, 1), ALU.mult)
                    last.then_inc(scaled, 1)
                for n, buf in enumerate((q_w, k_w, v_w)):
                    dve.wait_ge(w_head_done, n + 1)
                    nc.vector.tensor_tensor(tails[n][:, :, :], buf[:, :, :], heads[n][:, :, :].bitcast(F32),
                                            ALU.subtract).then_inc(w_tail_done, 1)

                def norm(j, v):
                    t, u = 2 * j + v, v % 2
                    dve.wait_ge(x_loaded[u], 16 * (j + v // 2 + 1))
                    for s in range(NS):
                        last = nc.vector.bn_stats(stats[:, s, :], xb[:, u, s, :])
                    last.then_inc(stats_done, 1)
                    dve.wait_ge(stats_done, t + 1)
                    dve.sem_inc(dve_passed, 1)
                    for s in range(NS):
                        last = nc.vector.bn_aggr(mom[:, s, :], stats[:, s, :])
                    last.then_inc(mom_done, 1)
                    dve.wait_ge(mom_done, t + 1)
                    nc.vector.tensor_scalar(var_eps[:, :], mom[:, :, 1], EPS, None, ALU.add).then_inc(var_done, 1)
                    dve.wait_ge(std_done, t + 1)
                    nc.vector.reciprocal(rstd[:, :], std[:, :]).then_inc(rstd_done, 1)
                    dve.wait_ge(rstd_done, t + 1)
                    if not (isinstance(t, int) and t == 0):
                        dve.wait_ge(transposed, NC * t)
                    for s in range(NS):
                        last = nc.vector.tensor_scalar(uh[:, s, :], xb[:, u, s, :], mom[:, s, 0:1], rstd[:, s:s + 1],
                                                       ALU.subtract, ALU.mult)
                    last.then_inc(normed, 1)

                def step(j, v):
                    t = 2 * j + v
                    first = isinstance(t, int) and t == 0
                    for c in range(NC):
                        dve.wait_ge(head_done, NC * t + c + 1)
                        nc.vector.tensor_tensor(u_tail[:, c, :], u_ps[:, c, :], u_head[:, c, :].bitcast(F32),
                                                ALU.subtract).then_inc(tail_done, 1)
                    if not (isinstance(t, int) and t == NT - 1):
                        norm(j, v + 1)
                    for k in range(8):
                        dve.wait_ge(copied, 10 * t + k + 1)
                        if not first and k == 0:
                            dve.wait_ge(qk_stored, 64 * t)
                        n = 2 * (k // 4)
                        nc.vector.tensor_tensor(qk[:, n + 1, k % 4, :].bitcast(F32R), o_ps[:, k % 4, :], qk[:, n, k % 4, :],
                                                ALU.subtract).then_inc(split, 1)
                    for k in (9, 11):
                        dve.wait_ge(out_ready, NOUT * t + k + 1)
                        if not first and k == 9:
                            dve.wait_ge(v_stored, 16 * t)
                        nc.vector.tensor_copy(v_rows[:, k - 8, :], o_ps[:, k % 4, :]).then_inc(split, 1)

                norm(0, 0)
                rolled(dve, 1, 2, NT, step, tail=1)

            @block.tensor
            def _(pe):
                def step(j, v):
                    t = 2 * j + v
                    first = isinstance(t, int) and t == 0
                    pe.wait_ge(normed, t + 1)
                    if not first:
                        pe.wait_ge(tail_done, NC * t)
                    for c in range(NC):
                        for s in range(NS):
                            last = nc.tensor.transpose(u_ps[:, c, P * s:P * (s + 1)], uh[:, s, P * c:P * (c + 1)], ident[:, :])
                        last.then_inc(transposed, 1)
                    if first:
                        pe.wait_ge(w_tail_done, 3)
                    for k in range(NOUT):
                        if k >= 4:
                            if k < 9:
                                pe.wait_ge(split, 10 * t + k - 3)
                            elif k < 12:
                                pe.wait_ge(split, 10 * t + k - 3)
                        elif not first:
                            if k % 2:
                                pe.wait_ge(split, 10 * (t - 1) + (9 if k == 1 else 10))
                            else:
                                pe.wait_ge(copied, 10 * (t - 1) + (9 if k == 0 else 10))
                        out = o_ps[:, k % 4, :]
                        for c in range(NC):
                            if k == 0:
                                pe.wait_ge(tail_done, NC * t + c + 1)
                            if k < 8:
                                cols, n = slice(P * (k % 4), P * (k % 4 + 1)), k // 4
                                last = products3(nc, out, heads[n][:, c, cols], tails[n][:, c, cols], u_head[:, c, :],
                                                 u_tail[:, c, :], c == 0, c == NC - 1)
                            else:
                                cols = slice(P * (k - 8), P * (k - 7))
                                last = products3(nc, out, u_head[:, c, cols], u_tail[:, c, cols], heads[2][:, c, :],
                                                 tails[2][:, c, :], c == 0, c == NC - 1)
                        last.then_inc(out_ready, 1)

                rolled(pe, 1, 2, NT, step)




def stage5(nc, d, persist):
    G = HEADS // 4
    ITS = BATCH * G
    NB = SEQ // P
    QK = 3 * HD
    HALF = 512
    STEPS = [(0, k) for k in range(NB // 2)] + [(1, k) for k in range(NB)]
    NSTEP = len(STEPS)
    NADD = NSTEP - 2
    SCORES = [(i, 0, P * (i + 1), i) for i in range(NB // 2)]
    for i in range(NB // 2, NB):
        SCORES += [(i, 0, HALF, i), (i, HALF, P * (i + 1) - HALF, NB // 2 + i)]
    NSCORE = 4 * len(SCORES)
    FIRST_SCORES, SCORE_STEPS = 4, 6
    PER_STEP = NSCORE // SCORE_STEPS
    MAXIMA_STEP = FIRST_SCORES + SCORE_STEPS

    def lo(half, blk):
        return max(0, P * blk - HALF * half)

    def ring_uses(k, v, first, last):
        uses = []
        if k == 1 and not first:
            uses.append(("sum", 1))
        if k == 3 and not first and v % G == 0:
            uses += [("rows", i) for i in range(NB)]
        if FIRST_SCORES <= k < MAXIMA_STEP and not last:
            uses += [("score", s) for s in range(PER_STEP * (k - FIRST_SCORES), PER_STEP * (k - FIRST_SCORES + 1))]
        if k == 6:
            uses.append(("sum", 0))
        if k == MAXIMA_STEP and not last:
            uses.append(("maxima", 0))
        return uses

    USES = NSCORE + 3
    PERIOD = G * USES + NB

    def before(j, v):
        if v == 0:
            return NSCORE + 1
        return 2 * (NSCORE + 1) + 1 + PERIOD * j + USES * (v - 1) + NB * ((v - 1) // G)

    def parity(v):
        return before(0, v) % 2

    def kinds(j, v):
        return isinstance(j, int) and v == 0, isinstance(j, int) and v == ITS - 1

    with ExitStack() as ctx:
        sb = lambda name, shape, dt=F32: ctx.enter_context(nc.sbuf_tensor("s5_" + name, shape, dt))
        ps = lambda name, shape, dt=F32: ctx.enter_context(nc.psum_tensor("s5_" + name, shape, dt))
        sem = lambda name: ctx.enter_context(nc.semaphore("s5_" + name))
        q_st = sb("q_stack", [P, 2, 4, SEQ], F32R)
        k_st = sb("k_stack", [P, 2, 4, SEQ], F32R)
        v_in = sb("v_rows", [P, 2, NB, P])
        prob = sb("prob", [P, 2, 4, HALF])
        row_sum = sb("row_sum", [P, 2, 4, HALF])
        y_head = sb("y_head", [P, G, SEQ], F32R)
        y_tail = sb("y_tail", [P, G, SEQ], F32R)
        x_rows = sb("x_rows", [P, NB, DM])
        o_head = sb("o_head", [P, NC, DM], F32R)
        o_tail = sb("o_tail", [P, NC, DM], F32R)
        ones = sb("ones", [P, HD])
        ident = sb("ident", [P, P], BF16)
        mask_q = sb("mask_q", [P, P], BF16)
        mask_k = sb("mask_k", [P, P], BF16)
        mx = sb("mx", [P, 4, 3 * NB // 2])
        nm = sb("nm", [P, 4, 4, NB], F32R)
        nm_t = sb("nm_t", [2 * 4 * NB, P], F32R)
        rec = sb("rec", [P, HALF])
        yn = sb("yn", [P, 2, HALF])
        s_ps = ps("s_ps", [P, 2, HALF])
        e_ps = ps("e_ps", [P, 4, HALF])
        y_ps = ps("y_ps", [P, 2, HALF])

        qk_loaded = [sem("qk_loaded0"), sem("qk_loaded1")]
        v_loaded = [sem("v_loaded0"), sem("v_loaded1")]
        maxima_loaded, w_loaded, w_head_done, w_tail_done, made, ones_rows = (
            sem("maxima_loaded"), sem("w_loaded"), sem("w_head"), sem("w_tail"), sem("made"), sem("ones_rows"))
        x_loaded, stored = sem("x_loaded"), sem("stored")
        sp_passed = sem("sp_passed")
        ring_ready, ring_free = sem("ring_ready"), sem("ring_free")
        max_done, negated = sem("max"), sem("negated")
        e_ready, exp_done = sem("e_ready"), sem("exp")
        av_done, added = sem("av"), sem("added")
        yn_done, yh_done, yt_done = sem("yn"), sem("y_head"), sem("y_tail")

        with nc.Block() as block:
            @block.sync
            def _(sp):
                def load(j, v):
                    b, g, u = j + v // G, v % G, v % 2
                    for name, stack, order in (("q_s", q_st, (0, 1, 0)), ("k_s", k_st, (0, 0, 1))):
                        src = d[name].rearrange("b g a (h e) t -> b g a e h t", h=4)
                        for n, part in enumerate(order):
                            sp.dma_start(stack[HD * n:HD * (n + 1), u].bitcast(F32), src[b, g, part]).then_inc(qk_loaded[u], 16)
                    src = d["v_s"].rearrange("(b k p) (g c) -> b g p k c", b=BATCH, p=P, g=G)
                    sp.dma_start(v_in[:, u], src[b, g]).then_inc(v_loaded[u], 16)

                def maxima(j, v):
                    sp.wait_ge(ring_free, before(j, v) + 2)
                    for a in range(2):
                        sp.dma_start(q_st[QK + a:QK + a + 1, v % 2].bitcast(F32).rearrange("a h (k t) -> a (h k) t", k=NB),
                                     nm_t[4 * NB * a:4 * NB * (a + 1), :].bitcast(F32)).then_inc(maxima_loaded, 16)

                rows_of = lambda name: d[name].rearrange("(b k p) c -> b p k c", b=BATCH, p=P)
                sp.dma_start(x_rows[:, 0:NC, :], d["wp"].rearrange("(c p) m -> p c m", p=P)).then_inc(w_loaded, 16)
                load(0, 0)
                load(0, 1)
                maxima(0, 0)

                def store(b, uses):
                    sp.wait_ge(ring_free, uses + 2)
                    sp.sem_inc(sp_passed, 1)
                    sp.dma_start(rows_of("out")[b], x_rows[:, :, :]).then_inc(stored, 16)

                def step(j, v):
                    first, last = kinds(j, v)
                    b = j + v // G
                    if not first and not last:
                        sp.wait_ge(av_done, NSTEP * (G * j + v))
                        load(j, v + 1)
                    if v % G == 0:
                        if first:
                            sp.wait_ge(w_tail_done, 1)
                        else:
                            store(b - 1, before(j, v) + 1 + NB)
                            sp.wait_ge(stored, 16 * b)
                        sp.dma_start(x_rows[:, :, :], rows_of("x1_s")[b]).then_inc(x_loaded, 16)
                    if not last:
                        maxima(j, v + 1)

                rolled(sp, 1, G, ITS, step, tail=1)
                store(BATCH - 1, before(0, ITS - 1) + 2 + 1 + NB)
                sp.wait_ge(stored, 16 * BATCH)

            @block.gpsimd
            def _(pool):
                nc.gpsimd.memset(ident[:, :], 0.0).then_inc(made, 1)
                nc.gpsimd.memset(mask_q[:, :], 0.0).then_inc(made, 1)
                nc.gpsimd.memset(mask_k[:, :], 0.0).then_inc(made, 1)
                nc.gpsimd.memset(ones[:, :], 1.0).then_inc(made, 1)
                pool.wait_ge(made, 4)
                nc.gpsimd.affine_select(out=ident[:, :], in_=ident[:, :], compare_op=ALU.not_equal, fill=1.0, base=0,
                                        pattern=[[-1, P]], channel_multiplier=1).then_inc(made, 1)
                nc.gpsimd.affine_select(out=mask_q[:, :], in_=mask_q[:, :], compare_op=ALU.is_ge, fill=-1e30, base=0,
                                        pattern=[[-1, P]], channel_multiplier=1).then_inc(made, 1)
                nc.gpsimd.affine_select(out=mask_k[:, :], in_=mask_k[:, :], compare_op=ALU.is_ge, fill=-1e30, base=0,
                                        pattern=[[1, P]], channel_multiplier=-1).then_inc(made, 1)

                def step(j, v):
                    it = G * j + v
                    n = 0
                    for k, (half, blk) in enumerate(STEPS):
                        if blk == 0:
                            continue
                        pool.wait_ge(exp_done, 4 * (NSTEP * it + k + 1))
                        if blk == 1:
                            pool.wait_ge(av_done, NSTEP * it + k)
                        else:
                            pool.wait_ge(added, NADD * it + n)
                        acc = row_sum[:, half, :, lo(half, blk):HALF]
                        nc.gpsimd.tensor_tensor(acc, acc, prob[:, k % 2, :, 0:HALF - lo(half, blk)], ALU.add).then_inc(added, 1)
                        n += 1

                rolled(pool, 1, G, ITS, step, tail=1)

            @block.scalar
            def _(act):
                act.wait_ge(w_loaded, 16)
                nc.scalar.activation(o_head[:, :, :], x_rows[:, 0:NC, :], ACT.Copy).then_inc(w_head_done, 1)

                def head(j, v, half):
                    it = G * j + v
                    act.wait_ge(yn_done, 2 * it + half + 1)
                    nc.scalar.activation(y_head[:, v % G, HALF * half:HALF * (half + 1)], yn[:, half], ACT.Copy).then_inc(yh_done, 1)

                def step(j, v):
                    it = G * j + v
                    first, _ = kinds(j, v)
                    for k, (half, blk) in enumerate(STEPS):
                        c = lo(half, blk)
                        if blk == 0:
                            if not first:
                                act.wait_ge(yn_done, 2 * it - 1 + half)
                        elif not (first and k < 2):
                            act.wait_ge(av_done, NSTEP * it + k - 1)
                            prev = [m for m in range(k - 1) if m % 2 == k % 2 and STEPS[m][1]]
                            adds = sum(1 for m in range(prev[-1] + 1) if STEPS[m][1]) if prev else 0
                            if not (first and adds == 0):
                                act.wait_ge(added, NADD * it + adds)
                        for hh in range(4):
                            act.wait_ge(e_ready, 4 * (NSTEP * it + k) + hh + 1)
                            dst = row_sum[:, half, hh, :] if blk == 0 else prob[:, k % 2, hh, 0:HALF - c]
                            nc.scalar.activation(dst, e_ps[:, hh, c:HALF], ACT.Exp).then_inc(exp_done, 1)
                        if k == 1 and not first:
                            head(j, v - 1, 1)
                        if k == 7:
                            head(j, v, 0)

                rolled(act, 1, G, ITS, step, tail=1)
                head(0, ITS - 1, 1)

            @block.vector
            def _(dve):
                dve.sem_inc(ring_free, 2)
                nc.vector.memset(nm[:, 2:4, :, :].bitcast(F32), 0.0).then_inc(ones_rows, 1)
                nc.vector.memset(k_st[QK:QK + 2, :, :, :].bitcast(F32), 1.0).then_inc(ones_rows, 1)
                dve.wait_ge(w_head_done, 1)
                nc.vector.tensor_tensor(o_tail[:, :, :], x_rows[:, 0:NC, :], o_head[:, :, :].bitcast(F32),
                                        ALU.subtract).then_inc(w_tail_done, 1)

                def maximum(s, n, bank):
                    hh, (blk, key, keys, slot) = s // len(SCORES), SCORES[s % len(SCORES)]
                    dve.wait_ge(ring_ready, n + 1)
                    nc.vector.reduce_max(mx[:, hh, slot:slot + 1], s_ps[:, bank, 0:keys], axis=AX_X).then_inc(ring_free, 1)

                def negate(it, n):
                    dve.wait_ge(ring_free, n + 2)
                    late = mx[:, :, NB // 2:NB]
                    nc.vector.tensor_tensor(late, late, mx[:, :, NB:3 * NB // 2], ALU.max).then_inc(max_done, 1)
                    dve.wait_ge(max_done, it + 1)
                    nc.vector.tensor_scalar(nm[:, 0], mx[:, :, 0:NB], -1.0, None, ALU.mult).then_inc(negated, 1)
                    dve.wait_ge(negated, 2 * it + 1)
                    nc.vector.scalar_tensor_tensor(nm[:, 1], mx[:, :, 0:NB], -1.0, nm[:, 0].bitcast(F32),
                                                   ALU.mult, ALU.subtract).then_inc(negated, 1)

                def copy_maxima(it, n, bank):
                    dve.wait_ge(ring_ready, n + 1)
                    if not (isinstance(it, int) and it == 0):
                        dve.wait_ge(maxima_loaded, 32 * it)
                    nc.vector.tensor_copy(nm_t[:, :], s_ps[0:2 * 4 * NB, bank, 0:P]).then_inc(ring_free, 1)

                def normalise(j, v, half, n, bank):
                    it = G * j + v
                    first, _ = kinds(j, v)
                    dve.wait_ge(ring_ready, n + 1)
                    if not (first and half == 0):
                        dve.wait_ge(yn_done, 2 * it + half)
                    nc.vector.reciprocal(rec[:, :], s_ps[:, bank, :]).then_inc(ring_free, 1)
                    dve.wait_ge(ring_free, n + 3)
                    if not first:
                        dve.wait_ge(yt_done, 2 * it - 1 + half)
                    nc.vector.tensor_tensor(yn[:, half], y_ps[:, half], rec[:, :], ALU.mult).then_inc(yn_done, 1)

                def tail(j, v, half):
                    dve.wait_ge(yh_done, 2 * (G * j + v) + half + 1)
                    cols = slice(HALF * half, HALF * (half + 1))
                    nc.vector.tensor_tensor(y_tail[:, v % G, cols], yn[:, half], y_head[:, v % G, cols].bitcast(F32),
                                            ALU.subtract).then_inc(yt_done, 1)

                def add_rows(b, i, n, bank):
                    if i == 0:
                        dve.wait_ge(x_loaded, 16 * (b + 1))
                    dve.wait_ge(ring_ready, n + 1)
                    nc.vector.tensor_tensor(x_rows[:, i, :], x_rows[:, i, :], s_ps[:, bank, :], ALU.add).then_inc(ring_free, 1)

                for s in range(NSCORE):
                    maximum(s, s, s % 2)
                negate(0, NSCORE)
                copy_maxima(0, NSCORE, NSCORE % 2)

                def step(j, v):
                    it, n, bank = G * j + v, before(j, v), parity(v)
                    first, last = kinds(j, v)
                    for k in range(NSTEP):
                        if k == 2 and not first:
                            tail(j, v - 1, 1)
                        if k == 8:
                            tail(j, v, 0)
                        if k == MAXIMA_STEP and not last:
                            negate(it + 1, n)
                        for kind, arg in ring_uses(k, v, first, last):
                            if kind == "sum" and arg == 0:
                                normalise(j, v, 0, n, bank)
                            elif kind == "sum":
                                normalise(j, v - 1, 1, n, bank)
                            elif kind == "rows":
                                add_rows(j + v // G - 1, arg, n, bank)
                            elif kind == "score":
                                if arg == 0:
                                    dve.wait_ge(negated, 2 * it + 2)
                                maximum(arg, n, bank)
                            else:
                                copy_maxima(it + 1, n, bank)
                            n, bank = n + 1, 1 - bank

                rolled(dve, 1, G, ITS, step, tail=1)
                n = before(0, ITS - 1) + 2
                normalise(0, ITS - 1, 1, n, n % 2)
                tail(0, ITS - 1, 1)
                for i in range(NB):
                    add_rows(BATCH - 1, i, n + 1 + i, (n + 1 + i) % 2)

            @block.tensor
            def _(pe):
                def score(j, v, s, n, bank):
                    hh, (blk, key, keys, _) = s // len(SCORES), SCORES[s % len(SCORES)]
                    u, queries, diagonal = v % 2, slice(P * blk, P * (blk + 1)), key + keys == P * (blk + 1)
                    if s == 0:
                        pe.wait_ge(qk_loaded[u], 96 * (2 * j + v // 2 + 1))
                    pe.wait_ge(ring_free, n + 1)
                    last = nc.tensor.matmul(s_ps[:, bank, 0:keys], q_st[0:QK, u, hh, queries], k_st[0:QK, u, hh, key:key + keys],
                                            start=True, stop=not diagonal)
                    if diagonal:
                        last = nc.tensor.matmul(s_ps[:, bank, keys - P:keys], ident[:, :], mask_q[:, :], start=False, stop=True)
                    last.then_inc(ring_ready, 1)

                def turn_maxima(it, n, bank):
                    pe.wait_ge(negated, 2 * it + 2)
                    pe.wait_ge(ring_free, n + 1)
                    nc.tensor.transpose(s_ps[:, bank, 0:P], nm[:, :, :, :].bitcast(F32).rearrange("p a h k -> p (a h k)"),
                                        persist["ident"][:, :]).then_inc(ring_ready, 1)

                def exponents(j, v, k):
                    it, u, (half, blk) = G * j + v, v % 2, STEPS[k]
                    first, _ = kinds(j, v)
                    c, diagonal = lo(half, blk), blk // (NB // 2) == half
                    if k == 0:
                        pe.wait_ge(maxima_loaded, 32 * (it + 1))
                    for hh in range(4):
                        if not (first and k == 0):
                            pe.wait_ge(exp_done, 4 * (NSTEP * it + k) + hh - 3)
                        last = nc.tensor.matmul(e_ps[:, hh, c:HALF], k_st[0:QK + 2, u, hh, P * blk:P * (blk + 1)],
                                                q_st[0:QK + 2, u, hh, HALF * half + c:HALF * (half + 1)],
                                                start=True, stop=not diagonal)
                        if diagonal:
                            last = nc.tensor.matmul(e_ps[:, hh, c:c + P], ident[:, :], mask_k[:, :], start=False, stop=True)
                        last.then_inc(e_ready, 1)

                def weigh(j, v, k):
                    it, u, (half, blk) = G * j + v, v % 2, STEPS[k]
                    first, _ = kinds(j, v)
                    c = lo(half, blk)
                    if k == 0:
                        pe.wait_ge(v_loaded[u], 16 * (2 * j + v // 2 + 1))
                    if blk == 0 and not first:
                        pe.wait_ge(yn_done, 2 * it - 1 + half)
                    pe.wait_ge(exp_done, 4 * (NSTEP * it + k + 1))
                    for hh in range(4):
                        p = row_sum[:, half, hh, :] if blk == 0 else prob[:, k % 2, hh, 0:HALF - c]
                        last = nc.tensor.matmul(y_ps[HD * hh:HD * (hh + 1), half, c:HALF], v_in[:, u, blk, HD * hh:HD * (hh + 1)],
                                                p, start=blk == 0, stop=blk == NB // 2 * (half + 1) - 1)
                    last.then_inc(av_done, 1)

                def total(j, v, half, n, bank):
                    pe.wait_ge(added, NADD * (G * j + v) + (NB // 2 - 1 if half == 0 else NADD))
                    pe.wait_ge(ring_free, n + 1)
                    for hh in range(4):
                        last = nc.tensor.matmul(s_ps[HD * hh:HD * (hh + 1), bank, :], ones[:, :], row_sum[:, half, hh, :],
                                                start=True, stop=True)
                    last.then_inc(ring_ready, 1)

                def out_rows(its, i, n, bank):
                    if i == 0:
                        pe.wait_ge(yt_done, 2 * its)
                        pe.wait_ge(w_tail_done, 1)
                    pe.wait_ge(ring_free, n + 1)
                    tokens = slice(P * i, P * (i + 1))
                    for g in range(G):
                        last = products3(nc, s_ps[:, bank, :], y_head[:, g, tokens], y_tail[:, g, tokens], o_head[:, g, :],
                                         o_tail[:, g, :], g == 0, g == G - 1)
                    last.then_inc(ring_ready, 1)

                pe.wait_ge(made, 7)
                pe.wait_ge(ones_rows, 2)
                for s in range(NSCORE):
                    score(0, 0, s, s, s % 2)
                turn_maxima(0, NSCORE, NSCORE % 2)

                def step(j, v):
                    it, n, bank = G * j + v, before(j, v), parity(v)
                    first, last = kinds(j, v)
                    for k in range(NSTEP):
                        exponents(j, v, k)
                        if k:
                            weigh(j, v, k - 1)
                        elif not first:
                            weigh(j, v - 1, NSTEP - 1)
                        for kind, arg in ring_uses(k, v, first, last):
                            if kind == "sum" and arg == 0:
                                total(j, v, 0, n, bank)
                            elif kind == "sum":
                                total(j, v - 1, 1, n, bank)
                            elif kind == "rows":
                                out_rows(it, arg, n, bank)
                            elif kind == "score":
                                score(j, v + 1, arg, n, bank)
                            else:
                                turn_maxima(it + 1, n, bank)
                            n, bank = n + 1, 1 - bank

                rolled(pe, 1, G, ITS, step, tail=1)
                weigh(0, ITS - 1, NSTEP - 1)
                n = before(0, ITS - 1) + 2
                total(0, ITS - 1, 1, n, n % 2)
                for i in range(NB):
                    out_rows(ITS, i, n + 1 + i, (n + 1 + i) % 2)


def build(nc, d):
    scratch = {"z_s": (BATCH, NC, P, SEQ), "x_s": (BATCH, P, SEQ), "B_s": (BATCH, P, SEQ), "C_s": (BATCH, NC, P, SEQ),
               "dt_s": (BATCH, NC, 2, P, SEQ), "dtx_s": (BATCH, NC, 2, P, SEQ), "y_s": (BATCH, NC, P, SEQ),
               "x1_s": (BATCH * SEQ, DM), "q_s": (BATCH, NC, 2, P, SEQ), "k_s": (BATCH, NC, 2, P, SEQ), "v_s": (BATCH * SEQ, DM)}
    for name, shape in scratch.items():
        d[name] = nc.dram_tensor(name, shape, F32).ap()
    with ExitStack() as ctx:
        ident = ctx.enter_context(nc.sbuf_tensor("ident", [P, P], F32))
        mean_all = ctx.enter_context(nc.sbuf_tensor("mean_all", [P, NT * NS], F32))
        rstd_all = ctx.enter_context(nc.sbuf_tensor("rstd_all", [P, NT * NS], F32))
        ident_ready = ctx.enter_context(nc.semaphore("ident_ready"))
        persist = dict(ident=ident, mean_all=mean_all, rstd_all=rstd_all, ident_ready=ident_ready)
        with nc.Block() as block:
            @block.gpsimd
            def _(pool):
                nc.gpsimd.memset(ident[:, :], 0.0).then_inc(ident_ready, 1)
                pool.wait_ge(ident_ready, 1)
                nc.gpsimd.affine_select(out=ident[:, :], in_=ident[:, :], compare_op=ALU.not_equal, fill=1.0, base=0,
                                        pattern=[[-1, P]], channel_multiplier=1).then_inc(ident_ready, 1)
        for stage in STAGES:
            stage(nc, d, persist)


STAGES = [stage1, stage2, stage3, stage4, stage5]


def kernel(L0_attn_hidden_states, L0_attn_in_proj_w, L0_attn_dt_proj_w, L0_attn_dt_proj_b, L0_attn_A_log, L0_attn_D_param,
           L0_attn_out_proj_w, L0_attn_gate_w, L0_attn_up_w, L0_attn_down_w, L0_attn_norm1_w, L0_attn_norm2_w, L0_ffn_Wa,
           L0_ffn_Wp, L0_ffn_w_std, L0_ffn_w_rec):
    import concourse.bacc as bacc
    import numpy as np
    from concourse.bass_utils import run_bass_kernel_spmd

    def transposed(w):
        return np.ascontiguousarray(np.asarray(w).T)

    def blocks(w):
        return transposed(np.asarray(w).reshape(NC, P))

    wa, std = np.asarray(L0_ffn_Wa), HD - 8
    ends = np.cumsum([HEADS * std, HEADS * std, DM, HEADS * 8])
    q_std, k_std, v_cols, q_low, k_low = np.split(wa, ends, axis=1)

    def by_head(a, b):
        parts = [a.reshape(DM, HEADS, std), b.reshape(DM, HEADS, 8)]
        return np.ascontiguousarray(np.concatenate(parts, axis=2).reshape(DM, DM))

    arrays = {
        "x": np.ascontiguousarray(np.asarray(L0_attn_hidden_states).reshape(BATCH * SEQ, DM)),
        "in_w": transposed(L0_attn_in_proj_w), "dt_w": transposed(L0_attn_dt_proj_w),
        "norm1": blocks(L0_attn_norm1_w), "norm2": blocks(L0_attn_norm2_w),
        "dt_b": blocks(L0_attn_dt_proj_b), "D": blocks(L0_attn_D_param),
        "A_log": np.ascontiguousarray(np.asarray(L0_attn_A_log).reshape(NC, REP, 8, P).transpose(3, 0, 2, 1).reshape(P, P)),
        "out_w": transposed(L0_attn_out_proj_w), "gate_w": transposed(L0_attn_gate_w),
        "up_w": transposed(L0_attn_up_w), "down_w": transposed(L0_attn_down_w),
        "wq": by_head(q_std, q_low), "wk": by_head(k_std, k_low), "wv": np.ascontiguousarray(v_cols),
        "wp": np.ascontiguousarray(np.asarray(L0_ffn_Wp)),
        "w_std": np.ascontiguousarray(np.asarray(L0_ffn_w_std)), "w_rec": np.ascontiguousarray(np.asarray(L0_ffn_w_rec)),
    }
    nc = bacc.Bacc("TRN2", target_bir_lowering=False, num_devices=1)
    d = {name: nc.dram_tensor(name, a.shape, F32, kind="ExternalInput").ap() for name, a in arrays.items()}
    d["out"] = nc.dram_tensor("out", (BATCH * SEQ, DM), F32, kind="ExternalOutput").ap()
    build(nc, d)
    nc.compile()
    result = run_bass_kernel_spmd(nc, [arrays], core_ids=[0])
    return np.asarray(result.results[0]["out"]).reshape(BATCH, SEQ, DM)
```

```python
from contextlib import ExitStack

import concourse.bass as bass
from concourse import mybir

F32 = mybir.dt.float32
F32R = mybir.dt.float32r
BF16 = mybir.dt.bfloat16
ALU = mybir.AluOpType
ACT = mybir.ActivationFunctionType
AX_X = mybir.AxisListType.X

P = 128
EPS = 1e-5
BATCH, SEQ, DM = 4, 1024, 512
NC = DM // P
STATE = 32
REP = 4
FF = 1408
NF = FF // P
TT = 512
NT = BATCH * SEQ // TT
NS = TT // P
UP = SEQ // TT
HEADS, HD = 16, 32


def rolled(eng, first, period, total, emit, tail=0):
    n = (total - first - tail) // period
    for v in range(first):
        emit(0, v)
    with eng.Fori(0, n) as j:
        for v in range(first, first + period):
            emit(j, v)
    for v in range(first + n * period, total):
        emit(0, v)


def split_weight(nc, dve, ready, n, head, tail, full):
    nc.vector.tensor_copy(head, full).then_inc(ready, 1)
    dve.wait_ge(ready, n + 1)
    nc.vector.tensor_tensor(tail, full, head.bitcast(F32), ALU.subtract).then_inc(ready, 1)


def products3(nc, out, w_head, w_tail, x_head, x_tail, first, last):
    nc.tensor.matmul(out, w_head, x_head, start=first, stop=False)
    nc.tensor.matmul(out, w_head, x_tail, start=False, stop=False)
    return nc.tensor.matmul(out, w_tail, x_head, start=False, stop=last)


def stage1(nc, d, persist):
    ident, mean_all, rstd_all = persist["ident"], persist["mean_all"], persist["rstd_all"]
    x_v = d["x"].rearrange("(b u s p) c -> b u p s c", b=BATCH, u=UP, p=P)
    ORDER = [10, 4, 5, 6, 7, 8, 9, None, None, None, None, 0, 1, 2, 3]
    NOUT = len(ORDER)
    USES = [sum(1 for k in range(NOUT) if k % 4 == b) for b in range(4)]

    with ExitStack() as ctx:
        sb = lambda name, shape, dt=F32: ctx.enter_context(nc.sbuf_tensor("s1_" + name, shape, dt))
        ps = lambda name, shape, dt=F32: ctx.enter_context(nc.psum_tensor("s1_" + name, shape, dt))
        sem = lambda name: ctx.enter_context(nc.semaphore("s1_" + name))
        w_head = sb("in_w_head", [P, NC, FF], F32R)
        w_tail = sb("in_w_tail", [P, NC, FF], F32R)
        dtw_head = sb("dt_w_head", [P, DM], F32R)
        dtw_tail = sb("dt_w_tail", [P, DM], F32R)
        norm1 = sb("norm1", [P, NC])
        dt_bias = sb("dt_bias", [P, NC])
        xb = sb("x_rows", [P, 2, NS, DM])
        uh = sb("u_rows", [P, NS, DM])
        u_head = sb("u_head", [P, NC, TT], F32R)
        u_tail = sb("u_tail", [P, NC, TT], F32R)
        stats = sb("stats", [P, NS, 6])
        mom = sb("moments", [P, NS, 2])
        var_eps = sb("var_eps", [P, NS])
        std1 = sb("std1", [P, NS])
        rstd1 = sb("rstd1", [P, NS])
        ms2 = sb("ms2", [P, NS])
        std2 = sb("std2", [P, NS])
        rstd2 = sb("rstd2", [P, NS])
        scale12 = sb("scale12", [P, NS])
        dtr_head = sb("dt_raw_head", [P, TT], F32R)
        dtr_tail = sb("dt_raw_tail", [P, TT], F32R)
        x_ch = sb("x_channels", [P, TT])
        x_rep = sb("x_repeated", [P, NC, TT])
        bcz = sb("bcz", [P, 9, TT])
        mag = sb("magnitude", [P, NC, TT])
        pos = sb("positive", [P, NC, TT])
        one_e = sb("one_plus_e", [P, NC, TT])
        log_w = sb("log_w", [P, NC, TT])
        inv_w = sb("inv_w", [P, NC, TT])
        parts = sb("parts", [P, 4, NC * TT])
        w_full = parts[:, :, :].rearrange("p a n -> p (a n)")[:, 0:NC * FF].rearrange("p (c m) -> p c m", c=NC)
        dtw_full = parts[:, 3, NC * TT - DM:NC * TT]
        u_ps = ps("u_ps", [P, NC, TT])
        o_ps = ps("o_ps", [P, 4, TT])

        w_loaded, w_ready = sem("w_loaded"), sem("w_ready")
        sp_passed, dve_passed = sem("sp_passed"), sem("dve_passed")
        x_loaded = [sem("x_loaded0"), sem("x_loaded1")]
        stats_done, mom_done, var_done, std1_done, rstd1_done = (
            sem("stats"), sem("moments"), sem("var_eps"), sem("std1"), sem("rstd1"))
        sq_done, ms_done, std2_done, rstd2_done, scale_done = (
            sem("sq"), sem("ms"), sem("std2"), sem("rstd2"), sem("scale"))
        normed = sem("normed")
        transposed = sem("transposed")
        head_done, tail_done = sem("u_head"), sem("u_tail")
        out_ready = sem("out_ready")
        o_free = [sem(f"o_free{b}") for b in range(4)]
        dtr_head_done = sem("dt_raw_head")
        x_repeated = sem("x_repeated")
        stored = [sem("stored_bc"), sem("stored_z"), sem("stored_parts"), sem("stored_x")]
        e_done, ln_masked, one_e_done, ln_done, inv_done = (
            sem("e"), sem("ln_masked"), sem("one_e"), sem("ln"), sem("inv"))
        err_done, corr_done, log1p_done, dt_done, dtx_done = (
            sem("err"), sem("corr"), sem("log1p"), sem("dt"), sem("dtx"))
        ph_done, parts_done = sem("part_heads"), sem("parts")

        by_dve, by_act = (2, 4, 6, 11, 13), (3, 5, 12, 14)

        def freed(k, t):
            return USES[k % 4] * t + k // 4 + 2

        with nc.Block() as block:
            @block.sync
            def _(sp):
                sp.dma_start(w_full, d["in_w"].rearrange("(c p) m -> p c m", p=P)).then_inc(w_loaded, 16)
                sp.dma_start(dtw_full, d["dt_w"]).then_inc(w_loaded, 16)
                sp.dma_start(norm1[:, :], d["norm1"]).then_inc(w_loaded, 16)
                sp.dma_start(dt_bias[:, :], d["dt_b"]).then_inc(w_loaded, 16)
                for u in range(2):
                    sp.dma_start(xb[:, u], x_v[0, u]).then_inc(x_loaded[u], 16)

                def step(j, v):
                    t, b, u = 2 * j + v, j + v // 2, v % 2
                    if not (isinstance(t, int) and t >= NT - 2):
                        sp.wait_ge(normed, t + 1)
                        sp.dma_start(xb[:, u], x_v[b + 1, u]).then_inc(x_loaded[u], 16)
                    tok = slice(u * TT, (u + 1) * TT)
                    sp.wait_ge(o_free[1], freed(1, t))
                    sp.wait_ge(dtx_done, t + 1)
                    for g in range(NC):
                        for r in range(REP):
                            sp.dma_start(x_rep[STATE * r:STATE * (r + 1), g, :],
                                         x_ch[STATE * g:STATE * (g + 1), :]).then_inc(x_repeated, 16)
                    sp.dma_start(d["x_s"][b, :, tok], x_ch[:, :]).then_inc(stored[3], 16)
                    for k in range(3, 7):
                        sp.wait_ge(o_free[k % 4], freed(k, t))
                        if k % 4 == 3:
                            sp.sem_inc(sp_passed, 1)
                    sp.dma_start(d["B_s"][b, :, tok], bcz[:, 0, :]).then_inc(stored[0], 16)
                    sp.dma_start(d["C_s"][b, :, :, tok].rearrange("k p t -> p k t"),
                                 bcz[:, 1:5, :]).then_inc(stored[0], 16)
                    for k in range(11, 15):
                        sp.wait_ge(o_free[k % 4], freed(k, t))
                        if k % 4 == 3:
                            sp.sem_inc(sp_passed, 1)
                    sp.dma_start(d["z_s"][b, :, :, tok].rearrange("k p t -> p k t"),
                                 bcz[:, 5:9, :]).then_inc(stored[1], 16)
                    sp.wait_ge(parts_done, t + 1)
                    for n, name in enumerate(("dt_s", "dtx_s")):
                        for part in range(2):
                            for half in range(2):
                                rows = slice(64 * part, 64 * part + 64)
                                src = parts[64 * half:64 * half + 64, 2 * n + part, :]
                                sp.dma_start(d[name][b, :, half, rows, tok].rearrange("k c t -> c k t"),
                                             src.rearrange("c (k t) -> c k t", k=NC)).then_inc(stored[2], 16)

                rolled(sp, 0, 2, NT, step, tail=2)
                sp.wait_ge(stored[3], 16 * NT)
                sp.wait_ge(stored[0], 32 * NT)
                sp.wait_ge(stored[1], 16 * NT)
                sp.wait_ge(stored[2], 128 * NT)

            @block.vector
            def _(dve):
                dve.sem_inc(tail_done, 1)
                dve.wait_ge(w_loaded, 64)
                for c in range(NC):
                    last = nc.vector.tensor_scalar(w_full[:, c, :], w_full[:, c, :], norm1[:, c:c + 1], None, ALU.mult)
                last.then_inc(w_ready, 1)
                dve.wait_ge(w_ready, 1)
                split_weight(nc, dve, w_ready, 1, w_head[:, :, :], w_tail[:, :, :], w_full)
                split_weight(nc, dve, w_ready, 3, dtw_head[:, :], dtw_tail[:, :], dtw_full)

                def norm(j, v):
                    t, u = 2 * j + v, v % 2
                    dve.wait_ge(x_loaded[u], 16 * (j + v // 2 + 1))
                    for s in range(NS):
                        last = nc.vector.bn_stats(stats[:, s, :], xb[:, u, s, :])
                    last.then_inc(stats_done, 1)
                    dve.wait_ge(stats_done, t + 1)
                    dve.sem_inc(dve_passed, 1)
                    for s in range(NS):
                        last = nc.vector.bn_aggr(mom[:, s, :], stats[:, s, :])
                    last.then_inc(mom_done, 1)
                    dve.wait_ge(mom_done, t + 1)
                    nc.vector.tensor_copy(mean_all[:, bass.ds(NS * t, NS)], mom[:, :, 0])
                    nc.vector.tensor_scalar(var_eps[:, :], mom[:, :, 1], EPS, None, ALU.add).then_inc(var_done, 1)
                    dve.wait_ge(std1_done, t + 1)
                    nc.vector.reciprocal(rstd1[:, :], std1[:, :]).then_inc(rstd1_done, 1)
                    dve.wait_ge(rstd1_done, t + 1)
                    nc.vector.tensor_copy(rstd_all[:, bass.ds(NS * t, NS)], rstd1[:, :])
                    nc.vector.tensor_tensor(ms2[:, :], rstd1[:, :], rstd1[:, :], ALU.mult).then_inc(sq_done, 1)
                    dve.wait_ge(sq_done, 2 * t + 1)
                    nc.vector.tensor_tensor(ms2[:, :], ms2[:, :], mom[:, :, 1], ALU.mult).then_inc(sq_done, 1)
                    dve.wait_ge(sq_done, 2 * t + 2)
                    nc.vector.tensor_scalar(ms2[:, :], ms2[:, :], EPS, None, ALU.add).then_inc(ms_done, 1)
                    dve.wait_ge(std2_done, t + 1)
                    nc.vector.reciprocal(rstd2[:, :], std2[:, :]).then_inc(rstd2_done, 1)
                    dve.wait_ge(rstd2_done, t + 1)
                    nc.vector.tensor_tensor(scale12[:, :], rstd1[:, :], rstd2[:, :], ALU.mult).then_inc(scale_done, 1)
                    dve.wait_ge(scale_done, t + 1)
                    if not (isinstance(t, int) and t == 0):
                        dve.wait_ge(transposed, NC * t)
                    for s in range(NS):
                        last = nc.vector.tensor_scalar(uh[:, s, :], xb[:, u, s, :], mom[:, s, 0:1], scale12[:, s:s + 1],
                                                       ALU.subtract, ALU.mult)
                    last.then_inc(normed, 1)

                def tails(j, v):
                    t = 2 * j + v
                    for c in range(NC):
                        dve.wait_ge(head_done, NC * t + c + 1)
                        nc.vector.tensor_tensor(u_tail[:, c, :], u_ps[:, c, :], u_head[:, c, :].bitcast(F32),
                                                ALU.subtract).then_inc(tail_done, 1)

                def finish(j, v):
                    t = 2 * j + v
                    dve.wait_ge(dtx_done, t + 2)
                    if not (isinstance(t, int) and t == 0):
                        dve.wait_ge(stored[2], 128 * t)
                    flat = lambda buf: buf[:, :, :].rearrange("p k t -> p (k t)")
                    nc.vector.tensor_copy(parts[:, 0, :].bitcast(F32R), flat(log_w))
                    nc.vector.tensor_copy(parts[:, 2, :].bitcast(F32R), flat(inv_w)).then_inc(ph_done, 1)
                    dve.wait_ge(ph_done, t + 1)
                    nc.vector.tensor_tensor(parts[:, 1, :].bitcast(F32R), flat(log_w), parts[:, 0, :], ALU.subtract)
                    nc.vector.tensor_tensor(parts[:, 3, :].bitcast(F32R), flat(inv_w), parts[:, 2, :],
                                            ALU.subtract).then_inc(parts_done, 1)

                def copies(j, v):
                    t = 2 * j + v
                    dve.wait_ge(dtr_head_done, t + 1)
                    nc.vector.tensor_tensor(dtr_tail[:, :], o_ps[:, 0, :], dtr_head[:, :].bitcast(F32),
                                            ALU.subtract).then_inc(o_free[0], 1)
                    for k in by_dve:
                        if k == 11:
                            if not (isinstance(t, int) and t == 0):
                                finish(j, v - 1)
                            dve.wait_ge(e_done, t + 1)
                            nc.vector.tensor_scalar(one_e[:, :, :], mag[:, :, :], 1.0, None, ALU.add).then_inc(one_e_done, 1)
                        dve.wait_ge(out_ready, NOUT * t + k + 1)
                        if not (isinstance(t, int) and t == 0):
                            if k == 2:
                                dve.wait_ge(stored[0], 32 * t)
                            if k == 11:
                                dve.wait_ge(stored[1], 16 * t)
                        slot = k - 2 if k < 7 else k - 6
                        nc.vector.tensor_copy(bcz[:, slot, :], o_ps[:, k % 4, :]).then_inc(o_free[k % 4], 1)
                    dve.wait_ge(ln_done, t + 1)
                    nc.vector.scalar_tensor_tensor(log_w[:, :, :], one_e[:, :, :], 1.0, log_w[:, :, :],
                                                   ALU.is_gt, ALU.mult).then_inc(ln_masked, 1)
                    nc.vector.scalar_tensor_tensor(one_e[:, :, :], one_e[:, :, :], 1.0, mag[:, :, :],
                                                   ALU.subtract, ALU.subtract).then_inc(err_done, 1)

                def step(j, v):
                    tails(j, v)
                    if not (isinstance(j, int) and v == NT - 1):
                        norm(j, v + 1)
                    copies(j, v)

                norm(0, 0)
                rolled(dve, 1, 2, NT, step, tail=1)
                finish(0, NT - 1)

            @block.scalar
            def _(act):
                act.sem_inc(o_free[1], 1)
                act.sem_inc(o_free[0], 1)
                act.sem_inc(o_free[2], 1)
                act.sem_inc(o_free[3], 1)

                def roots(t):
                    act.wait_ge(var_done, t + 1)
                    nc.scalar.activation(std1[:, :], var_eps[:, :], ACT.Sqrt).then_inc(std1_done, 1)
                    act.wait_ge(ms_done, t + 1)
                    nc.scalar.activation(std2[:, :], ms2[:, :], ACT.Sqrt).then_inc(std2_done, 1)

                def step(j, v):
                    t = 2 * j + v
                    first = isinstance(t, int) and t == 0
                    if not first:
                        act.wait_ge(out_ready, NOUT * t)
                    for c in range(NC):
                        act.wait_ge(transposed, NC * t + c + 1)
                        nc.scalar.activation(u_head[:, c, :], u_ps[:, c, :], ACT.Copy).then_inc(head_done, 1)
                    if not (isinstance(t, int) and t == NT - 1):
                        roots(t + 1)
                    act.wait_ge(out_ready, NOUT * t + 1)
                    nc.scalar.activation(dtr_head[:, :], o_ps[:, 0, :], ACT.Copy).then_inc(dtr_head_done, 1)
                    act.wait_ge(out_ready, NOUT * t + 2)
                    if not first:
                        act.wait_ge(stored[3], 16 * t)
                        act.wait_ge(x_repeated, 256 * t)
                    nc.scalar.activation(x_ch[:, :], o_ps[:, 1, :], ACT.Copy).then_inc(o_free[1], 1)
                    for k in range(3, NOUT):
                        if k in by_act:
                            act.wait_ge(out_ready, NOUT * t + k + 1)
                            if not first:
                                if k == 3:
                                    act.wait_ge(stored[0], 32 * t)
                                if k == 12:
                                    act.wait_ge(stored[1], 16 * t)
                            slot = k - 2 if k < 7 else k - 6
                            nc.scalar.activation(bcz[:, slot, :], o_ps[:, k % 4, :], ACT.Copy).then_inc(o_free[k % 4], 1)
                        if k == 7 and not first:
                            act.wait_ge(dtx_done, t + 1)
                        if 7 <= k < 11:
                            c = k - 7
                            act.wait_ge(out_ready, NOUT * t + k + 1)
                            nc.scalar.activation(mag[:, c, :], o_ps[:, k % 4, :], ACT.Abs, bias=dt_bias[:, c:c + 1])
                            nc.scalar.activation(pos[:, c, :], o_ps[:, k % 4, :], ACT.Relu,
                                                 bias=dt_bias[:, c:c + 1]).then_inc(o_free[k % 4], 1)
                        if k == 10:
                            act.wait_ge(o_free[2], freed(10, t))
                            nc.scalar.activation(mag[:, :, :], mag[:, :, :], ACT.Exp, scale=-1.0).then_inc(e_done, 1)
                            act.wait_ge(one_e_done, t + 1)
                            if not first:
                                act.wait_ge(parts_done, t)
                            nc.scalar.activation(log_w[:, :, :], one_e[:, :, :], ACT.Ln).then_inc(ln_done, 1)
                            act.wait_ge(ln_masked, t + 1)
                            nc.scalar.activation(inv_w[:, :, :], log_w[:, :, :], ACT.Exp, scale=-1.0).then_inc(inv_done, 1)

                roots(0)
                rolled(act, 1, 2, NT, step, tail=1)

            @block.gpsimd
            def _(pool):
                pool.sem_inc(dtx_done, 1)

                def step(j, v):
                    t = 2 * j + v
                    pool.wait_ge(err_done, t + 1)
                    pool.wait_ge(inv_done, t + 1)
                    nc.gpsimd.tensor_tensor(inv_w[:, :, :], inv_w[:, :, :], one_e[:, :, :], ALU.mult).then_inc(corr_done, 1)
                    pool.wait_ge(corr_done, t + 1)
                    nc.gpsimd.tensor_tensor(log_w[:, :, :], log_w[:, :, :], inv_w[:, :, :], ALU.subtract).then_inc(log1p_done, 1)
                    pool.wait_ge(log1p_done, t + 1)
                    pool.wait_ge(o_free[2], freed(10, t))
                    nc.gpsimd.tensor_tensor(log_w[:, :, :], log_w[:, :, :], pos[:, :, :], ALU.add).then_inc(dt_done, 1)
                    pool.wait_ge(dt_done, t + 1)
                    pool.wait_ge(x_repeated, 256 * (t + 1))
                    nc.gpsimd.tensor_tensor(inv_w[:, :, :], log_w[:, :, :], x_rep[:, :, :], ALU.mult).then_inc(dtx_done, 1)

                rolled(pool, 1, 2, NT, step)

            @block.tensor
            def _(pe):
                def step(j, v):
                    t = 2 * j + v
                    first = isinstance(t, int) and t == 0
                    pe.wait_ge(normed, t + 1)
                    pe.wait_ge(tail_done, NC * t + 1)
                    for c in range(NC):
                        for s in range(NS):
                            last = nc.tensor.transpose(u_ps[:, c, P * s:P * (s + 1)], uh[:, s, P * c:P * (c + 1)], ident[:, :])
                        last.then_inc(transposed, 1)
                    if first:
                        pe.wait_ge(w_ready, 5)
                    for k, m in enumerate(ORDER):
                        uses = USES[k % 4] * t + k // 4
                        pe.wait_ge(o_free[k % 4], uses + 1)
                        out = o_ps[:, k % 4, :]
                        if m is None:
                            rows = slice(P * (k - 7), P * (k - 6))
                            last = products3(nc, out, dtw_head[:, rows], dtw_tail[:, rows], dtr_head[:, :], dtr_tail[:, :],
                                             True, True)
                        else:
                            rows = slice(P * m, P * (m + 1))
                            for c in range(NC):
                                if k == 0:
                                    pe.wait_ge(tail_done, NC * t + c + 2)
                                last = products3(nc, out, w_head[:, c, rows], w_tail[:, c, rows], u_head[:, c, :],
                                                 u_tail[:, c, :], c == 0, c == NC - 1)
                        last.then_inc(out_ready, 1)

                pe.wait_ge(persist["ident_ready"], 2)
                rolled(pe, 1, 2, NT, step)
    return None


def stage2(nc, d, persist):
    ITS = BATCH * NC
    TILES = P // 4
    with ExitStack() as ctx:
        sb = lambda name, shape, dt=F32: ctx.enter_context(nc.sbuf_tensor("s2_" + name, shape, dt))
        ps = lambda name, shape, dt=F32: ctx.enter_context(nc.psum_tensor("s2_" + name, shape, dt))
        sem = lambda name: ctx.enter_context(nc.semaphore("s2_" + name))
        dt_in = sb("dt_in", [P, 2, 2, SEQ], F32R)
        dtx_in = sb("dtx_in", [P, 2, 2, SEQ], F32R)
        B_in = sb("B_in", [P, 2, SEQ])
        C_in = sb("C_in", [P, 2, REP, SEQ])
        x_in = sb("x_in", [P, 2, SEQ])
        y_sb = sb("y_sb", [P, 2, SEQ])
        negA = sb("negA", [P, ITS * TILES])
        D_all = sb("D_all", [P, ITS])
        A_cur = sb("A_cur", [P, 2, TILES])
        D_cur = sb("D_cur", [P, 2, 1])
        dtxB = sb("dtxB", [P, 4, SEQ])
        h = sb("h", [P, 4, SEQ])
        hc = sb("hc", [P, 8, SEQ])
        ones = sb("ones", [P, 16 * 128])
        spread = sb("spread", [P, 16, P], F32R)
        gather = sb("gather", [P, 8, STATE])
        dt_ps = ps("dt_ps", [P, 2, SEQ])
        dtx_ps = ps("dtx_ps", [P, SEQ])
        y_ps = ps("y_ps", [P, SEQ])

        loaded = [sem("loaded0"), sem("loaded1")]
        const_loaded, A_ready, made = sem("const_loaded"), sem("A_ready"), sem("made")
        A_copied = sem("A_copied")
        dt_ready, exp_done = sem("dt_ready"), sem("exp_done")
        dtx_ready, b_done = sem("dtx_ready"), sem("b_done")
        scanned, multiplied = sem("scanned"), sem("multiplied")
        summed = sem("summed")
        y_out = sem("y_out")
        y_stored = [sem("y_stored0"), sem("y_stored1")]
        DMAS = 14

        with nc.Block() as block:
            @block.sync
            def _(sp):
                for b in range(BATCH):
                    sp.dma_start(negA[:, P * b:P * (b + 1)], d["A_log"]).then_inc(const_loaded, 16)
                    sp.dma_start(D_all[:, NC * b:NC * (b + 1)], d["D"]).then_inc(const_loaded, 16)

                def load(it, u):
                    flat = lambda name: d[name].rearrange("b k h r t -> (b k) r h t")
                    inc = lambda ins: ins.then_inc(loaded[u], 16)
                    inc(sp.dma_start(dt_in[:, u].bitcast(F32), flat("dt_s")[it]))
                    inc(sp.dma_start(dtx_in[:, u].bitcast(F32), flat("dtx_s")[it]))
                    for n in range(4):
                        rows = slice(STATE * n, STATE * (n + 1))
                        inc(sp.dma_start(B_in[rows, u], d["B_s"].rearrange("b (g n) t -> (b g) n t", n=STATE)[it]))
                        inc(sp.dma_start(C_in[rows, u], d["C_s"].rearrange("b k (r n) t -> (b k) n r t", n=STATE)[it]))
                        inc(sp.dma_start(x_in[rows, u], d["x_s"].rearrange("b (g n) t -> (b g) n t", n=STATE)[it]))

                def store(it, u):
                    sp.dma_start(d["y_s"].rearrange("b k p t -> (b k) p t")[it], y_sb[:, u]).then_inc(y_stored[u], 16)

                def step(j, v):
                    it, u = 2 * j + v, v % 2
                    if not (isinstance(j, int) and j == 0 and v < 2):
                        sp.wait_ge(y_out, it + 1)
                        store(it - 2, u)
                    load(it, u)

                assert DMAS == 2 + 3 * 4
                rolled(sp, 2, 2, ITS, step)
                for it in (ITS - 2, ITS - 1):
                    sp.wait_ge(y_out, it + 3)
                    store(it, it % 2)
                for u in range(2):
                    sp.wait_ge(y_stored[u], 16 * (ITS // 2))

            @block.gpsimd
            def _(pool):
                pool.sem_inc(multiplied, 4)
                nc.gpsimd.memset(ones[:, :], 0.0).then_inc(made, 1)
                pat = ones[:, :].rearrange("p (q j n) -> p q j n", q=16, j=4)
                pool.wait_ge(made, 1)
                for n in range(2):
                    nc.gpsimd.affine_select(out=pat, in_=pat, compare_op=ALU.not_equal, fill=1.0, base=-64 * n,
                                            pattern=[[-4, 16], [-1, 4], [0, STATE]], channel_multiplier=1).then_inc(made, 1)
                    pool.wait_ge(made, n + 2)
                nc.gpsimd.tensor_copy(spread[:, :, :].rearrange("p q m -> p (q m)"), ones[:, :]).then_inc(made, 1)
                nc.gpsimd.memset(gather[:, :, :], 1.0).then_inc(made, 1)
                pool.wait_ge(made, 5)
                nc.gpsimd.affine_select(out=gather[:, :, :], in_=gather[:, :, :], compare_op=ALU.is_ge, fill=0.0, base=0,
                                        pattern=[[P, 8], [-STATE, STATE]], channel_multiplier=1).then_inc(made, 1)
                pool.wait_ge(made, 6)
                nc.gpsimd.affine_select(out=gather[:, :, :], in_=gather[:, :, :], compare_op=ALU.is_ge, fill=0.0,
                                        base=STATE - 1, pattern=[[-P, 8], [STATE, STATE]],
                                        channel_multiplier=-1).then_inc(made, 1)

                def step(j, v):
                    w, u = 2 * TILES * j + v, (v // TILES) % 2
                    r = v % 4
                    if v % TILES == 0:
                        pool.wait_ge(loaded[u], 16 * DMAS * (j + v // (2 * TILES) + 1))
                    pool.wait_ge(scanned, w + 5)
                    if v % 4 == 0:
                        pool.wait_ge(summed, 2 * TILES // 4 * j + v // 4 + 1)
                    nc.gpsimd.tensor_tensor(hc[:, v % 8], h[:, v % 4], C_in[:, u, r], ALU.mult).then_inc(multiplied, 1)

                rolled(pool, 0, 2 * TILES, ITS * TILES, step)

            @block.scalar
            def _(act):
                act.wait_ge(const_loaded, 32 * BATCH)
                nc.scalar.activation(negA[:, :], negA[:, :], ACT.Exp).then_inc(A_ready, 1)
                act.wait_ge(A_ready, 1)
                nc.scalar.mul(negA[:, :], negA[:, :], -1.0).then_inc(A_ready, 1)

                def step(j, v):
                    w, u = 2 * TILES * j + v, (v // TILES) % 2
                    if v % TILES == 0:
                        act.wait_ge(A_copied, 2 * j + v // TILES + 1)
                    for k in range(2):
                        act.wait_ge(dt_ready, 2 * w + k + 1)
                        tok = dt_ps[:, v % 2, 512 * k:512 * (k + 1)]
                        nc.scalar.activation(tok, tok, ACT.Exp,
                                             scale=A_cur[:, u, v % TILES:v % TILES + 1]).then_inc(exp_done, 1)

                rolled(act, 0, 2 * TILES, ITS * TILES, step)

            @block.vector
            def _(dve):
                dve.sem_inc(scanned, 4)
                dve.sem_inc(b_done, 1)
                dve.sem_inc(y_out, 2)
                dve.wait_ge(A_ready, 2)

                def evac(it, u, n):
                    dve.wait_ge(A_copied, it + 1)
                    dve.wait_ge(summed, TILES // 4 * (it + 1) + 2)
                    if not (isinstance(n, int) and n == 0):
                        dve.wait_ge(y_stored[u], 16 * n)
                    nc.vector.scalar_tensor_tensor(y_sb[:, u], x_in[:, u], D_cur[:, u], y_ps[:, :],
                                                   ALU.mult, ALU.add).then_inc(y_out, 1)

                def scan(w, slot):
                    dve.wait_ge(b_done, w + 2)
                    dve.wait_ge(exp_done, 2 * w + 2)
                    dve.wait_ge(multiplied, w + 1)
                    nc.vector.tensor_tensor_scan(h[:, slot], dt_ps[:, slot % 2], dtxB[:, slot], 0.0,
                                                 ALU.mult, ALU.add).then_inc(scanned, 1)

                def step(j, v):
                    w, it, u = 2 * TILES * j + v, 2 * j + v // TILES, (v // TILES) % 2
                    if v % TILES == 0:
                        dve.wait_ge(loaded[u], 16 * DMAS * (j + v // (2 * TILES) + 1))
                        nc.vector.tensor_copy(D_cur[:, u], D_all[:, bass.ds(it, 1)])
                        nc.vector.tensor_copy(A_cur[:, u], negA[:, bass.ds(TILES * it, TILES)]).then_inc(A_copied, 1)
                    dve.wait_ge(dtx_ready, w + 1)
                    dve.wait_ge(scanned, w + 1)
                    nc.vector.tensor_tensor(dtxB[:, v % 4], dtx_ps[:, :], B_in[:, u], ALU.mult).then_inc(b_done, 1)
                    if not (isinstance(j, int) and j == 0 and v == 0):
                        scan(w - 1, (v - 1) % 4)
                    if v >= TILES and v % TILES == 6:
                        vb = v // TILES - 1
                        evac(2 * j + vb, vb % 2, j + vb // 2)

                rolled(dve, 7, 2 * TILES, ITS * TILES, step)
                scan(ITS * TILES - 1, 3)
                evac(ITS - 1, 1, ITS // 2 - 1)

            @block.tensor
            def _(pe):
                pe.sem_inc(summed, 2)
                LAG = 6

                def spread_tile(j, v):
                    w, u = 2 * TILES * j + v, (v // TILES) % 2
                    q, r = (v % TILES) // 4, v % 4
                    half, sel = r // 2, (r % 2) * 8 + q
                    if v % TILES == 0:
                        pe.wait_ge(loaded[u], 16 * DMAS * (j + v // (2 * TILES) + 1))
                    pe.wait_ge(b_done, w + 1)
                    for k in range(2):
                        cols = slice(512 * k, 512 * (k + 1))
                        last = nc.tensor.matmul(dtx_ps[:, cols], spread[:, sel], dtx_in[:, u, half, cols], start=True, stop=True)
                    last.then_inc(dtx_ready, 1)
                    pe.wait_ge(scanned, w + 3)
                    for k in range(2):
                        cols = slice(512 * k, 512 * (k + 1))
                        nc.tensor.matmul(dt_ps[:, v % 2, cols], spread[:, sel], dt_in[:, u, half, cols],
                                         start=True, stop=True).then_inc(dt_ready, 1)

                def sum_tiles(j, v, k):
                    w, q = 2 * TILES * j + v, (v % TILES) // 4
                    if q == 0 and k == 0:
                        pe.wait_ge(y_out, 2 * j + v // TILES + 2)
                    pe.wait_ge(multiplied, w + 8)
                    for r in range(4):
                        last = nc.tensor.matmul(y_ps[STATE * r:STATE * (r + 1), 512 * k:512 * (k + 1)], gather[:, q],
                                                hc[:, (v + r) % 8, 512 * k:512 * (k + 1)], start=(q == 0), stop=(q == 7))
                    if k == 1:
                        last.then_inc(summed, 1)

                def step(j, v):
                    spread_tile(j, v)
                    for k in range(2):
                        if v % 4 == (LAG + k) % 4 and not (isinstance(j, int) and j == 0 and v < LAG + k):
                            sum_tiles(j, v - LAG - k, k)

                pe.wait_ge(made, 7)
                rolled(pe, LAG + 1, 2 * TILES, ITS * TILES, step)
                for k in range(2):
                    sum_tiles(0, ITS * TILES - 4, k)


def stage3(nc, d, persist):
    ident, mean_all, rstd_all = persist["ident"], persist["mean_all"], persist["rstd_all"]
    rows_v = lambda name: d[name].rearrange("(b u s p) c -> b u p s c", b=BATCH, u=UP, p=P)
    with ExitStack() as ctx:
        sb = lambda name, shape, dt=F32: ctx.enter_context(nc.sbuf_tensor("s3_" + name, shape, dt))
        ps = lambda name, shape, dt=F32: ctx.enter_context(nc.psum_tensor("s3_" + name, shape, dt))
        sem = lambda name: ctx.enter_context(nc.semaphore("s3_" + name))
        out_head, out_tail = (sb(n, [P, NC, DM], F32R) for n in ("out_head", "out_tail"))
        gate_head, gate_tail = (sb(n, [P, NC, FF], F32R) for n in ("gate_head", "gate_tail"))
        up_head, up_tail = (sb(n, [P, NC, FF], F32R) for n in ("up_head", "up_tail"))
        down_head, down_tail = (sb(n, [P, NF, DM], F32R) for n in ("down_head", "down_tail"))
        norm2 = sb("norm2", [P, NC])
        work = sb("work", [P, 3, NC * TT])
        Y, Z, X = (work[:, n, :].rearrange("p (k t) -> p k t", k=NC) for n in range(3))
        a_head = sb("a_head", [P, NC, TT], F32R)
        a_tail = sb("a_tail", [P, NC, TT], F32R)
        sg = sb("silu_gate", [P, TT])
        gu = sb("gate_up", [P, TT])
        gu_head = sb("gu_head", [P, 2, TT], F32R)
        gu_tail = sb("gu_tail", [P, 2, TT], F32R)
        sumsq = sb("sumsq", [P, NS])
        msq = sb("msq", [P, NS])
        std = sb("std", [P, NS])
        rstd = sb("rstd", [P, NS])
        mean_cur = sb("mean_cur", [P, NS])
        rstd_cur = sb("rstd_cur", [P, NS])
        gu_ps = ps("gu_ps", [P, 4, TT])
        acc_ps = ps("acc_ps", [P, NC, TT])

        w_loaded = [sem(f"w_loaded{n}") for n in range(4)]
        w_head_done, w_tail_done, cur_done = sem("w_head"), sem("w_tail"), sem("cur")
        norm_loaded = sem("norm_loaded")
        sp_passed = sem("sp_passed")
        yz_loaded, x_loaded, x1_stored = sem("yz_loaded"), sem("x_loaded"), sem("x1_stored")
        silu_z, gated, a_head_y, a_tail_y = sem("silu_z"), sem("gated"), sem("a_head_y"), sem("a_tail_y")
        o_ready, u0_done, h_done, xh_done = sem("o_ready"), sem("u0"), sem("h"), sem("xh")
        sq_done, msq_done, std_done, rstd_done, hn_done = (
            sem("sq"), sem("msq"), sem("std"), sem("rstd"), sem("hn"))
        transposed, a_head_x, a_tail_x = sem("transposed"), sem("a_head_x"), sem("a_tail_x")
        gu_ready = sem("gu_ready")
        sg_done, gu_done, guh_done, gut_done = sem("sg"), sem("gu"), sem("gu_head"), sem("gu_tail")
        down_done = sem("down")
        x1_done = sem("x1")

        weights = [(d["out_w"], out_head, out_tail, NC, DM, False), (d["gate_w"], gate_head, gate_tail, NC, FF, True),
                   (d["up_w"], up_head, up_tail, NC, FF, True), (d["down_w"], down_head, down_tail, NF, DM, False)]
        SLOT = FF
        flat = work[:, :, :].rearrange("p a n -> p (a n)")
        pieces = []
        for src, head, tail, blocks, cols, scaled in weights:
            per = max(1, SLOT // cols)
            for c in range(0, blocks, per):
                n = min(per, blocks - c)
                slot = len(pieces) % 4
                pieces.append((src.rearrange("(c p) m -> p c m", p=P)[:, c:c + n, :],
                               flat[:, slot * SLOT:slot * SLOT + n * cols].rearrange("p (c m) -> p c m", c=n),
                               head[:, c:c + n, :], tail[:, c:c + n, :], norm2[:, c:c + 1] if scaled else 1.0))
        first_gate = 2
        assert NC * DM <= 2 * SLOT

        with nc.Block() as block:
            @block.sync
            def _(sp):
                sp.dma_start(norm2[:, :], d["norm2"]).then_inc(norm_loaded, 16)
                for n, (src, slot, _, _, _) in enumerate(pieces):
                    if n >= 4:
                        sp.wait_ge(w_tail_done, n - 3)
                    sp.dma_start(slot, src).then_inc(w_loaded[n % 4], 16)
                sp.wait_ge(w_tail_done, len(pieces))

                def step(j, v):
                    t, b, u = 2 * j + v, j + v // 2, v % 2
                    first = isinstance(t, int) and t == 0
                    tok = slice(u * TT, (u + 1) * TT)
                    if not first:
                        sp.wait_ge(hn_done, NS * t)
                        sp.wait_ge(xh_done, t)
                        sp.wait_ge(transposed, NC * t)
                    sp.dma_start(Y, d["y_s"][b, :, :, tok].rearrange("k p t -> p k t")).then_inc(yz_loaded, 16)
                    sp.dma_start(Z, d["z_s"][b, :, :, tok].rearrange("k p t -> p k t")).then_inc(yz_loaded, 16)
                    if not first:
                        sp.wait_ge(x1_done, t)
                        sp.sem_inc(sp_passed, 1)
                        sp.dma_start(rows_v("x1_s")[j + (v - 1) // 2, (v - 1) % 2], X).then_inc(x1_stored, 16)
                        sp.wait_ge(x1_stored, 16 * t)
                    sp.dma_start(X, rows_v("x")[b, u]).then_inc(x_loaded, 16)

                rolled(sp, 1, 2, NT, step)
                sp.wait_ge(x1_done, NT)
                sp.dma_start(rows_v("x1_s")[BATCH - 1, UP - 1], X).then_inc(x1_stored, 16)
                sp.wait_ge(x1_stored, 16 * NT)

            @block.scalar
            def _(act):
                act.wait_ge(norm_loaded, 16)
                for n, (_, slot, head, _, scale) in enumerate(pieces):
                    act.wait_ge(w_loaded[n % 4], 16 * (n // 4 + 1))
                    nc.scalar.activation(head, slot, ACT.Copy, scale=scale).then_inc(w_head_done, 1)

                def step(j, v):
                    t = 2 * j + v
                    first = isinstance(t, int) and t == 0
                    act.wait_ge(yz_loaded, 32 * (t + 1))
                    nc.scalar.activation(Z, Z, ACT.Silu).then_inc(silu_z, 1)
                    act.wait_ge(gated, t + 1)
                    if not first:
                        act.wait_ge(gu_ready, 2 * NF * t)
                    nc.scalar.activation(a_head[:, :, :], Y, ACT.Copy).then_inc(a_head_y, 1)
                    for s in range(NS):
                        act.wait_ge(h_done, NS * t + s + 1)
                        last = nc.scalar.activation(Z[:, s, :], Y[:, s, :], ACT.Square, accum_out=sumsq[:, s:s + 1])
                    last.then_inc(sq_done, 1)
                    act.wait_ge(msq_done, t + 1)
                    nc.scalar.activation(std[:, :], msq[:, :], ACT.Sqrt).then_inc(std_done, 1)
                    act.wait_ge(rstd_done, t + 1)
                    for s in range(NS):
                        nc.scalar.activation(Z[:, s, :], Y[:, s, :], ACT.Copy, scale=rstd[:, s:s + 1]).then_inc(hn_done, 1)
                    act.wait_ge(o_ready, NS * (t + 1))
                    for c in range(NC):
                        act.wait_ge(transposed, NC * t + c + 1)
                        nc.scalar.activation(a_head[:, c, :], acc_ps[:, c, :], ACT.Copy).then_inc(a_head_x, 1)
                    for f in range(NF):
                        n = NF * t + f
                        act.wait_ge(gu_ready, 2 * n + 1)
                        if not (first and f == 0):
                            act.wait_ge(gu_done, n)
                        nc.scalar.activation(sg[:, :], gu_ps[:, 2 * f % 4, :], ACT.Silu).then_inc(sg_done, 1)
                        act.wait_ge(gu_done, n + 1)
                        if not (first and f < 2):
                            act.wait_ge(down_done, n - 1)
                        nc.scalar.activation(gu_head[:, f % 2, :], gu[:, :], ACT.Copy).then_inc(guh_done, 1)

                rolled(act, 1, 2, NT, step)

            @block.vector
            def _(dve):
                for n, (_, slot, head, tail, scale) in enumerate(pieces):
                    dve.wait_ge(w_head_done, n + 1)
                    nc.vector.scalar_tensor_tensor(tail, slot, scale, head.bitcast(F32), ALU.mult,
                                                   ALU.subtract).then_inc(w_tail_done, 1)

                def step(j, v):
                    t = 2 * j + v
                    first = isinstance(t, int) and t == 0
                    dve.wait_ge(silu_z, t + 1)
                    nc.vector.tensor_tensor(Y, Y, Z, ALU.mult).then_inc(gated, 1)
                    dve.wait_ge(a_head_y, t + 1)
                    nc.vector.tensor_tensor(a_tail[:, :, :], Y, a_head[:, :, :].bitcast(F32), ALU.subtract).then_inc(a_tail_y, 1)
                    dve.wait_ge(x_loaded, 16 * (t + 1))
                    dve.wait_ge(a_tail_y, t + 1)
                    nc.vector.tensor_copy(mean_cur[:, :], mean_all[:, bass.ds(NS * t, NS)])
                    nc.vector.tensor_copy(rstd_cur[:, :], rstd_all[:, bass.ds(NS * t, NS)]).then_inc(cur_done, 1)
                    dve.wait_ge(cur_done, t + 1)
                    for s in range(NS):
                        last = nc.vector.tensor_scalar(Y[:, s, :], X[:, s, :], mean_cur[:, s:s + 1], rstd_cur[:, s:s + 1],
                                                       ALU.subtract, ALU.mult)
                    last.then_inc(u0_done, 1)
                    dve.wait_ge(u0_done, t + 1)
                    for s in range(NS):
                        dve.wait_ge(o_ready, NS * t + s + 1)
                        nc.vector.tensor_tensor(Y[:, s, :], Y[:, s, :], gu_ps[:, s, :], ALU.add).then_inc(h_done, 1)
                    dve.wait_ge(h_done, NS * (t + 1))
                    dve.wait_ge(sq_done, t + 1)
                    nc.vector.tensor_scalar(msq[:, :], sumsq[:, :], 1.0 / DM, EPS, ALU.mult, ALU.add).then_inc(msq_done, 1)
                    nc.vector.tensor_tensor(X, X, Y, ALU.add).then_inc(xh_done, 1)
                    dve.wait_ge(std_done, t + 1)
                    nc.vector.reciprocal(rstd[:, :], std[:, :]).then_inc(rstd_done, 1)
                    for c in range(NC):
                        dve.wait_ge(a_head_x, NC * t + c + 1)
                        nc.vector.tensor_tensor(a_tail[:, c, :], acc_ps[:, c, :], a_head[:, c, :].bitcast(F32),
                                                ALU.subtract).then_inc(a_tail_x, 1)
                    for f in range(NF):
                        n = NF * t + f
                        dve.wait_ge(sg_done, n + 1)
                        dve.wait_ge(gu_ready, 2 * n + 2)
                        if not (first and f == 0):
                            dve.wait_ge(gut_done, n)
                        nc.vector.tensor_tensor(gu[:, :], sg[:, :], gu_ps[:, (2 * f + 1) % 4, :], ALU.mult).then_inc(gu_done, 1)
                        dve.wait_ge(guh_done, n + 1)
                        nc.vector.tensor_tensor(gu_tail[:, f % 2, :], gu[:, :], gu_head[:, f % 2, :].bitcast(F32),
                                                ALU.subtract).then_inc(gut_done, 1)
                    dve.wait_ge(down_done, NF * (t + 1))
                    dve.wait_ge(xh_done, t + 1)
                    nc.vector.tensor_tensor(X, X, acc_ps[:, :, :], ALU.add).then_inc(x1_done, 1)

                rolled(dve, 1, 2, NT, step)

            @block.tensor
            def _(pe):
                def step(j, v):
                    t = 2 * j + v
                    first = isinstance(t, int) and t == 0
                    if first:
                        pe.wait_ge(w_tail_done, first_gate)
                    pe.wait_ge(a_tail_y, t + 1)
                    if not first:
                        pe.wait_ge(gut_done, NF * t)
                    for s in range(NS):
                        for c in range(NC):
                            cols = slice(P * s, P * (s + 1))
                            last = products3(nc, gu_ps[:, s, :], a_head[:, c, cols], a_tail[:, c, cols], out_head[:, c, :],
                                             out_tail[:, c, :], c == 0, c == NC - 1)
                        last.then_inc(o_ready, 1)
                    if not first:
                        pe.wait_ge(x1_done, t)
                    pe.wait_ge(hn_done, NS * (t + 1))
                    for c in range(NC):
                        for s in range(NS):
                            last = nc.tensor.transpose(acc_ps[:, c, P * s:P * (s + 1)], Z[:, s, P * c:P * (c + 1)], ident[:, :])
                        last.then_inc(transposed, 1)
                    if first:
                        pe.wait_ge(w_tail_done, len(pieces))

                    def down(f):
                        pe.wait_ge(gut_done, NF * t + f + 1)
                        if f == 0:
                            pe.wait_ge(a_tail_x, NC * (t + 1))
                        for s in range(NS):
                            cols = slice(P * s, P * (s + 1))
                            last = products3(nc, acc_ps[:, s, :], gu_head[:, f % 2, cols], gu_tail[:, f % 2, cols],
                                             down_head[:, f, :], down_tail[:, f, :], f == 0, f == NF - 1)
                        last.then_inc(down_done, 1)

                    for f in range(NF):
                        n = NF * t + f
                        if not (first and f < 2):
                            pe.wait_ge(gu_done, n - 1)
                        if f < 2:
                            pe.wait_ge(h_done, NS * (t + 1))
                        rows = slice(P * f, P * (f + 1))
                        for k, (head, tail) in enumerate(((gate_head, gate_tail), (up_head, up_tail))):
                            for c in range(NC):
                                if f == 0 and k == 0:
                                    pe.wait_ge(a_tail_x, NC * t + c + 1)
                                last = products3(nc, gu_ps[:, (2 * f + k) % 4, :], head[:, c, rows], tail[:, c, rows],
                                                 a_head[:, c, :], a_tail[:, c, :], c == 0, c == NC - 1)
                            last.then_inc(gu_ready, 1)
                        if f:
                            down(f - 1)
                    down(NF - 1)

                rolled(pe, 1, 2, NT, step)


def stage4(nc, d, persist):
    ident = persist["ident"]
    RA = 8
    STD = HD - RA
    rows_v = lambda name: d[name].rearrange("(b u s p) c -> b u p s c", b=BATCH, u=UP, p=P)
    with ExitStack() as ctx:
        sb = lambda name, shape, dt=F32: ctx.enter_context(nc.sbuf_tensor("s4_" + name, shape, dt))
        ps = lambda name, shape, dt=F32: ctx.enter_context(nc.psum_tensor("s4_" + name, shape, dt))
        sem = lambda name: ctx.enter_context(nc.semaphore("s4_" + name))
        q_w, k_w, v_w = (sb(n, [P, NC, DM]) for n in ("q_w", "k_w", "v_w"))
        heads = [sb(n, [P, NC, DM], F32R) for n in ("q_head", "k_head", "v_head")]
        tails = [sb(n, [P, NC, DM], F32R) for n in ("q_tail", "k_tail", "v_tail")]
        w_sr = sb("w_sr", [P, 2, HEADS])
        s_sr = sb("s_sr", [P, 2, HEADS])
        q_sr = sb("q_sr", [P, 2, HEADS])
        use_ra = sb("use_ra", [P, 2, HEADS])
        mix = sb("mix", [P, 4, HEADS, RA])
        xb = sb("x_rows", [P, 2, NS, DM])
        uh = sb("u_rows", [P, NS, DM])
        stats = sb("stats", [P, NS, 6])
        mom = sb("moments", [P, NS, 2])
        var_eps = sb("var_eps", [P, NS])
        std = sb("std", [P, NS])
        rstd = sb("rstd", [P, NS])
        u_head = sb("u_head", [P, NC, TT], F32R)
        u_tail = sb("u_tail", [P, NC, TT], F32R)
        qk = sb("qk", [P, 4, NC, TT])
        v_rows = sb("v_rows", [P, NS, DM])
        u_ps = ps("u_ps", [P, NC, TT])
        o_ps = ps("o_ps", [P, 4, TT])

        w_loaded, s_ready, mixed, scaled = sem("w_loaded"), sem("s_ready"), sem("mixed"), sem("scaled")
        w_head_done, w_tail_done = sem("w_head"), sem("w_tail")
        dve_passed = sem("dve_passed")
        x_loaded = [sem("x_loaded0"), sem("x_loaded1")]
        stats_done, mom_done, var_done, std_done, rstd_done, normed = (
            sem("stats"), sem("moments"), sem("var_eps"), sem("std"), sem("rstd"), sem("normed"))
        transposed, head_done, tail_done = sem("transposed"), sem("u_head"), sem("u_tail")
        out_ready = sem("out_ready")
        copied, split = sem("copied"), sem("split")
        qk_stored, v_stored = sem("qk_stored"), sem("v_stored")
        NOUT = 12

        with nc.Block() as block:
            @block.sync
            def _(sp):
                for buf, name in ((q_w, "wq"), (k_w, "wk"), (v_w, "wv")):
                    sp.dma_start(buf[:, :, :], d[name].rearrange("(c p) m -> p c m", p=P)).then_inc(w_loaded, 16)
                for n, name in enumerate(("w_std", "w_rec")):
                    sp.dma_start(w_sr[:, n, :], d[name].partition_broadcast(P)).then_inc(w_loaded, 16)
                for u in range(2):
                    sp.dma_start(xb[:, u], rows_v("x1_s")[0, u]).then_inc(x_loaded[u], 16)

                def step(j, v):
                    t, b, u = 2 * j + v, j + v // 2, v % 2
                    tok = slice(u * TT, (u + 1) * TT)
                    if not (isinstance(t, int) and t >= NT - 2):
                        sp.wait_ge(normed, t + 1)
                        sp.dma_start(xb[:, u], rows_v("x1_s")[b + 1, u]).then_inc(x_loaded[u], 16)
                    sp.wait_ge(split, 10 * t + 8)
                    for n, name in enumerate(("q_s", "q_s", "k_s", "k_s")):
                        sp.dma_start(d[name][b, :, n % 2, :, tok].rearrange("k p t -> p k t"), qk[:, n]).then_inc(qk_stored, 16)
                    sp.wait_ge(split, 10 * t + 10)
                    sp.wait_ge(copied, 10 * t + 10)
                    sp.dma_start(rows_v("v_s")[b, u], v_rows[:, :, :]).then_inc(v_stored, 16)

                rolled(sp, 0, 2, NT, step, tail=2)
                sp.wait_ge(qk_stored, 64 * NT)
                sp.wait_ge(v_stored, 16 * NT)

            @block.scalar
            def _(act):
                act.wait_ge(s_ready, 1)
                nc.scalar.activation(s_sr[:, :, :], w_sr[:, :, :], ACT.Sqrt).then_inc(s_ready, 1)

                def root(t):
                    act.wait_ge(var_done, t + 1)
                    nc.scalar.activation(std[:, :], var_eps[:, :], ACT.Sqrt).then_inc(std_done, 1)

                for n, buf in enumerate((q_w, k_w, v_w)):
                    act.wait_ge(scaled, min(n + 1, 2))
                    nc.scalar.activation(heads[n][:, :, :], buf[:, :, :], ACT.Copy).then_inc(w_head_done, 1)

                def step(j, v):
                    t = 2 * j + v
                    first = isinstance(t, int) and t == 0
                    if not first:
                        act.wait_ge(out_ready, NOUT * t)
                    for c in range(NC):
                        act.wait_ge(transposed, NC * t + c + 1)
                        nc.scalar.activation(u_head[:, c, :], u_ps[:, c, :], ACT.Copy).then_inc(head_done, 1)
                    if not (isinstance(t, int) and t == NT - 1):
                        root(t + 1)
                    for k in range(8):
                        act.wait_ge(out_ready, NOUT * t + k + 1)
                        if not first and k == 0:
                            act.wait_ge(qk_stored, 64 * t)
                        nc.scalar.activation(qk[:, 2 * (k // 4), k % 4, :].bitcast(F32R), o_ps[:, k % 4, :],
                                             ACT.Copy).then_inc(copied, 1)
                    for k in (8, 10):
                        act.wait_ge(out_ready, NOUT * t + k + 1)
                        if not first and k == 8:
                            act.wait_ge(v_stored, 16 * t)
                        nc.scalar.activation(v_rows[:, k - 8, :], o_ps[:, k % 4, :], ACT.Copy).then_inc(copied, 1)

                root(0)
                rolled(act, 1, 2, NT, step, tail=1)

            @block.vector
            def _(dve):
                dve.wait_ge(w_loaded, 80)
                nc.vector.tensor_scalar(use_ra[:, 0], w_sr[:, 1], 0.1, None, ALU.is_gt).then_inc(mixed, 1)
                dve.wait_ge(mixed, 1)
                nc.vector.tensor_scalar(use_ra[:, 1], use_ra[:, 0], -1.0, 1.0, ALU.mult, ALU.add).then_inc(mixed, 1)
                nc.vector.tensor_scalar(w_sr[:, :, :], w_sr[:, :, :], 1e-8, None, ALU.max).then_inc(s_ready, 1)
                dve.wait_ge(mixed, 2)
                per_head = lambda buf, n: buf[:, n, :].unsqueeze(2).broadcast_to([P, HEADS, RA])
                for c in range(NC):
                    tail_of = lambda buf: buf[:, c, :].rearrange("p (h e) -> p h e", h=HEADS)[:, :, STD:HD]
                    q_t, k_t = tail_of(q_w), tail_of(k_w)
                    if c:
                        dve.wait_ge(mixed, 2 + 2 * c)
                    nc.vector.tensor_tensor(mix[:, 0], k_t, per_head(use_ra, 0), ALU.mult)
                    nc.vector.tensor_tensor(mix[:, 1], q_t, per_head(use_ra, 1), ALU.mult)
                    nc.vector.tensor_tensor(mix[:, 2], q_t, per_head(use_ra, 0), ALU.mult)
                    nc.vector.tensor_tensor(mix[:, 3], k_t, per_head(use_ra, 1), ALU.mult).then_inc(mixed, 1)
                    dve.wait_ge(mixed, 3 + 2 * c)
                    nc.vector.tensor_tensor(q_t, mix[:, 0], mix[:, 1], ALU.add)
                    nc.vector.tensor_tensor(k_t, mix[:, 2], mix[:, 3], ALU.add).then_inc(mixed, 1)
                dve.wait_ge(s_ready, 2)
                nc.vector.tensor_scalar(q_sr[:, :, :], s_sr[:, :, :], float(HD) ** -0.5, None, ALU.mult).then_inc(s_ready, 1)
                dve.wait_ge(s_ready, 3)
                dve.wait_ge(mixed, 2 + 2 * NC)
                for buf, scale in ((q_w, q_sr), (k_w, s_sr)):
                    for c in range(NC):
                        w = buf[:, c, :].rearrange("p (h e) -> p h e", h=HEADS)
                        nc.vector.tensor_tensor(w[:, :, 0:STD], w[:, :, 0:STD],
                                                scale[:, 0].unsqueeze(2).broadcast_to([P, HEADS, STD]), ALU.mult)
                        last = nc.vector.tensor_tensor(w[:, :, STD:HD], w[:, :, STD:HD], per_head(scale, 1), ALU.mult)
                    last.then_inc(scaled, 1)
                for n, buf in enumerate((q_w, k_w, v_w)):
                    dve.wait_ge(w_head_done, n + 1)
                    nc.vector.tensor_tensor(tails[n][:, :, :], buf[:, :, :], heads[n][:, :, :].bitcast(F32),
                                            ALU.subtract).then_inc(w_tail_done, 1)

                def norm(j, v):
                    t, u = 2 * j + v, v % 2
                    dve.wait_ge(x_loaded[u], 16 * (j + v // 2 + 1))
                    for s in range(NS):
                        last = nc.vector.bn_stats(stats[:, s, :], xb[:, u, s, :])
                    last.then_inc(stats_done, 1)
                    dve.wait_ge(stats_done, t + 1)
                    dve.sem_inc(dve_passed, 1)
                    for s in range(NS):
                        last = nc.vector.bn_aggr(mom[:, s, :], stats[:, s, :])
                    last.then_inc(mom_done, 1)
                    dve.wait_ge(mom_done, t + 1)
                    nc.vector.tensor_scalar(var_eps[:, :], mom[:, :, 1], EPS, None, ALU.add).then_inc(var_done, 1)
                    dve.wait_ge(std_done, t + 1)
                    nc.vector.reciprocal(rstd[:, :], std[:, :]).then_inc(rstd_done, 1)
                    dve.wait_ge(rstd_done, t + 1)
                    if not (isinstance(t, int) and t == 0):
                        dve.wait_ge(transposed, NC * t)
                    for s in range(NS):
                        last = nc.vector.tensor_scalar(uh[:, s, :], xb[:, u, s, :], mom[:, s, 0:1], rstd[:, s:s + 1],
                                                       ALU.subtract, ALU.mult)
                    last.then_inc(normed, 1)

                def step(j, v):
                    t = 2 * j + v
                    first = isinstance(t, int) and t == 0
                    for c in range(NC):
                        dve.wait_ge(head_done, NC * t + c + 1)
                        nc.vector.tensor_tensor(u_tail[:, c, :], u_ps[:, c, :], u_head[:, c, :].bitcast(F32),
                                                ALU.subtract).then_inc(tail_done, 1)
                    if not (isinstance(t, int) and t == NT - 1):
                        norm(j, v + 1)
                    for k in range(8):
                        dve.wait_ge(copied, 10 * t + k + 1)
                        if not first and k == 0:
                            dve.wait_ge(qk_stored, 64 * t)
                        n = 2 * (k // 4)
                        nc.vector.tensor_tensor(qk[:, n + 1, k % 4, :].bitcast(F32R), o_ps[:, k % 4, :], qk[:, n, k % 4, :],
                                                ALU.subtract).then_inc(split, 1)
                    for k in (9, 11):
                        dve.wait_ge(out_ready, NOUT * t + k + 1)
                        if not first and k == 9:
                            dve.wait_ge(v_stored, 16 * t)
                        nc.vector.tensor_copy(v_rows[:, k - 8, :], o_ps[:, k % 4, :]).then_inc(split, 1)

                norm(0, 0)
                rolled(dve, 1, 2, NT, step, tail=1)

            @block.tensor
            def _(pe):
                def step(j, v):
                    t = 2 * j + v
                    first = isinstance(t, int) and t == 0
                    pe.wait_ge(normed, t + 1)
                    if not first:
                        pe.wait_ge(tail_done, NC * t)
                    for c in range(NC):
                        for s in range(NS):
                            last = nc.tensor.transpose(u_ps[:, c, P * s:P * (s + 1)], uh[:, s, P * c:P * (c + 1)], ident[:, :])
                        last.then_inc(transposed, 1)
                    if first:
                        pe.wait_ge(w_tail_done, 3)
                    for k in range(NOUT):
                        if k >= 4:
                            if k < 9:
                                pe.wait_ge(split, 10 * t + k - 3)
                            elif k < 12:
                                pe.wait_ge(split, 10 * t + k - 3)
                        elif not first:
                            if k % 2:
                                pe.wait_ge(split, 10 * (t - 1) + (9 if k == 1 else 10))
                            else:
                                pe.wait_ge(copied, 10 * (t - 1) + (9 if k == 0 else 10))
                        out = o_ps[:, k % 4, :]
                        for c in range(NC):
                            if k == 0:
                                pe.wait_ge(tail_done, NC * t + c + 1)
                            if k < 8:
                                cols, n = slice(P * (k % 4), P * (k % 4 + 1)), k // 4
                                last = products3(nc, out, heads[n][:, c, cols], tails[n][:, c, cols], u_head[:, c, :],
                                                 u_tail[:, c, :], c == 0, c == NC - 1)
                            else:
                                cols = slice(P * (k - 8), P * (k - 7))
                                last = products3(nc, out, u_head[:, c, cols], u_tail[:, c, cols], heads[2][:, c, :],
                                                 tails[2][:, c, :], c == 0, c == NC - 1)
                        last.then_inc(out_ready, 1)

                rolled(pe, 1, 2, NT, step)




def stage5(nc, d, persist):
    G = HEADS // 4
    ITS = BATCH * G
    NB = SEQ // P
    QK = 3 * HD
    HALF = 512
    PARTS = [(0, k) for k in range(NB)] + [(1, k) for k in range(NB // 2)]
    NSTEP = len(PARTS)
    NADD = [NB - 1, NSTEP - 2]
    ENDS = [NB, NSTEP]
    LATE = [(hh, i, HALF, P * (i + 1) - HALF, NB // 2 + i) for hh in range(4) for i in range(NB // 2, NB)]
    SCORES = LATE + [(hh, i, 0, min(P * (i + 1), HALF), i) for hh in range(4) for i in range(NB)]
    NSCORE = len(SCORES)
    COUNTS = [4, 4, 4, 4, 6, 6, 5, 5, 5, 5, 0, 0]
    MAXIMA_STEP = 10
    assert sum(COUNTS) == NSCORE and sum(COUNTS[:4]) == len(LATE)

    def base(part):
        return HALF * (1 - part)

    def lo(part, blk):
        return max(0, P * blk - base(part))

    def diagonal(part, blk):
        return P * blk >= base(part)

    def ring_uses(k, v, first, last):
        uses = []
        if not last:
            uses += [("score", s) for s in range(sum(COUNTS[:k]), sum(COUNTS[:k + 1]))]
            if k == MAXIMA_STEP:
                uses.append(("maxima", 0))
        if k == MAXIMA_STEP and not first and v % G == 0:
            uses += [("rows", i) for i in range(NB)]
        return uses

    USES = NSCORE + 1
    PERIOD = G * USES + NB

    def before(j, v):
        if v == 0:
            return USES
        return 2 * USES + PERIOD * j + USES * (v - 1) + NB * ((v - 1) // G)

    def parity(v):
        return before(0, v) % 2

    def kinds(j, v):
        return isinstance(j, int) and v == 0, isinstance(j, int) and v == ITS - 1

    with ExitStack() as ctx:
        sb = lambda name, shape, dt=F32: ctx.enter_context(nc.sbuf_tensor("s5_" + name, shape, dt))
        ps = lambda name, shape, dt=F32: ctx.enter_context(nc.psum_tensor("s5_" + name, shape, dt))
        sem = lambda name: ctx.enter_context(nc.semaphore("s5_" + name))
        q_st = sb("q_stack", [P, 2, 4, SEQ], F32R)
        k_st = sb("k_stack", [P, 2, 4, SEQ], F32R)
        v_in = sb("v_rows", [P, 2, NB, P])
        prob = sb("prob", [P, 2, 4, HALF])
        row_sum = sb("row_sum", [P, 2, 4, HALF])
        y_head = sb("y_head", [P, G, SEQ], F32R)
        y_tail = sb("y_tail", [P, G, SEQ], F32R)
        x_rows = sb("x_rows", [P, NB, DM])
        o_head = sb("o_head", [P, NC, DM], F32R)
        o_tail = sb("o_tail", [P, NC, DM], F32R)
        ones = sb("ones", [P, HD])
        ident = sb("ident", [P, P], BF16)
        mask_q = sb("mask_q", [P, P], BF16)
        mask_k = sb("mask_k", [P, P], BF16)
        mx = sb("mx", [P, 4, 3 * NB // 2])
        nm = sb("nm", [P, 4, 4, NB], F32R)
        nm_t = sb("nm_t", [2 * 4 * NB, P], F32R)
        rec = sb("rec", [P, HALF])
        yn = sb("yn", [P, 2, HALF])
        s_ps = ps("s_ps", [P, 2, HALF])
        e_ps = ps("e_ps", [P, 4, HALF])
        y_ps = ps("y_ps", [P, 2, HALF])

        qk_loaded = [[sem(f"qk_loaded{part}{u}") for u in range(2)] for part in range(2)]
        v_loaded = [sem("v_loaded0"), sem("v_loaded1")]
        maxima_loaded, w_loaded, w_head_done, w_tail_done, made, ones_rows = (
            sem("maxima_loaded"), sem("w_loaded"), sem("w_head"), sem("w_tail"), sem("made"), sem("ones_rows"))
        x_loaded, stored = sem("x_loaded"), sem("stored")
        sp_passed = sem("sp_passed")
        ring_ready, ring_free = sem("ring_ready"), sem("ring_free")
        max_done, negated = sem("max"), sem("negated")
        e_ready, exp_done = sem("e_ready"), sem("exp")
        av_done, added = sem("av"), sem("added")
        sum_ready, rec_done = sem("sum_ready"), sem("rec")
        y_out, yn_done, yh_done, yt_done = sem("y_out"), sem("yn"), sem("y_head"), sem("y_tail")

        with nc.Block() as block:
            @block.sync
            def _(sp):
                def load(j, v, part):
                    b, g, u = j + v // G, v % G, v % 2
                    tok, blocks = slice(base(part), base(part) + HALF), slice(base(part) // P, base(part) // P + NB // 2)
                    for name, stack, order in (("q_s", q_st, (0, 1, 0)), ("k_s", k_st, (0, 0, 1))):
                        src = d[name].rearrange("b g a (h e) t -> b g a e h t", h=4)
                        for n, a in enumerate(order):
                            sp.dma_start(stack[HD * n:HD * (n + 1), u, :, tok].bitcast(F32),
                                         src[b, g, a, :, :, tok]).then_inc(qk_loaded[part][u], 16)
                    src = d["v_s"].rearrange("(b k p) (g c) -> b g p k c", b=BATCH, p=P, g=G)
                    sp.dma_start(v_in[:, u, blocks], src[b, g, :, blocks]).then_inc(v_loaded[u], 16)

                def maxima(j, v, rows_too=False):
                    sp.wait_ge(ring_free, before(j, v) + 2 - (NB if rows_too else 0))
                    for a in range(2):
                        sp.dma_start(q_st[QK + a:QK + a + 1, v % 2].bitcast(F32).rearrange("a h (k t) -> a (h k) t", k=NB),
                                     nm_t[4 * NB * a:4 * NB * (a + 1), :].bitcast(F32)).then_inc(maxima_loaded, 16)

                rows_of = lambda name: d[name].rearrange("(b k p) c -> b p k c", b=BATCH, p=P)
                sp.dma_start(x_rows[:, 0:NC, :], d["wp"].rearrange("(c p) m -> p c m", p=P)).then_inc(w_loaded, 16)
                load(0, 0, 0)
                load(0, 0, 1)
                load(0, 1, 0)
                maxima(0, 0)

                def store(b, uses):
                    sp.wait_ge(ring_free, uses + 2)
                    sp.sem_inc(sp_passed, 1)
                    sp.dma_start(rows_of("out")[b], x_rows[:, :, :]).then_inc(stored, 16)

                def step(j, v):
                    first, last = kinds(j, v)
                    it, b = G * j + v, j + v // G
                    rows = v % G == 0 and not first
                    if not last:
                        if not first:
                            sp.wait_ge(av_done, NSTEP * it)
                            sp.sem_inc(sp_passed, 1)
                        load(j, v + 1, 1)
                        if not (isinstance(j, int) and v == ITS - 2):
                            sp.wait_ge(av_done, NSTEP * it + ENDS[0])
                            sp.sem_inc(sp_passed, 1)
                            load(j, v + 2, 0)
                        maxima(j, v + 1, rows)
                    if rows:
                        store(b - 1, before(j, v) + USES + NB)
                        sp.wait_ge(stored, 16 * b)
                    elif first:
                        sp.wait_ge(w_tail_done, 1)
                    if v % G == 0:
                        sp.dma_start(x_rows[:, :, :], rows_of("x1_s")[b]).then_inc(x_loaded, 16)

                rolled(sp, 1, G, ITS, step, tail=1)
                store(BATCH - 1, before(0, ITS - 1) + NB)
                sp.wait_ge(stored, 16 * BATCH)

            @block.gpsimd
            def _(pool):
                nc.gpsimd.memset(ident[:, :], 0.0).then_inc(made, 1)
                nc.gpsimd.memset(mask_q[:, :], 0.0).then_inc(made, 1)
                nc.gpsimd.memset(mask_k[:, :], 0.0).then_inc(made, 1)
                nc.gpsimd.memset(ones[:, :], 1.0).then_inc(made, 1)
                pool.wait_ge(made, 4)
                nc.gpsimd.affine_select(out=ident[:, :], in_=ident[:, :], compare_op=ALU.not_equal, fill=1.0, base=0,
                                        pattern=[[-1, P]], channel_multiplier=1).then_inc(made, 1)
                nc.gpsimd.affine_select(out=mask_q[:, :], in_=mask_q[:, :], compare_op=ALU.is_ge, fill=-1e30, base=0,
                                        pattern=[[-1, P]], channel_multiplier=1).then_inc(made, 1)
                nc.gpsimd.affine_select(out=mask_k[:, :], in_=mask_k[:, :], compare_op=ALU.is_ge, fill=-1e30, base=0,
                                        pattern=[[1, P]], channel_multiplier=-1).then_inc(made, 1)

                def step(j, v):
                    it = G * j + v
                    n = 0
                    for k, (part, blk) in enumerate(PARTS):
                        if blk == 0:
                            continue
                        pool.wait_ge(exp_done, 4 * (NSTEP * it + k + 1))
                        if blk == 1:
                            pool.wait_ge(av_done, NSTEP * it + k)
                        else:
                            pool.wait_ge(added, NADD[1] * it + n)
                        acc = row_sum[:, part, :, lo(part, blk):HALF]
                        nc.gpsimd.tensor_tensor(acc, acc, prob[:, k % 2, :, 0:HALF - lo(part, blk)], ALU.add).then_inc(added, 1)
                        n += 1

                rolled(pool, 1, G, ITS, step, tail=1)

            @block.scalar
            def _(act):
                act.wait_ge(w_loaded, 16)
                nc.scalar.activation(o_head[:, :, :], x_rows[:, 0:NC, :], ACT.Copy).then_inc(w_head_done, 1)

                def bring_out(j, v, part):
                    it = G * j + v
                    first, _ = kinds(j, v)
                    act.wait_ge(av_done, NSTEP * it + ENDS[part])
                    if not first:
                        act.wait_ge(yt_done, 2 * it - 1 + part)
                    nc.scalar.activation(yn[:, part], y_ps[:, part], ACT.Copy).then_inc(y_out, 1)

                def head(j, v, part):
                    act.wait_ge(yn_done, 2 * (G * j + v) + part + 1)
                    nc.scalar.activation(y_head[:, v % G, base(part):base(part) + HALF], yn[:, part], ACT.Copy).then_inc(yh_done, 1)

                def step(j, v):
                    it = G * j + v
                    first, _ = kinds(j, v)
                    for k, (part, blk) in enumerate(PARTS):
                        c = lo(part, blk)
                        if blk == 0:
                            if not first:
                                act.wait_ge(sum_ready, 2 * it - 1 + part)
                        elif not (first and k < 2):
                            act.wait_ge(av_done, NSTEP * it + k - 1)
                            prev = [m for m in range(k - 1) if m % 2 == k % 2 and PARTS[m][1]]
                            adds = sum(1 for m in range(prev[-1] + 1) if PARTS[m][1]) if prev else 0
                            if not (first and adds == 0):
                                act.wait_ge(added, NADD[1] * it + adds)
                        for hh in range(4):
                            act.wait_ge(e_ready, 4 * (NSTEP * it + k) + hh + 1)
                            dst = row_sum[:, part, hh, :] if blk == 0 else prob[:, k % 2, hh, 0:HALF - c]
                            nc.scalar.activation(dst, e_ps[:, hh, c:HALF], ACT.Exp).then_inc(exp_done, 1)
                        if k == 1 and not first:
                            bring_out(j, v - 1, 1)
                            head(j, v - 1, 0)
                        if k == 8:
                            bring_out(j, v, 0)
                        if k == 9 and not first:
                            head(j, v - 1, 1)

                rolled(act, 1, G, ITS, step, tail=1)
                bring_out(0, ITS - 1, 1)
                head(0, ITS - 1, 0)
                head(0, ITS - 1, 1)

            @block.vector
            def _(dve):
                dve.sem_inc(ring_free, 2)
                nc.vector.memset(nm[:, 2:4, :, :].bitcast(F32), 0.0).then_inc(ones_rows, 1)
                nc.vector.memset(k_st[QK:QK + 2, :, :, :].bitcast(F32), 1.0).then_inc(ones_rows, 1)
                dve.wait_ge(w_head_done, 1)
                nc.vector.tensor_tensor(o_tail[:, :, :], x_rows[:, 0:NC, :], o_head[:, :, :].bitcast(F32),
                                        ALU.subtract).then_inc(w_tail_done, 1)

                def maximum(s, n, bank):
                    hh, blk, key, keys, slot = SCORES[s]
                    dve.wait_ge(ring_ready, n + 1)
                    nc.vector.reduce_max(mx[:, hh, slot:slot + 1], s_ps[:, bank, 0:keys], axis=AX_X).then_inc(ring_free, 1)

                def negate(it, n):
                    dve.wait_ge(ring_free, n + 2)
                    late = mx[:, :, NB // 2:NB]
                    nc.vector.tensor_tensor(late, late, mx[:, :, NB:3 * NB // 2], ALU.max).then_inc(max_done, 1)
                    dve.wait_ge(max_done, it + 1)
                    nc.vector.tensor_scalar(nm[:, 0], mx[:, :, 0:NB], -1.0, None, ALU.mult).then_inc(negated, 1)
                    dve.wait_ge(negated, 2 * it + 1)
                    nc.vector.scalar_tensor_tensor(nm[:, 1], mx[:, :, 0:NB], -1.0, nm[:, 0].bitcast(F32),
                                                   ALU.mult, ALU.subtract).then_inc(negated, 1)

                def copy_maxima(it, n, bank):
                    dve.wait_ge(ring_ready, n + 1)
                    if not (isinstance(it, int) and it == 0):
                        dve.wait_ge(maxima_loaded, 32 * it)
                    nc.vector.tensor_copy(nm_t[:, :], s_ps[0:2 * 4 * NB, bank, 0:P]).then_inc(ring_free, 1)

                def reciprocals(j, v, part, cols):
                    it = G * j + v
                    first, _ = kinds(j, v)
                    if cols.start == 0:
                        dve.wait_ge(sum_ready, 2 * it + part + 1)
                        if not (first and part == 0):
                            dve.wait_ge(yn_done, 2 * it + part)
                    last = nc.vector.reciprocal(rec[:, cols], y_ps[:, part, cols])
                    if cols.stop == HALF:
                        last.then_inc(rec_done, 1)

                def normalise(j, v, part):
                    it = G * j + v
                    dve.wait_ge(rec_done, 2 * it + part + 1)
                    dve.wait_ge(y_out, 2 * it + part + 1)
                    nc.vector.tensor_tensor(yn[:, part], yn[:, part], rec[:, :], ALU.mult).then_inc(yn_done, 1)

                def tail(j, v, part):
                    dve.wait_ge(yh_done, 2 * (G * j + v) + part + 1)
                    cols = slice(base(part), base(part) + HALF)
                    nc.vector.tensor_tensor(y_tail[:, v % G, cols], yn[:, part], y_head[:, v % G, cols].bitcast(F32),
                                            ALU.subtract).then_inc(yt_done, 1)

                def add_rows(b, i, n, bank):
                    if i == 0:
                        dve.wait_ge(x_loaded, 16 * (b + 1))
                    dve.wait_ge(ring_ready, n + 1)
                    nc.vector.tensor_tensor(x_rows[:, i, :], x_rows[:, i, :], s_ps[:, bank, :], ALU.add).then_inc(ring_free, 1)

                for s in range(NSCORE):
                    maximum(s, s, s % 2)
                negate(0, NSCORE)
                copy_maxima(0, NSCORE, NSCORE % 2)

                def step(j, v):
                    it, n, bank = G * j + v, before(j, v), parity(v)
                    first, last = kinds(j, v)
                    for k in range(NSTEP):
                        if k == 2 and not first:
                            tail(j, v - 1, 0)
                        if 4 <= k < 8 and not first:
                            reciprocals(j, v - 1, 1, slice(P * (k - 4), P * (k - 3)))
                        if k == 7 and not first:
                            normalise(j, v - 1, 1)
                        if k == MAXIMA_STEP and not first:
                            tail(j, v - 1, 1)
                        if k == MAXIMA_STEP and not last:
                            negate(it + 1, n)
                        for kind, arg in ring_uses(k, v, first, last):
                            if kind == "rows":
                                add_rows(j + v // G - 1, arg, n, bank)
                            elif kind == "score":
                                if arg == 0:
                                    dve.wait_ge(negated, 2 * it + 2)
                                maximum(arg, n, bank)
                            else:
                                copy_maxima(it + 1, n, bank)
                            n, bank = n + 1, 1 - bank
                    reciprocals(j, v, 0, slice(0, HALF))
                    normalise(j, v, 0)

                rolled(dve, 1, G, ITS, step, tail=1)
                reciprocals(0, ITS - 1, 1, slice(0, HALF))
                normalise(0, ITS - 1, 1)
                tail(0, ITS - 1, 0)
                tail(0, ITS - 1, 1)
                n = before(0, ITS - 1)
                for i in range(NB):
                    add_rows(BATCH - 1, i, n + i, (n + i) % 2)

            @block.tensor
            def _(pe):
                def score(j, v, s, n, bank):
                    hh, blk, key, keys, _ = SCORES[s]
                    u, queries, on_diagonal = v % 2, slice(P * blk, P * (blk + 1)), key + keys == P * (blk + 1)
                    if s in (0, len(LATE)):
                        pe.wait_ge(qk_loaded[1 if s else 0][u], 96 * (2 * j + v // 2 + 1))
                    pe.wait_ge(ring_free, n + 1)
                    last = nc.tensor.matmul(s_ps[:, bank, 0:keys], q_st[0:QK, u, hh, queries], k_st[0:QK, u, hh, key:key + keys],
                                            start=True, stop=not on_diagonal)
                    if on_diagonal:
                        last = nc.tensor.matmul(s_ps[:, bank, keys - P:keys], ident[:, :], mask_q[:, :], start=False, stop=True)
                    last.then_inc(ring_ready, 1)

                def turn_maxima(it, n, bank):
                    pe.wait_ge(negated, 2 * it + 2)
                    pe.wait_ge(ring_free, n + 1)
                    nc.tensor.transpose(s_ps[:, bank, 0:P], nm[:, :, :, :].bitcast(F32).rearrange("p a h k -> p (a h k)"),
                                        persist["ident"][:, :]).then_inc(ring_ready, 1)

                def exponents(j, v, k, hh):
                    it, u, (part, blk) = G * j + v, v % 2, PARTS[k]
                    first, _ = kinds(j, v)
                    c = lo(part, blk)
                    if k == 0 and hh == 0:
                        pe.wait_ge(maxima_loaded, 32 * (it + 1))
                    if not (first and k == 0):
                        pe.wait_ge(exp_done, 4 * (NSTEP * it + k) + hh - 3)
                    last = nc.tensor.matmul(e_ps[:, hh, c:HALF], k_st[0:QK + 2, u, hh, P * blk:P * (blk + 1)],
                                            q_st[0:QK + 2, u, hh, base(part) + c:base(part) + HALF],
                                            start=True, stop=not diagonal(part, blk))
                    if diagonal(part, blk):
                        last = nc.tensor.matmul(e_ps[:, hh, c:c + P], ident[:, :], mask_k[:, :], start=False, stop=True)
                    last.then_inc(e_ready, 1)

                def weigh(j, v, k):
                    it, u, (part, blk) = G * j + v, v % 2, PARTS[k]
                    first, _ = kinds(j, v)
                    c = lo(part, blk)
                    if k == 0:
                        pe.wait_ge(v_loaded[u], 32 * (2 * j + v // 2 + 1))
                    if blk == 0 and not first:
                        pe.wait_ge(rec_done, 2 * it - 1 + part)
                    pe.wait_ge(exp_done, 4 * (NSTEP * it + k + 1))
                    for hh in range(4):
                        p = row_sum[:, part, hh, :] if blk == 0 else prob[:, k % 2, hh, 0:HALF - c]
                        last = nc.tensor.matmul(y_ps[HD * hh:HD * (hh + 1), part, c:HALF], v_in[:, u, blk, HD * hh:HD * (hh + 1)],
                                                p, start=blk == 0, stop=k + 1 == ENDS[part])
                    last.then_inc(av_done, 1)

                def total(j, v, part):
                    it = G * j + v
                    pe.wait_ge(added, NADD[1] * it + NADD[part])
                    pe.wait_ge(y_out, 2 * it + part + 1)
                    for hh in range(4):
                        last = nc.tensor.matmul(y_ps[HD * hh:HD * (hh + 1), part, :], ones[:, :], row_sum[:, part, hh, :],
                                                start=True, stop=True)
                    last.then_inc(sum_ready, 1)

                def out_rows(its, i, n, bank):
                    if i == 0:
                        pe.wait_ge(yt_done, 2 * its)
                        pe.wait_ge(w_tail_done, 1)
                    pe.wait_ge(ring_free, n + 1)
                    tokens = slice(P * i, P * (i + 1))
                    for g in range(G):
                        last = products3(nc, s_ps[:, bank, :], y_head[:, g, tokens], y_tail[:, g, tokens], o_head[:, g, :],
                                         o_tail[:, g, :], g == 0, g == G - 1)
                    last.then_inc(ring_ready, 1)

                pe.wait_ge(made, 7)
                pe.wait_ge(ones_rows, 2)
                for s in range(NSCORE):
                    score(0, 0, s, s, s % 2)
                turn_maxima(0, NSCORE, NSCORE % 2)

                def step(j, v):
                    it, n, bank = G * j + v, before(j, v), parity(v)
                    first, last = kinds(j, v)
                    for k in range(NSTEP):
                        uses = ring_uses(k, v, first, last)
                        scores = [arg for kind, arg in uses if kind == "score"]
                        for hh in range(4):
                            exponents(j, v, k, hh)
                            for s in scores[len(scores) * hh // 4:len(scores) * (hh + 1) // 4]:
                                score(j, v + 1, s, n, bank)
                                n, bank = n + 1, 1 - bank
                        if k:
                            weigh(j, v, k - 1)
                        elif not first:
                            weigh(j, v - 1, NSTEP - 1)
                        for kind, arg in uses:
                            if kind == "rows":
                                out_rows(it, arg, n, bank)
                            elif kind == "maxima":
                                turn_maxima(it + 1, n, bank)
                            if kind != "score":
                                n, bank = n + 1, 1 - bank
                        if k == 3 and not first:
                            total(j, v - 1, 1)
                        if k == NSTEP - 1:
                            total(j, v, 0)

                rolled(pe, 1, G, ITS, step, tail=1)
                weigh(0, ITS - 1, NSTEP - 1)
                total(0, ITS - 1, 1)
                n = before(0, ITS - 1)
                for i in range(NB):
                    out_rows(ITS, i, n + i, (n + i) % 2)


def build(nc, d):
    scratch = {"z_s": (BATCH, NC, P, SEQ), "x_s": (BATCH, P, SEQ), "B_s": (BATCH, P, SEQ), "C_s": (BATCH, NC, P, SEQ),
               "dt_s": (BATCH, NC, 2, P, SEQ), "dtx_s": (BATCH, NC, 2, P, SEQ), "y_s": (BATCH, NC, P, SEQ),
               "x1_s": (BATCH * SEQ, DM), "q_s": (BATCH, NC, 2, P, SEQ), "k_s": (BATCH, NC, 2, P, SEQ), "v_s": (BATCH * SEQ, DM)}
    for name, shape in scratch.items():
        d[name] = nc.dram_tensor(name, shape, F32).ap()
    with ExitStack() as ctx:
        ident = ctx.enter_context(nc.sbuf_tensor("ident", [P, P], F32))
        mean_all = ctx.enter_context(nc.sbuf_tensor("mean_all", [P, NT * NS], F32))
        rstd_all = ctx.enter_context(nc.sbuf_tensor("rstd_all", [P, NT * NS], F32))
        ident_ready = ctx.enter_context(nc.semaphore("ident_ready"))
        persist = dict(ident=ident, mean_all=mean_all, rstd_all=rstd_all, ident_ready=ident_ready)
        with nc.Block() as block:
            @block.gpsimd
            def _(pool):
                nc.gpsimd.memset(ident[:, :], 0.0).then_inc(ident_ready, 1)
                pool.wait_ge(ident_ready, 1)
                nc.gpsimd.affine_select(out=ident[:, :], in_=ident[:, :], compare_op=ALU.not_equal, fill=1.0, base=0,
                                        pattern=[[-1, P]], channel_multiplier=1).then_inc(ident_ready, 1)
        for stage in STAGES:
            stage(nc, d, persist)


STAGES = [stage1, stage2, stage3, stage4, stage5]


def kernel(L0_attn_hidden_states, L0_attn_in_proj_w, L0_attn_dt_proj_w, L0_attn_dt_proj_b, L0_attn_A_log, L0_attn_D_param,
           L0_attn_out_proj_w, L0_attn_gate_w, L0_attn_up_w, L0_attn_down_w, L0_attn_norm1_w, L0_attn_norm2_w, L0_ffn_Wa,
           L0_ffn_Wp, L0_ffn_w_std, L0_ffn_w_rec):
    import concourse.bacc as bacc
    import numpy as np
    from concourse.bass_utils import run_bass_kernel_spmd

    def transposed(w):
        return np.ascontiguousarray(np.asarray(w).T)

    def blocks(w):
        return transposed(np.asarray(w).reshape(NC, P))

    wa, std = np.asarray(L0_ffn_Wa), HD - 8
    ends = np.cumsum([HEADS * std, HEADS * std, DM, HEADS * 8])
    q_std, k_std, v_cols, q_low, k_low = np.split(wa, ends, axis=1)

    def by_head(a, b):
        parts = [a.reshape(DM, HEADS, std), b.reshape(DM, HEADS, 8)]
        return np.ascontiguousarray(np.concatenate(parts, axis=2).reshape(DM, DM))

    arrays = {
        "x": np.ascontiguousarray(np.asarray(L0_attn_hidden_states).reshape(BATCH * SEQ, DM)),
        "in_w": transposed(L0_attn_in_proj_w), "dt_w": transposed(L0_attn_dt_proj_w),
        "norm1": blocks(L0_attn_norm1_w), "norm2": blocks(L0_attn_norm2_w),
        "dt_b": blocks(L0_attn_dt_proj_b), "D": blocks(L0_attn_D_param),
        "A_log": np.ascontiguousarray(np.asarray(L0_attn_A_log).reshape(NC, REP, 8, P).transpose(3, 0, 2, 1).reshape(P, P)),
        "out_w": transposed(L0_attn_out_proj_w), "gate_w": transposed(L0_attn_gate_w),
        "up_w": transposed(L0_attn_up_w), "down_w": transposed(L0_attn_down_w),
        "wq": by_head(q_std, q_low), "wk": by_head(k_std, k_low), "wv": np.ascontiguousarray(v_cols),
        "wp": np.ascontiguousarray(np.asarray(L0_ffn_Wp)),
        "w_std": np.ascontiguousarray(np.asarray(L0_ffn_w_std)), "w_rec": np.ascontiguousarray(np.asarray(L0_ffn_w_rec)),
    }
    nc = bacc.Bacc("TRN2", target_bir_lowering=False, num_devices=1)
    d = {name: nc.dram_tensor(name, a.shape, F32, kind="ExternalInput").ap() for name, a in arrays.items()}
    d["out"] = nc.dram_tensor("out", (BATCH * SEQ, DM), F32, kind="ExternalOutput").ap()
    build(nc, d)
    nc.compile()
    result = run_bass_kernel_spmd(nc, [arrays], core_ids=[0])
    return np.asarray(result.results[0]["out"]).reshape(BATCH, SEQ, DM)
```

```python
from contextlib import ExitStack

import concourse.bass as bass
from concourse import mybir

F32 = mybir.dt.float32
F32R = mybir.dt.float32r
BF16 = mybir.dt.bfloat16
ALU = mybir.AluOpType
ACT = mybir.ActivationFunctionType
AX_X = mybir.AxisListType.X

P = 128
EPS = 1e-5
BATCH, SEQ, DM = 4, 1024, 512
NC = DM // P
STATE = 32
REP = 4
FF = 1408
NF = FF // P
TT = 512
NT = BATCH * SEQ // TT
NS = TT // P
UP = SEQ // TT
HEADS, HD = 16, 32


def rolled(eng, first, period, total, emit, tail=0):
    n = (total - first - tail) // period
    for v in range(first):
        emit(0, v)
    with eng.Fori(0, n) as j:
        for v in range(first, first + period):
            emit(j, v)
    for v in range(first + n * period, total):
        emit(0, v)


def products3(nc, out, w_head, w_tail, x_head, x_tail, first, last):
    nc.tensor.matmul(out, w_head, x_head, start=first, stop=False)
    nc.tensor.matmul(out, w_head, x_tail, start=False, stop=False)
    return nc.tensor.matmul(out, w_tail, x_head, start=False, stop=last)


def stage1(nc, d, persist):
    ident, mean_all, rstd_all = persist["ident"], persist["mean_all"], persist["rstd_all"]
    x_v = d["x"].rearrange("(b u s p) c -> b u p s c", b=BATCH, u=UP, p=P)
    ORDER = [10, 4, 5, 6, 7, 8, 9, None, None, None, None, 0, 1, 2, 3]
    NOUT = len(ORDER)
    USES = [sum(1 for k in range(NOUT) if k % 4 == b) for b in range(4)]

    with ExitStack() as ctx:
        sb = lambda name, shape, dt=F32: ctx.enter_context(nc.sbuf_tensor("s1_" + name, shape, dt))
        ps = lambda name, shape, dt=F32: ctx.enter_context(nc.psum_tensor("s1_" + name, shape, dt))
        sem = lambda name: ctx.enter_context(nc.semaphore("s1_" + name))
        w_head = sb("in_w_head", [P, NC, FF], F32R)
        w_tail = sb("in_w_tail", [P, NC, FF], F32R)
        dtw_head = sb("dt_w_head", [P, DM], F32R)
        dtw_tail = sb("dt_w_tail", [P, DM], F32R)
        norm1 = sb("norm1", [P, NC])
        dt_bias = sb("dt_bias", [P, NC])
        xb = sb("x_rows", [P, 2, NS, DM])
        uh = sb("u_rows", [P, NS, DM])
        u_head = sb("u_head", [P, NC, TT], F32R)
        u_tail = sb("u_tail", [P, NC, TT], F32R)
        stats = sb("stats", [P, NS, 6])
        mom = sb("moments", [P, NS, 2])
        var_eps = sb("var_eps", [P, NS])
        std1 = sb("std1", [P, NS])
        rstd1 = sb("rstd1", [P, NS])
        ms2 = sb("ms2", [P, NS])
        std2 = sb("std2", [P, NS])
        rstd2 = sb("rstd2", [P, NS])
        scale12 = sb("scale12", [P, NS])
        dtr_head = sb("dt_raw_head", [P, TT], F32R)
        dtr_tail = sb("dt_raw_tail", [P, TT], F32R)
        x_ch = sb("x_channels", [P, TT])
        x_rep = sb("x_repeated", [P, NC, TT])
        bcz = sb("bcz", [P, 9, TT])
        mag = sb("magnitude", [P, NC, TT])
        pos = sb("positive", [P, NC, TT])
        one_e = sb("one_plus_e", [P, NC, TT])
        log_w = sb("log_w", [P, NC, TT])
        inv_w = sb("inv_w", [P, NC, TT])
        parts = sb("parts", [P, 4, NC * TT])
        w_full = parts[:, :, :].rearrange("p a n -> p (a n)")[:, 0:NC * FF].rearrange("p (c m) -> p c m", c=NC)
        dtw_full = parts[:, 3, NC * TT - DM:NC * TT]
        u_ps = ps("u_ps", [P, NC, TT])
        o_ps = ps("o_ps", [P, 4, TT])

        w_loaded = [sem(f"w_loaded{n}") for n in range(NC + 1)]
        const_loaded, w_head_done, w_ready = sem("const_loaded"), sem("w_head"), sem("w_ready")
        x_loaded = [sem("x_loaded0"), sem("x_loaded1")]
        stats_done, mom_done, var_done, std1_done, rstd1_done = (
            sem("stats"), sem("moments"), sem("var_eps"), sem("std1"), sem("rstd1"))
        sq_done, ms_done, std2_done, rstd2_done, scale_done = (
            sem("sq"), sem("ms"), sem("std2"), sem("rstd2"), sem("scale"))
        normed = sem("normed")
        transposed = sem("transposed")
        head_done, tail_done = sem("u_head"), sem("u_tail")
        out_ready = sem("out_ready")
        o_free = [sem(f"o_free{b}") for b in range(4)]
        dtr_head_done = sem("dt_raw_head")
        x_repeated = sem("x_repeated")
        stored = [sem("stored_bc"), sem("stored_z"), sem("stored_parts"), sem("stored_x")]
        e_done, ln_masked, one_e_done, ln_done, inv_done = (
            sem("e"), sem("ln_masked"), sem("one_e"), sem("ln"), sem("inv"))
        err_done, corr_done, log1p_done, dt_done, dtx_done = (
            sem("err"), sem("corr"), sem("log1p"), sem("dt"), sem("dtx"))
        ph_done, parts_done = sem("part_heads"), sem("parts")

        weights = [(w_full[:, c, :], w_head[:, c, :], w_tail[:, c, :], norm1[:, c:c + 1]) for c in range(NC)]
        weights.append((dtw_full, dtw_head[:, :], dtw_tail[:, :], 1.0))
        by_dve, by_act = (2, 4, 6, 11, 13), (3, 5, 12, 14)

        def freed(k, t):
            return USES[k % 4] * t + k // 4 + 2

        def softplus(eng, ops, t):
            eng.wait_ge(err_done, t + 1)
            eng.wait_ge(inv_done, t + 1)
            ops.tensor_tensor(inv_w[:, :, :], inv_w[:, :, :], one_e[:, :, :], ALU.mult).then_inc(corr_done, 1)
            eng.wait_ge(corr_done, t + 1)
            ops.tensor_tensor(log_w[:, :, :], log_w[:, :, :], inv_w[:, :, :], ALU.subtract).then_inc(log1p_done, 1)
            eng.wait_ge(log1p_done, t + 1)
            eng.wait_ge(o_free[2], freed(10, t))
            ops.tensor_tensor(log_w[:, :, :], log_w[:, :, :], pos[:, :, :], ALU.add).then_inc(dt_done, 1)
            eng.wait_ge(dt_done, t + 1)
            eng.wait_ge(x_repeated, 256 * (t + 1))
            ops.tensor_tensor(inv_w[:, :, :], log_w[:, :, :], x_rep[:, :, :], ALU.mult).then_inc(dtx_done, 1)

        with nc.Block() as block:
            @block.sync
            def _(sp):
                sp.dma_start(xb[:, 0], x_v[0, 0]).then_inc(x_loaded[0], 16)
                sp.dma_start(norm1[:, :], d["norm1"]).then_inc(const_loaded, 16)
                sp.dma_start(dt_bias[:, :], d["dt_b"]).then_inc(const_loaded, 16)
                for c in range(NC):
                    sp.dma_start(w_full[:, c, :], d["in_w"][P * c:P * (c + 1), :]).then_inc(w_loaded[c], 16)
                sp.dma_start(dtw_full, d["dt_w"]).then_inc(w_loaded[NC], 16)
                sp.dma_start(xb[:, 1], x_v[0, 1]).then_inc(x_loaded[1], 16)

                def step(j, v):
                    t, b, u = 2 * j + v, j + v // 2, v % 2
                    if not (isinstance(t, int) and t >= NT - 2):
                        sp.wait_ge(normed, t + 1)
                        sp.dma_start(xb[:, u], x_v[b + 1, u]).then_inc(x_loaded[u], 16)
                    tok = slice(u * TT, (u + 1) * TT)
                    sp.wait_ge(o_free[1], freed(1, t))
                    sp.wait_ge(dtx_done, t + 1)
                    for g in range(NC):
                        for r in range(REP):
                            sp.dma_start(x_rep[STATE * r:STATE * (r + 1), g, :],
                                         x_ch[STATE * g:STATE * (g + 1), :]).then_inc(x_repeated, 16)
                    sp.dma_start(d["x_s"][b, :, tok], x_ch[:, :]).then_inc(stored[3], 16)
                    for k in range(3, 7):
                        sp.wait_ge(o_free[k % 4], freed(k, t))
                        if k % 4 == 3:
                            sp.sem_inc(persist["passed"], 1)
                    sp.dma_start(d["B_s"][b, :, tok], bcz[:, 0, :]).then_inc(stored[0], 16)
                    sp.dma_start(d["C_s"][b, :, :, tok].rearrange("k p t -> p k t"),
                                 bcz[:, 1:5, :]).then_inc(stored[0], 16)
                    for k in range(11, 15):
                        sp.wait_ge(o_free[k % 4], freed(k, t))
                        if k % 4 == 3:
                            sp.sem_inc(persist["passed"], 1)
                    sp.dma_start(d["z_s"][b, :, :, tok].rearrange("k p t -> p k t"),
                                 bcz[:, 5:9, :]).then_inc(stored[1], 16)
                    sp.wait_ge(parts_done, t + 1)
                    for n, name in enumerate(("dt_s", "dtx_s")):
                        for part in range(2):
                            for half in range(2):
                                rows = slice(64 * part, 64 * part + 64)
                                src = parts[64 * half:64 * half + 64, 2 * n + part, :]
                                sp.dma_start(d[name][b, :, half, rows, tok].rearrange("k c t -> c k t"),
                                             src.rearrange("c (k t) -> c k t", k=NC)).then_inc(stored[2], 16)

                rolled(sp, 0, 2, NT, step, tail=2)
                sp.wait_ge(stored[3], 16 * NT)
                sp.wait_ge(stored[0], 32 * NT)
                sp.wait_ge(stored[1], 16 * NT)
                sp.wait_ge(stored[2], 128 * NT)

            @block.vector
            def _(dve):
                dve.sem_inc(tail_done, 1)

                def weight_tails():
                    for n, (full, head, tail, scale) in enumerate(weights):
                        dve.wait_ge(w_head_done, n + 1)
                        nc.vector.scalar_tensor_tensor(tail, full, scale, head.bitcast(F32), ALU.mult,
                                                       ALU.subtract).then_inc(w_ready, 1)

                def norm(j, v):
                    t, u = 2 * j + v, v % 2
                    dve.wait_ge(x_loaded[u], 16 * (j + v // 2 + 1))
                    for s in range(NS):
                        last = nc.vector.bn_stats(stats[:, s, :], xb[:, u, s, :])
                    last.then_inc(stats_done, 1)
                    dve.wait_ge(stats_done, t + 1)
                    dve.sem_inc(persist["passed"], 1)
                    for s in range(NS):
                        last = nc.vector.bn_aggr(mom[:, s, :], stats[:, s, :])
                    last.then_inc(mom_done, 1)
                    dve.wait_ge(mom_done, t + 1)
                    nc.vector.tensor_copy(mean_all[:, bass.ds(NS * t, NS)], mom[:, :, 0])
                    nc.vector.tensor_scalar(var_eps[:, :], mom[:, :, 1], EPS, None, ALU.add).then_inc(var_done, 1)
                    dve.wait_ge(std1_done, t + 1)
                    nc.vector.reciprocal(rstd1[:, :], std1[:, :]).then_inc(rstd1_done, 1)
                    dve.wait_ge(rstd1_done, t + 1)
                    nc.vector.tensor_copy(rstd_all[:, bass.ds(NS * t, NS)], rstd1[:, :])
                    nc.vector.tensor_tensor(ms2[:, :], rstd1[:, :], rstd1[:, :], ALU.mult).then_inc(sq_done, 1)
                    dve.wait_ge(sq_done, 2 * t + 1)
                    nc.vector.tensor_tensor(ms2[:, :], ms2[:, :], mom[:, :, 1], ALU.mult).then_inc(sq_done, 1)
                    dve.wait_ge(sq_done, 2 * t + 2)
                    nc.vector.tensor_scalar(ms2[:, :], ms2[:, :], EPS, None, ALU.add).then_inc(ms_done, 1)
                    dve.wait_ge(std2_done, t + 1)
                    nc.vector.reciprocal(rstd2[:, :], std2[:, :]).then_inc(rstd2_done, 1)
                    dve.wait_ge(rstd2_done, t + 1)
                    nc.vector.tensor_tensor(scale12[:, :], rstd1[:, :], rstd2[:, :], ALU.mult).then_inc(scale_done, 1)
                    dve.wait_ge(scale_done, t + 1)
                    if not (isinstance(t, int) and t == 0):
                        dve.wait_ge(transposed, NC * t)
                    for s in range(NS):
                        last = nc.vector.tensor_scalar(uh[:, s, :], xb[:, u, s, :], mom[:, s, 0:1], scale12[:, s:s + 1],
                                                       ALU.subtract, ALU.mult)
                    last.then_inc(normed, 1)

                def tails(j, v):
                    t = 2 * j + v
                    for c in range(NC):
                        dve.wait_ge(head_done, NC * t + c + 1)
                        nc.vector.tensor_tensor(u_tail[:, c, :], u_ps[:, c, :], u_head[:, c, :].bitcast(F32),
                                                ALU.subtract).then_inc(tail_done, 1)

                def finish(j, v):
                    t = 2 * j + v
                    dve.wait_ge(dtx_done, t + 2)
                    if not (isinstance(t, int) and t == 0):
                        dve.wait_ge(stored[2], 128 * t)
                    flat = lambda buf: buf[:, :, :].rearrange("p k t -> p (k t)")
                    nc.vector.tensor_copy(parts[:, 0, :].bitcast(F32R), flat(log_w))
                    nc.vector.tensor_copy(parts[:, 2, :].bitcast(F32R), flat(inv_w)).then_inc(ph_done, 1)
                    dve.wait_ge(ph_done, t + 1)
                    nc.vector.tensor_tensor(parts[:, 1, :].bitcast(F32R), flat(log_w), parts[:, 0, :], ALU.subtract)
                    nc.vector.tensor_tensor(parts[:, 3, :].bitcast(F32R), flat(inv_w), parts[:, 2, :],
                                            ALU.subtract).then_inc(parts_done, 1)

                def copies(j, v):
                    t = 2 * j + v
                    dve.wait_ge(dtr_head_done, t + 1)
                    nc.vector.tensor_tensor(dtr_tail[:, :], o_ps[:, 0, :], dtr_head[:, :].bitcast(F32),
                                            ALU.subtract).then_inc(o_free[0], 1)
                    for k in by_dve:
                        if k == 11:
                            if not (isinstance(t, int) and t == 0):
                                finish(j, v - 1)
                            dve.wait_ge(e_done, t + 1)
                            nc.vector.tensor_scalar(one_e[:, :, :], mag[:, :, :], 1.0, None, ALU.add).then_inc(one_e_done, 1)
                        dve.wait_ge(out_ready, NOUT * t + k + 1)
                        if not (isinstance(t, int) and t == 0):
                            if k == 2:
                                dve.wait_ge(stored[0], 32 * t)
                            if k == 11:
                                dve.wait_ge(stored[1], 16 * t)
                        slot = k - 2 if k < 7 else k - 6
                        nc.vector.tensor_copy(bcz[:, slot, :], o_ps[:, k % 4, :]).then_inc(o_free[k % 4], 1)
                    dve.wait_ge(ln_done, t + 1)
                    nc.vector.scalar_tensor_tensor(log_w[:, :, :], one_e[:, :, :], 1.0, log_w[:, :, :],
                                                   ALU.is_gt, ALU.mult).then_inc(ln_masked, 1)
                    nc.vector.scalar_tensor_tensor(one_e[:, :, :], one_e[:, :, :], 1.0, mag[:, :, :],
                                                   ALU.subtract, ALU.subtract).then_inc(err_done, 1)

                def step(j, v):
                    tails(j, v)
                    if not (isinstance(j, int) and v == NT - 1):
                        norm(j, v + 1)
                    copies(j, v)

                norm(0, 0)
                weight_tails()
                rolled(dve, 1, 2, NT, step, tail=1)
                dve.wait_ge(dtx_done, NT)
                softplus(dve, nc.vector, NT - 1)
                finish(0, NT - 1)

            @block.scalar
            def _(act):
                act.sem_inc(o_free[1], 1)
                act.sem_inc(o_free[0], 1)
                act.sem_inc(o_free[2], 1)
                act.sem_inc(o_free[3], 1)

                def roots(t):
                    act.wait_ge(var_done, t + 1)
                    nc.scalar.activation(std1[:, :], var_eps[:, :], ACT.Sqrt).then_inc(std1_done, 1)
                    act.wait_ge(ms_done, t + 1)
                    nc.scalar.activation(std2[:, :], ms2[:, :], ACT.Sqrt).then_inc(std2_done, 1)

                def step(j, v):
                    t = 2 * j + v
                    first = isinstance(t, int) and t == 0
                    if not first:
                        act.wait_ge(out_ready, NOUT * t)
                    for c in range(NC):
                        act.wait_ge(transposed, NC * t + c + 1)
                        nc.scalar.activation(u_head[:, c, :], u_ps[:, c, :], ACT.Copy).then_inc(head_done, 1)
                    if not (isinstance(t, int) and t == NT - 1):
                        roots(t + 1)
                    act.wait_ge(out_ready, NOUT * t + 1)
                    nc.scalar.activation(dtr_head[:, :], o_ps[:, 0, :], ACT.Copy).then_inc(dtr_head_done, 1)
                    act.wait_ge(out_ready, NOUT * t + 2)
                    if not first:
                        act.wait_ge(stored[3], 16 * t)
                        act.wait_ge(x_repeated, 256 * t)
                    nc.scalar.activation(x_ch[:, :], o_ps[:, 1, :], ACT.Copy).then_inc(o_free[1], 1)
                    for k in range(3, NOUT):
                        if k in by_act:
                            act.wait_ge(out_ready, NOUT * t + k + 1)
                            if not first:
                                if k == 3:
                                    act.wait_ge(stored[0], 32 * t)
                                if k == 12:
                                    act.wait_ge(stored[1], 16 * t)
                            slot = k - 2 if k < 7 else k - 6
                            nc.scalar.activation(bcz[:, slot, :], o_ps[:, k % 4, :], ACT.Copy).then_inc(o_free[k % 4], 1)
                        if k == 7 and not first:
                            act.wait_ge(dtx_done, t + 1)
                        if 7 <= k < 11:
                            c = k - 7
                            act.wait_ge(out_ready, NOUT * t + k + 1)
                            nc.scalar.activation(mag[:, c, :], o_ps[:, k % 4, :], ACT.Abs, bias=dt_bias[:, c:c + 1])
                            nc.scalar.activation(pos[:, c, :], o_ps[:, k % 4, :], ACT.Relu,
                                                 bias=dt_bias[:, c:c + 1]).then_inc(o_free[k % 4], 1)
                        if k == 10:
                            act.wait_ge(o_free[2], freed(10, t))
                            nc.scalar.activation(mag[:, :, :], mag[:, :, :], ACT.Exp, scale=-1.0).then_inc(e_done, 1)
                            act.wait_ge(one_e_done, t + 1)
                            if not first:
                                act.wait_ge(parts_done, t)
                            nc.scalar.activation(log_w[:, :, :], one_e[:, :, :], ACT.Ln).then_inc(ln_done, 1)
                            act.wait_ge(ln_masked, t + 1)
                            nc.scalar.activation(inv_w[:, :, :], log_w[:, :, :], ACT.Exp, scale=-1.0).then_inc(inv_done, 1)

                act.wait_ge(const_loaded, 32)
                roots(0)
                for n, (full, head, _, scale) in enumerate(weights):
                    act.wait_ge(w_loaded[n], 16)
                    nc.scalar.activation(head, full, ACT.Copy, scale=scale).then_inc(w_head_done, 1)
                rolled(act, 1, 2, NT, step, tail=1)

            @block.gpsimd
            def _(pool):
                pool.sem_inc(dtx_done, 1)

                rolled(pool, 1, 2, NT - 1, lambda j, v: softplus(pool, nc.gpsimd, 2 * j + v))

            @block.tensor
            def _(pe):
                def step(j, v):
                    t = 2 * j + v
                    first = isinstance(t, int) and t == 0
                    pe.wait_ge(normed, t + 1)
                    pe.wait_ge(tail_done, NC * t + 1)
                    for c in range(NC):
                        for s in range(NS):
                            last = nc.tensor.transpose(u_ps[:, c, P * s:P * (s + 1)], uh[:, s, P * c:P * (c + 1)], ident[:, :])
                        last.then_inc(transposed, 1)
                    if first:
                        pe.wait_ge(w_ready, NC + 1)
                    for k, m in enumerate(ORDER):
                        uses = USES[k % 4] * t + k // 4
                        pe.wait_ge(o_free[k % 4], uses + 1)
                        out = o_ps[:, k % 4, :]
                        if m is None:
                            rows = slice(P * (k - 7), P * (k - 6))
                            last = products3(nc, out, dtw_head[:, rows], dtw_tail[:, rows], dtr_head[:, :], dtr_tail[:, :],
                                             True, True)
                        else:
                            rows = slice(P * m, P * (m + 1))
                            for c in range(NC):
                                if k == 0:
                                    pe.wait_ge(tail_done, NC * t + c + 2)
                                last = products3(nc, out, w_head[:, c, rows], w_tail[:, c, rows], u_head[:, c, :],
                                                 u_tail[:, c, :], c == 0, c == NC - 1)
                        last.then_inc(out_ready, 1)

                pe.wait_ge(persist["ident_ready"], 2)
                rolled(pe, 1, 2, NT, step)


def stage2(nc, d, persist):
    ITS = BATCH * NC
    TILES = P // 4
    with ExitStack() as ctx:
        sb = lambda name, shape, dt=F32: ctx.enter_context(nc.sbuf_tensor("s2_" + name, shape, dt))
        ps = lambda name, shape, dt=F32: ctx.enter_context(nc.psum_tensor("s2_" + name, shape, dt))
        sem = lambda name: ctx.enter_context(nc.semaphore("s2_" + name))
        dt_in = sb("dt_in", [P, 2, 2, SEQ], F32R)
        dtx_in = sb("dtx_in", [P, 2, 2, SEQ], F32R)
        B_in = sb("B_in", [P, 2, SEQ])
        C_in = sb("C_in", [P, 2, REP, SEQ])
        x_in = sb("x_in", [P, 2, SEQ])
        y_sb = sb("y_sb", [P, 2, SEQ])
        negA = sb("negA", [P, ITS * TILES])
        D_all = sb("D_all", [P, ITS])
        A_cur = sb("A_cur", [P, 2, TILES])
        D_cur = sb("D_cur", [P, 2, 1])
        dtxB = sb("dtxB", [P, 4, SEQ])
        h = sb("h", [P, 4, SEQ])
        hc = sb("hc", [P, 8, SEQ])
        ones = sb("ones", [P, 16 * 128])
        spread = sb("spread", [P, 16, P], F32R)
        gather = sb("gather", [P, 8, STATE])
        dt_ps = ps("dt_ps", [P, 2, SEQ])
        dtx_ps = ps("dtx_ps", [P, SEQ])
        y_ps = ps("y_ps", [P, SEQ])

        loaded = [sem("loaded0"), sem("loaded1")]
        cx_loaded = [sem("cx_loaded0"), sem("cx_loaded1")]
        const_loaded, A_ready, made = sem("const_loaded"), sem("A_ready"), sem("made")
        A_copied = sem("A_copied")
        dt_ready, exp_done = sem("dt_ready"), sem("exp_done")
        dtx_ready, b_done = sem("dtx_ready"), sem("b_done")
        scanned, multiplied = sem("scanned"), sem("multiplied")
        summed = sem("summed")
        y_out = sem("y_out")
        y_stored = [sem("y_stored0"), sem("y_stored1")]
        DMAS, CX_DMAS = 6, 8

        with nc.Block() as block:
            @block.sync
            def _(sp):
                def constants():
                    for b in range(BATCH):
                        sp.dma_start(negA[:, P * b:P * (b + 1)], d["A_log"]).then_inc(const_loaded, 16)
                        sp.dma_start(D_all[:, NC * b:NC * (b + 1)], d["D"]).then_inc(const_loaded, 16)

                def load(it, u):
                    flat = lambda name: d[name].rearrange("b k h r t -> (b k) r h t")
                    inc = lambda ins: ins.then_inc(loaded[u], 16)
                    inc(sp.dma_start(dt_in[:, u].bitcast(F32), flat("dt_s")[it]))
                    inc(sp.dma_start(dtx_in[:, u].bitcast(F32), flat("dtx_s")[it]))
                    for n in range(4):
                        rows = slice(STATE * n, STATE * (n + 1))
                        inc(sp.dma_start(B_in[rows, u], d["B_s"].rearrange("b (g n) t -> (b g) n t", n=STATE)[it]))
                    if isinstance(it, int) and it == 0:
                        constants()
                    inc = lambda ins: ins.then_inc(cx_loaded[u], 16)
                    for n in range(4):
                        rows = slice(STATE * n, STATE * (n + 1))
                        inc(sp.dma_start(C_in[rows, u], d["C_s"].rearrange("b k (r n) t -> (b k) n r t", n=STATE)[it]))
                        inc(sp.dma_start(x_in[rows, u], d["x_s"].rearrange("b (g n) t -> (b g) n t", n=STATE)[it]))

                def store(it, u):
                    sp.dma_start(d["y_s"].rearrange("b k p t -> (b k) p t")[it], y_sb[:, u]).then_inc(y_stored[u], 16)

                def step(j, v):
                    it, u = 2 * j + v, v % 2
                    if not (isinstance(j, int) and j == 0 and v < 2):
                        sp.wait_ge(y_out, it + 1)
                        store(it - 2, u)
                    load(it, u)

                assert (DMAS, CX_DMAS) == (2 + 4, 2 * 4)
                rolled(sp, 2, 2, ITS, step)
                for it in (ITS - 2, ITS - 1):
                    sp.wait_ge(y_out, it + 3)
                    store(it, it % 2)
                for u in range(2):
                    sp.wait_ge(y_stored[u], 16 * (ITS // 2))

            @block.gpsimd
            def _(pool):
                pool.sem_inc(multiplied, 4)
                nc.gpsimd.memset(ones[:, :], 0.0).then_inc(made, 1)
                pat = ones[:, :].rearrange("p (q j n) -> p q j n", q=16, j=4)
                pool.wait_ge(made, 1)
                for n in range(2):
                    nc.gpsimd.affine_select(out=pat, in_=pat, compare_op=ALU.not_equal, fill=1.0, base=-64 * n,
                                            pattern=[[-4, 16], [-1, 4], [0, STATE]], channel_multiplier=1).then_inc(made, 1)
                    pool.wait_ge(made, n + 2)
                nc.gpsimd.memset(gather[:, :, :], 1.0).then_inc(made, 1)
                pool.wait_ge(made, 4)
                nc.gpsimd.affine_select(out=gather[:, :, :], in_=gather[:, :, :], compare_op=ALU.is_ge, fill=0.0, base=0,
                                        pattern=[[P, 8], [-STATE, STATE]], channel_multiplier=1).then_inc(made, 1)
                pool.wait_ge(made, 5)
                nc.gpsimd.affine_select(out=gather[:, :, :], in_=gather[:, :, :], compare_op=ALU.is_ge, fill=0.0,
                                        base=STATE - 1, pattern=[[-P, 8], [STATE, STATE]],
                                        channel_multiplier=-1).then_inc(made, 1)

                def step(j, v):
                    w, u = 2 * TILES * j + v, (v // TILES) % 2
                    r = v % 4
                    if v % TILES == 0:
                        pool.wait_ge(cx_loaded[u], 16 * CX_DMAS * (j + v // (2 * TILES) + 1))
                    pool.wait_ge(scanned, w + 5)
                    if v % 4 == 0:
                        pool.wait_ge(summed, 2 * TILES // 4 * j + v // 4 + 1)
                    nc.gpsimd.tensor_tensor(hc[:, v % 8], h[:, v % 4], C_in[:, u, r], ALU.mult).then_inc(multiplied, 1)

                rolled(pool, 0, 2 * TILES, ITS * TILES, step)

            @block.scalar
            def _(act):
                act.wait_ge(made, 3)
                nc.scalar.activation(spread[:, :, :].rearrange("p q m -> p (q m)"), ones[:, :], ACT.Copy).then_inc(A_ready, 1)
                act.wait_ge(const_loaded, 32 * BATCH)
                nc.scalar.activation(negA[:, :], negA[:, :], ACT.Exp).then_inc(A_ready, 1)
                act.wait_ge(A_ready, 2)
                nc.scalar.mul(negA[:, :], negA[:, :], -1.0).then_inc(A_ready, 1)

                def step(j, v):
                    w, u = 2 * TILES * j + v, (v // TILES) % 2
                    if v % TILES == 0:
                        act.wait_ge(A_copied, 2 * j + v // TILES + 1)
                    for k in range(2):
                        act.wait_ge(dt_ready, 2 * w + k + 1)
                        tok = dt_ps[:, v % 2, 512 * k:512 * (k + 1)]
                        nc.scalar.activation(tok, tok, ACT.Exp,
                                             scale=A_cur[:, u, v % TILES:v % TILES + 1]).then_inc(exp_done, 1)

                rolled(act, 0, 2 * TILES, ITS * TILES, step)

            @block.vector
            def _(dve):
                dve.sem_inc(scanned, 4)
                dve.sem_inc(b_done, 1)
                dve.sem_inc(y_out, 2)
                dve.wait_ge(A_ready, 3)

                def evac(it, u, n):
                    dve.wait_ge(A_copied, it + 1)
                    dve.wait_ge(summed, TILES // 4 * (it + 1) + 2)
                    if not (isinstance(n, int) and n == 0):
                        dve.wait_ge(y_stored[u], 16 * n)
                    nc.vector.scalar_tensor_tensor(y_sb[:, u], x_in[:, u], D_cur[:, u], y_ps[:, :],
                                                   ALU.mult, ALU.add).then_inc(y_out, 1)

                def scan(w, slot):
                    dve.wait_ge(b_done, w + 2)
                    dve.wait_ge(exp_done, 2 * w + 2)
                    dve.wait_ge(multiplied, w + 1)
                    nc.vector.tensor_tensor_scan(h[:, slot], dt_ps[:, slot % 2], dtxB[:, slot], 0.0,
                                                 ALU.mult, ALU.add).then_inc(scanned, 1)

                def step(j, v):
                    w, it, u = 2 * TILES * j + v, 2 * j + v // TILES, (v // TILES) % 2
                    if v % TILES == 0:
                        dve.wait_ge(loaded[u], 16 * DMAS * (j + v // (2 * TILES) + 1))
                        nc.vector.tensor_copy(D_cur[:, u], D_all[:, bass.ds(it, 1)])
                        nc.vector.tensor_copy(A_cur[:, u], negA[:, bass.ds(TILES * it, TILES)]).then_inc(A_copied, 1)
                    dve.wait_ge(dtx_ready, w + 1)
                    dve.wait_ge(scanned, w + 1)
                    nc.vector.tensor_tensor(dtxB[:, v % 4], dtx_ps[:, :], B_in[:, u], ALU.mult).then_inc(b_done, 1)
                    if not (isinstance(j, int) and j == 0 and v == 0):
                        scan(w - 1, (v - 1) % 4)
                    if v >= TILES and v % TILES == 5:
                        vb = v // TILES - 1
                        evac(2 * j + vb, vb % 2, j + vb // 2)

                rolled(dve, 7, 2 * TILES, ITS * TILES, step)
                scan(ITS * TILES - 1, 3)
                evac(ITS - 1, 1, ITS // 2 - 1)

            @block.tensor
            def _(pe):
                pe.sem_inc(summed, 2)
                LAG = 6

                def spread_tile(j, v):
                    w, u = 2 * TILES * j + v, (v // TILES) % 2
                    q, r = (v % TILES) // 4, v % 4
                    half, sel = r // 2, (r % 2) * 8 + q
                    if v % TILES == 0:
                        pe.wait_ge(loaded[u], 16 * DMAS * (j + v // (2 * TILES) + 1))
                    pe.wait_ge(b_done, w + 1)
                    for k in range(2):
                        cols = slice(512 * k, 512 * (k + 1))
                        last = nc.tensor.matmul(dtx_ps[:, cols], spread[:, sel], dtx_in[:, u, half, cols], start=True, stop=True)
                    last.then_inc(dtx_ready, 1)
                    pe.wait_ge(scanned, w + 3)
                    for k in range(2):
                        cols = slice(512 * k, 512 * (k + 1))
                        nc.tensor.matmul(dt_ps[:, v % 2, cols], spread[:, sel], dt_in[:, u, half, cols],
                                         start=True, stop=True).then_inc(dt_ready, 1)

                def sum_tiles(j, v, k):
                    w, q = 2 * TILES * j + v, (v % TILES) // 4
                    if q == 0 and k == 0:
                        pe.wait_ge(y_out, 2 * j + v // TILES + 2)
                    pe.wait_ge(multiplied, w + 8)
                    for r in range(4):
                        last = nc.tensor.matmul(y_ps[STATE * r:STATE * (r + 1), 512 * k:512 * (k + 1)], gather[:, q],
                                                hc[:, (v + r) % 8, 512 * k:512 * (k + 1)], start=(q == 0), stop=(q == 7))
                    if k == 1:
                        last.then_inc(summed, 1)

                def step(j, v):
                    spread_tile(j, v)
                    for k in range(2):
                        if v % 4 == (LAG + k) % 4 and not (isinstance(j, int) and j == 0 and v < LAG + k):
                            sum_tiles(j, v - LAG - k, k)

                pe.wait_ge(made, 6)
                pe.wait_ge(A_ready, 1)
                rolled(pe, LAG + 1, 2 * TILES, ITS * TILES, step)
                for k in range(2):
                    sum_tiles(0, ITS * TILES - 4, k)


def stage3(nc, d, persist):
    ident, mean_all, rstd_all = persist["ident"], persist["mean_all"], persist["rstd_all"]
    rows_v = lambda name: d[name].rearrange("(b u s p) c -> b u p s c", b=BATCH, u=UP, p=P)
    with ExitStack() as ctx:
        sb = lambda name, shape, dt=F32: ctx.enter_context(nc.sbuf_tensor("s3_" + name, shape, dt))
        ps = lambda name, shape, dt=F32: ctx.enter_context(nc.psum_tensor("s3_" + name, shape, dt))
        sem = lambda name: ctx.enter_context(nc.semaphore("s3_" + name))
        out_head, out_tail = (sb(n, [P, NC, DM], F32R) for n in ("out_head", "out_tail"))
        gate_head, gate_tail = (sb(n, [P, NC, FF], F32R) for n in ("gate_head", "gate_tail"))
        up_head, up_tail = (sb(n, [P, NC, FF], F32R) for n in ("up_head", "up_tail"))
        down_head, down_tail = (sb(n, [P, NF, DM], F32R) for n in ("down_head", "down_tail"))
        norm2 = sb("norm2", [P, NC])
        work = sb("work", [P, 4, NC * TT])
        Y, Z, *X = (work[:, n, :].rearrange("p (k t) -> p k t", k=NC) for n in range(4))
        a_head = sb("a_head", [P, NC, TT], F32R)
        a_tail = sb("a_tail", [P, NC, TT], F32R)
        gu = sb("gate_up", [P, TT])
        gu_head = sb("gu_head", [P, 2, TT], F32R)
        gu_tail = sb("gu_tail", [P, 2, TT], F32R)
        sumsq = sb("sumsq", [P, NS])
        msq = sb("msq", [P, NS])
        std = sb("std", [P, NS])
        rstd = sb("rstd", [P, NS])
        mean_cur = sb("mean_cur", [P, NS])
        rstd_cur = sb("rstd_cur", [P, NS])
        gu_ps = ps("gu_ps", [P, 4, TT])
        acc_ps = ps("acc_ps", [P, NC, TT])

        w_loaded = [sem(f"w_loaded{n}") for n in range(4)]
        w_head_done, w_tail_done, cur_done = sem("w_head"), sem("w_tail"), sem("cur")
        norm_loaded = sem("norm_loaded")
        yz_loaded, x1_stored = sem("yz_loaded"), sem("x1_stored")
        x_loaded = [sem("x_loaded0"), sem("x_loaded1")]
        silu_z, gated, a_head_y, a_tail_y = sem("silu_z"), sem("gated"), sem("a_head_y"), sem("a_tail_y")
        o_ready, u0_done, h_done, xh_done = sem("o_ready"), sem("u0"), sem("h"), sem("xh")
        sq_done, msq_done, std_done, rstd_done, hn_done = (
            sem("sq"), sem("msq"), sem("std"), sem("rstd"), sem("hn"))
        transposed, a_head_x, a_tail_x = sem("transposed"), sem("a_head_x"), sem("a_tail_x")
        gu_ready = sem("gu_ready")
        sg_done, gu_done, guh_done, gut_done = sem("sg"), sem("gu"), sem("gu_head"), sem("gu_tail")
        down_done = sem("down")
        x1_done = sem("x1")

        weights = [(d["out_w"], out_head, out_tail, NC, DM, False), (d["gate_w"], gate_head, gate_tail, NC, FF, True),
                   (d["up_w"], up_head, up_tail, NC, FF, True), (d["down_w"], down_head, down_tail, NF, DM, False)]
        SLOT = FF
        flat = work[:, :, :].rearrange("p a n -> p (a n)")
        pieces = []
        for src, head, tail, blocks, cols, scaled in weights:
            per = max(1, SLOT // cols)
            for c in range(0, blocks, per):
                n = min(per, blocks - c)
                slot = len(pieces) % 4
                pieces.append((src.rearrange("(c p) m -> p c m", p=P)[:, c:c + n, :],
                               flat[:, slot * SLOT:slot * SLOT + n * cols].rearrange("p (c m) -> p c m", c=n),
                               head[:, c:c + n, :], tail[:, c:c + n, :], norm2[:, c:c + 1] if scaled else 1.0))
        first_gate = 2
        first_down = first_gate + 2 * NC
        assert NC * DM <= 2 * SLOT

        with nc.Block() as block:
            @block.sync
            def _(sp):
                sp.dma_start(norm2[:, :], d["norm2"]).then_inc(norm_loaded, 16)
                for n, (src, slot, _, _, _) in enumerate(pieces):
                    if n >= 4:
                        sp.wait_ge(w_tail_done, n - 3)
                    sp.dma_start(slot, src).then_inc(w_loaded[n % 4], 16)
                sp.wait_ge(w_tail_done, len(pieces))

                def load_yz(j, v):
                    tok = slice(v % 2 * TT, (v % 2 + 1) * TT)
                    sp.dma_start(Y, d["y_s"][j + v // 2, :, :, tok].rearrange("k p t -> p k t")).then_inc(yz_loaded, 16)
                    sp.dma_start(Z, d["z_s"][j + v // 2, :, :, tok].rearrange("k p t -> p k t")).then_inc(yz_loaded, 16)

                def load_x(j, v):
                    sp.dma_start(X[v % 2], rows_v("x")[j + v // 2, v % 2]).then_inc(x_loaded[v % 2], 16)

                def store(j, v):
                    sp.dma_start(rows_v("x1_s")[j + v // 2, v % 2], X[v % 2]).then_inc(x1_stored, 16)

                def step(j, v):
                    t = 2 * j + v
                    if not (isinstance(t, int) and t == 0):
                        sp.wait_ge(x1_done, t)
                        sp.sem_inc(persist["passed"], 1)
                        store(j, v - 1)
                        sp.wait_ge(x1_stored, 16 * t)
                        sp.sem_inc(persist["passed"], 1)
                    if not (isinstance(t, int) and t == NT - 1):
                        load_x(j, v + 1)
                        sp.wait_ge(hn_done, NS * (t + 1))
                        sp.wait_ge(xh_done, t + 1)
                        sp.wait_ge(transposed, NC * (t + 1))
                        sp.sem_inc(persist["passed"], 1)
                        load_yz(j, v + 1)

                load_yz(0, 0)
                load_x(0, 0)
                rolled(sp, 1, 2, NT, step, tail=1)
                sp.wait_ge(x1_done, NT)
                store(0, NT - 1)
                sp.wait_ge(x1_stored, 16 * NT)

            @block.scalar
            def _(act):
                act.wait_ge(norm_loaded, 16)
                for n, (_, slot, head, _, scale) in enumerate(pieces):
                    act.wait_ge(w_loaded[n % 4], 16 * (n // 4 + 1))
                    nc.scalar.activation(head, slot, ACT.Copy, scale=scale).then_inc(w_head_done, 1)

                def silu(t):
                    act.wait_ge(yz_loaded, 32 * (t + 1))
                    nc.scalar.activation(Z, Z, ACT.Silu).then_inc(silu_z, 1)

                def heads_y(t):
                    act.wait_ge(gated, t + 1)
                    if not (isinstance(t, int) and t == 0):
                        act.wait_ge(gu_ready, 2 * NF * t)
                    nc.scalar.activation(a_head[:, :, :], Y, ACT.Copy).then_inc(a_head_y, 1)

                def step(j, v):
                    t = 2 * j + v
                    first, last = isinstance(t, int) and t == 0, isinstance(t, int) and t == NT - 1
                    for s in range(NS):
                        n = NS * t + s + 1
                        act.wait_ge(h_done, n)
                        nc.scalar.activation(Z[:, s, :], Y[:, s, :], ACT.Square, accum_out=sumsq[:, s:s + 1]).then_inc(sq_done, 1)
                        act.wait_ge(msq_done, n)
                        nc.scalar.activation(std[:, s:s + 1], msq[:, s:s + 1], ACT.Sqrt).then_inc(std_done, 1)
                        act.wait_ge(rstd_done, n)
                        nc.scalar.activation(Z[:, s, :], Y[:, s, :], ACT.Copy, scale=rstd[:, s:s + 1]).then_inc(hn_done, 1)
                    act.wait_ge(o_ready, NS * (t + 1))
                    for c in range(NC):
                        act.wait_ge(transposed, NC * t + c + 1)
                        nc.scalar.activation(a_head[:, c, :], acc_ps[:, c, :], ACT.Copy).then_inc(a_head_x, 1)
                    for f in range(NF):
                        n = NF * t + f
                        act.wait_ge(gu_ready, 2 * n + 1)
                        if not (first and f == 0):
                            act.wait_ge(gut_done, n)
                        nc.scalar.activation(gu[:, :], gu_ps[:, 2 * f % 4, :], ACT.Silu).then_inc(sg_done, 1)
                        act.wait_ge(gu_done, n + 1)
                        if not (first and f < 2):
                            act.wait_ge(down_done, n - 1)
                        nc.scalar.activation(gu_head[:, f % 2, :], gu[:, :], ACT.Copy).then_inc(guh_done, 1)
                        if f == NF - 3 and not last:
                            silu(t + 1)
                    if not last:
                        heads_y(t + 1)

                silu(0)
                heads_y(0)
                rolled(act, 1, 2, NT, step, tail=1)

            @block.vector
            def _(dve):
                for n, (_, slot, head, tail, scale) in enumerate(pieces):
                    dve.wait_ge(w_head_done, n + 1)
                    nc.vector.scalar_tensor_tensor(tail, slot, scale, head.bitcast(F32), ALU.mult,
                                                   ALU.subtract).then_inc(w_tail_done, 1)

                def gate_y(t):
                    dve.wait_ge(silu_z, t + 1)
                    nc.vector.tensor_tensor(Y, Y, Z, ALU.mult).then_inc(gated, 1)

                def tails_y(t):
                    dve.wait_ge(a_head_y, t + 1)
                    nc.vector.tensor_tensor(a_tail[:, :, :], Y, a_head[:, :, :].bitcast(F32), ALU.subtract).then_inc(a_tail_y, 1)

                def layer_norm(j, v):
                    t, u = 2 * j + v, v % 2
                    dve.wait_ge(x_loaded[u], 16 * (j + v // 2 + 1))
                    dve.wait_ge(a_tail_y, t + 1)
                    nc.vector.tensor_copy(mean_cur[:, :], mean_all[:, bass.ds(NS * t, NS)])
                    nc.vector.tensor_copy(rstd_cur[:, :], rstd_all[:, bass.ds(NS * t, NS)]).then_inc(cur_done, 1)
                    dve.wait_ge(cur_done, t + 1)
                    for s in range(NS):
                        u0 = nc.vector.tensor_scalar(Y[:, s, :], X[u][:, s, :], mean_cur[:, s:s + 1], rstd_cur[:, s:s + 1],
                                                     ALU.subtract, ALU.mult)
                    u0.then_inc(u0_done, 1)
                    dve.wait_ge(u0_done, t + 1)

                def step(j, v):
                    t, u = 2 * j + v, v % 2
                    last = isinstance(t, int) and t == NT - 1
                    for s in range(NS):
                        n = NS * t + s + 1
                        dve.wait_ge(o_ready, n)
                        nc.vector.tensor_tensor(Y[:, s, :], Y[:, s, :], gu_ps[:, s, :], ALU.add).then_inc(h_done, 1)
                        dve.wait_ge(sq_done, n)
                        nc.vector.tensor_scalar(msq[:, s:s + 1], sumsq[:, s:s + 1], 1.0 / DM, EPS, ALU.mult, ALU.add).then_inc(msq_done, 1)
                        dve.wait_ge(std_done, n)
                        nc.vector.reciprocal(rstd[:, s:s + 1], std[:, s:s + 1]).then_inc(rstd_done, 1)
                    dve.wait_ge(h_done, NS * (t + 1))
                    nc.vector.tensor_tensor(X[u], X[u], Y, ALU.add).then_inc(xh_done, 1)
                    for c in range(NC):
                        dve.wait_ge(a_head_x, NC * t + c + 1)
                        nc.vector.tensor_tensor(a_tail[:, c, :], acc_ps[:, c, :], a_head[:, c, :].bitcast(F32),
                                                ALU.subtract).then_inc(a_tail_x, 1)
                    for f in range(NF):
                        n = NF * t + f
                        dve.wait_ge(sg_done, n + 1)
                        dve.wait_ge(gu_ready, 2 * n + 2)
                        nc.vector.tensor_tensor(gu[:, :], gu[:, :], gu_ps[:, (2 * f + 1) % 4, :], ALU.mult).then_inc(gu_done, 1)
                        dve.wait_ge(guh_done, n + 1)
                        nc.vector.tensor_tensor(gu_tail[:, f % 2, :], gu[:, :], gu_head[:, f % 2, :].bitcast(F32),
                                                ALU.subtract).then_inc(gut_done, 1)
                        if f == NF - 2 and not last:
                            gate_y(t + 1)
                    if not last:
                        tails_y(t + 1)
                        layer_norm(j, v + 1)
                    dve.wait_ge(down_done, NF * (t + 1))
                    dve.wait_ge(xh_done, t + 1)
                    nc.vector.tensor_tensor(X[u], X[u], acc_ps[:, :, :], ALU.add).then_inc(x1_done, 1)

                gate_y(0)
                tails_y(0)
                layer_norm(0, 0)
                rolled(dve, 1, 2, NT, step, tail=1)

            @block.tensor
            def _(pe):
                def step(j, v):
                    t = 2 * j + v
                    first = isinstance(t, int) and t == 0
                    if first:
                        pe.wait_ge(w_tail_done, first_gate)
                    pe.wait_ge(a_tail_y, t + 1)
                    if not first:
                        pe.wait_ge(gut_done, NF * t)
                    def turn(s):
                        if s == 0 and not first:
                            pe.wait_ge(x1_done, t)
                        pe.wait_ge(hn_done, NS * t + s + 1)
                        for c in range(NC):
                            last = nc.tensor.transpose(acc_ps[:, c, P * s:P * (s + 1)], Z[:, s, P * c:P * (c + 1)], ident[:, :])
                            if s == NS - 1:
                                last.then_inc(transposed, 1)

                    for s in range(NS):
                        for c in range(NC):
                            cols = slice(P * s, P * (s + 1))
                            last = products3(nc, gu_ps[:, s, :], a_head[:, c, cols], a_tail[:, c, cols], out_head[:, c, :],
                                             out_tail[:, c, :], c == 0, c == NC - 1)
                        last.then_inc(o_ready, 1)
                        if s >= 2:
                            turn(s - 2)
                    turn(NS - 2)
                    turn(NS - 1)
                    if first:
                        pe.wait_ge(w_tail_done, first_down)

                    def down(f):
                        pe.wait_ge(gut_done, NF * t + f + 1)
                        if f == 0 and first:
                            pe.wait_ge(w_tail_done, len(pieces))
                        if f == 0:
                            pe.wait_ge(a_tail_x, NC * (t + 1))
                        for s in range(NS):
                            cols = slice(P * s, P * (s + 1))
                            last = products3(nc, acc_ps[:, s, :], gu_head[:, f % 2, cols], gu_tail[:, f % 2, cols],
                                             down_head[:, f, :], down_tail[:, f, :], f == 0, f == NF - 1)
                        last.then_inc(down_done, 1)

                    for f in range(NF):
                        n = NF * t + f
                        if not (first and f < 2):
                            pe.wait_ge(gu_done, n - 1)
                        if f < 2:
                            pe.wait_ge(h_done, NS * (t + 1))
                        rows = slice(P * f, P * (f + 1))
                        for k, (head, tail) in enumerate(((gate_head, gate_tail), (up_head, up_tail))):
                            for c in range(NC):
                                if f == 0 and k == 0:
                                    pe.wait_ge(a_tail_x, NC * t + c + 1)
                                last = products3(nc, gu_ps[:, (2 * f + k) % 4, :], head[:, c, rows], tail[:, c, rows],
                                                 a_head[:, c, :], a_tail[:, c, :], c == 0, c == NC - 1)
                            last.then_inc(gu_ready, 1)
                        if f:
                            down(f - 1)
                    down(NF - 1)

                rolled(pe, 1, 2, NT, step, tail=1)


def stage4(nc, d, persist):
    ident = persist["ident"]
    RA = 8
    STD = HD - RA
    rows_v = lambda name: d[name].rearrange("(b u s p) c -> b u p s c", b=BATCH, u=UP, p=P)
    with ExitStack() as ctx:
        sb = lambda name, shape, dt=F32: ctx.enter_context(nc.sbuf_tensor("s4_" + name, shape, dt))
        ps = lambda name, shape, dt=F32: ctx.enter_context(nc.psum_tensor("s4_" + name, shape, dt))
        sem = lambda name: ctx.enter_context(nc.semaphore("s4_" + name))
        q_w, k_w, v_w = (sb(n, [P, NC, DM]) for n in ("q_w", "k_w", "v_w"))
        heads = [sb(n, [P, NC, DM], F32R) for n in ("q_head", "k_head", "v_head")]
        tails = [sb(n, [P, NC, DM], F32R) for n in ("q_tail", "k_tail", "v_tail")]
        w_sr = sb("w_sr", [P, 2, HEADS])
        s_sr = sb("s_sr", [P, 2, HEADS])
        q_sr = sb("q_sr", [P, 2, HEADS])
        use_ra = sb("use_ra", [P, 2, HEADS])
        mix = sb("mix", [P, 4, NC, HEADS, RA])
        xb = sb("x_rows", [P, 2, NS, DM])
        uh = sb("u_rows", [P, NS, DM])
        stats = sb("stats", [P, NS, 6])
        mom = sb("moments", [P, NS, 2])
        var_eps = sb("var_eps", [P, NS])
        std = sb("std", [P, NS])
        rstd = sb("rstd", [P, NS])
        u_head = sb("u_head", [P, NC, TT], F32R)
        u_tail = sb("u_tail", [P, NC, TT], F32R)
        qk = sb("qk", [P, 4, NC, TT])
        v_rows = sb("v_rows", [P, NS, DM])
        u_ps = ps("u_ps", [P, NC, TT])
        o_ps = ps("o_ps", [P, 4, TT])

        w_loaded, wv_loaded, s_ready, mixed, scaled = (
            sem("w_loaded"), sem("wv_loaded"), sem("s_ready"), sem("mixed"), sem("scaled"))
        w_head_done, w_tail_done = sem("w_head"), sem("w_tail")
        x_loaded = [sem("x_loaded0"), sem("x_loaded1")]
        stats_done, mom_done, var_done, std_done, rstd_done, normed = (
            sem("stats"), sem("moments"), sem("var_eps"), sem("std"), sem("rstd"), sem("normed"))
        transposed, head_done, tail_done = sem("transposed"), sem("u_head"), sem("u_tail")
        out_ready = sem("out_ready")
        copied, split = sem("copied"), sem("split")
        qk_stored, v_stored = sem("qk_stored"), sem("v_stored")
        NOUT = 12

        with nc.Block() as block:
            @block.sync
            def _(sp):
                sp.dma_start(xb[:, 0], rows_v("x1_s")[0, 0]).then_inc(x_loaded[0], 16)
                for n, name in enumerate(("w_std", "w_rec")):
                    sp.dma_start(w_sr[:, n, :], d[name].partition_broadcast(P)).then_inc(w_loaded, 16)
                for buf, name, loaded in ((q_w, "wq", w_loaded), (k_w, "wk", w_loaded), (v_w, "wv", wv_loaded)):
                    sp.dma_start(buf[:, :, :], d[name].rearrange("(c p) m -> p c m", p=P)).then_inc(loaded, 16)
                sp.dma_start(xb[:, 1], rows_v("x1_s")[0, 1]).then_inc(x_loaded[1], 16)

                def step(j, v):
                    t, b, u = 2 * j + v, j + v // 2, v % 2
                    tok = slice(u * TT, (u + 1) * TT)
                    if not (isinstance(t, int) and t >= NT - 2):
                        sp.wait_ge(normed, t + 1)
                        sp.dma_start(xb[:, u], rows_v("x1_s")[b + 1, u]).then_inc(x_loaded[u], 16)
                    sp.wait_ge(split, 10 * t + 8)
                    for n, name in enumerate(("q_s", "q_s", "k_s", "k_s")):
                        sp.dma_start(d[name][b, :, n % 2, :, tok].rearrange("k p t -> p k t"), qk[:, n]).then_inc(qk_stored, 16)
                    sp.wait_ge(split, 10 * t + 10)
                    sp.wait_ge(copied, 10 * t + 10)
                    sp.dma_start(rows_v("v_s")[b, u], v_rows[:, :, :]).then_inc(v_stored, 16)

                rolled(sp, 0, 2, NT, step, tail=2)
                sp.wait_ge(qk_stored, 64 * NT)
                sp.wait_ge(v_stored, 16 * NT)

            @block.scalar
            def _(act):
                def root(t):
                    act.wait_ge(var_done, t + 1)
                    nc.scalar.activation(std[:, :], var_eps[:, :], ACT.Sqrt).then_inc(std_done, 1)

                def u_heads(t):
                    for c in range(NC):
                        act.wait_ge(transposed, NC * t + c + 1)
                        nc.scalar.activation(u_head[:, c, :], u_ps[:, c, :], ACT.Copy).then_inc(head_done, 1)

                def step(j, v):
                    t = 2 * j + v
                    first = isinstance(t, int) and t == 0
                    if not first:
                        act.wait_ge(out_ready, NOUT * t)
                        u_heads(t)
                    if not (isinstance(t, int) and t == NT - 1):
                        root(t + 1)
                    for k in range(8):
                        act.wait_ge(out_ready, NOUT * t + k + 1)
                        if not first and k == 0:
                            act.wait_ge(qk_stored, 64 * t)
                        nc.scalar.activation(qk[:, 2 * (k // 4), k % 4, :].bitcast(F32R), o_ps[:, k % 4, :],
                                             ACT.Copy).then_inc(copied, 1)
                    for k in (8, 10):
                        act.wait_ge(out_ready, NOUT * t + k + 1)
                        if not first and k == 8:
                            act.wait_ge(v_stored, 16 * t)
                        nc.scalar.activation(v_rows[:, k - 8, :], o_ps[:, k % 4, :], ACT.Copy).then_inc(copied, 1)

                root(0)
                act.wait_ge(s_ready, 1)
                nc.scalar.activation(s_sr[:, :, :], w_sr[:, :, :], ACT.Sqrt).then_inc(s_ready, 1)
                u_heads(0)
                for n, buf in enumerate((q_w, k_w, v_w)):
                    if n < 2:
                        act.wait_ge(scaled, n + 1)
                    else:
                        act.wait_ge(wv_loaded, 16)
                    nc.scalar.activation(heads[n][:, :, :], buf[:, :, :], ACT.Copy).then_inc(w_head_done, 1)
                rolled(act, 1, 2, NT, step, tail=1)

            @block.vector
            def _(dve):
                def norm(j, v):
                    t, u = 2 * j + v, v % 2
                    dve.wait_ge(x_loaded[u], 16 * (j + v // 2 + 1))
                    for s in range(NS):
                        last = nc.vector.bn_stats(stats[:, s, :], xb[:, u, s, :])
                    last.then_inc(stats_done, 1)
                    dve.wait_ge(stats_done, t + 1)
                    dve.sem_inc(persist["passed"], 1)
                    for s in range(NS):
                        last = nc.vector.bn_aggr(mom[:, s, :], stats[:, s, :])
                    last.then_inc(mom_done, 1)
                    dve.wait_ge(mom_done, t + 1)
                    nc.vector.tensor_scalar(var_eps[:, :], mom[:, :, 1], EPS, None, ALU.add).then_inc(var_done, 1)
                    dve.wait_ge(std_done, t + 1)
                    nc.vector.reciprocal(rstd[:, :], std[:, :]).then_inc(rstd_done, 1)
                    dve.wait_ge(rstd_done, t + 1)
                    if not (isinstance(t, int) and t == 0):
                        dve.wait_ge(transposed, NC * t)
                    for s in range(NS):
                        last = nc.vector.tensor_scalar(uh[:, s, :], xb[:, u, s, :], mom[:, s, 0:1], rstd[:, s:s + 1],
                                                       ALU.subtract, ALU.mult)
                    last.then_inc(normed, 1)

                def u_tails(t):
                    for c in range(NC):
                        dve.wait_ge(head_done, NC * t + c + 1)
                        nc.vector.tensor_tensor(u_tail[:, c, :], u_ps[:, c, :], u_head[:, c, :].bitcast(F32),
                                                ALU.subtract).then_inc(tail_done, 1)

                def step(j, v):
                    t = 2 * j + v
                    first = isinstance(t, int) and t == 0
                    if not first:
                        u_tails(t)
                    if not (isinstance(t, int) and t == NT - 1):
                        norm(j, v + 1)
                    for k in range(8):
                        dve.wait_ge(copied, 10 * t + k + 1)
                        if not first and k == 0:
                            dve.wait_ge(qk_stored, 64 * t)
                        n = 2 * (k // 4)
                        nc.vector.tensor_tensor(qk[:, n + 1, k % 4, :].bitcast(F32R), o_ps[:, k % 4, :], qk[:, n, k % 4, :],
                                                ALU.subtract).then_inc(split, 1)
                    for k in (9, 11):
                        dve.wait_ge(out_ready, NOUT * t + k + 1)
                        if not first and k == 9:
                            dve.wait_ge(v_stored, 16 * t)
                        nc.vector.tensor_copy(v_rows[:, k - 8, :], o_ps[:, k % 4, :]).then_inc(split, 1)

                def per_head(buf, n, dims):
                    return buf[:, n, :].unsqueeze(1).unsqueeze(3).broadcast_to([P, NC, HEADS, dims])

                def scale(buf, factors):
                    w = buf[:, :, :].rearrange("p c (h e) -> p c h e", h=HEADS)
                    nc.vector.tensor_tensor(w[:, :, :, 0:STD], w[:, :, :, 0:STD], per_head(factors, 0, STD), ALU.mult)
                    nc.vector.tensor_tensor(w[:, :, :, STD:HD], w[:, :, :, STD:HD], per_head(factors, 1, RA),
                                            ALU.mult).then_inc(scaled, 1)

                norm(0, 0)
                dve.wait_ge(w_loaded, 64)
                nc.vector.tensor_scalar(use_ra[:, 0], w_sr[:, 1], 0.1, None, ALU.is_gt).then_inc(mixed, 1)
                dve.wait_ge(mixed, 1)
                nc.vector.tensor_scalar(use_ra[:, 1], use_ra[:, 0], -1.0, 1.0, ALU.mult, ALU.add).then_inc(mixed, 1)
                nc.vector.tensor_scalar(w_sr[:, :, :], w_sr[:, :, :], 1e-8, None, ALU.max).then_inc(s_ready, 1)
                dve.wait_ge(mixed, 2)
                q_t, k_t = (buf[:, :, :].rearrange("p c (h e) -> p c h e", h=HEADS)[:, :, :, STD:HD] for buf in (q_w, k_w))
                nc.vector.tensor_tensor(mix[:, 0], k_t, per_head(use_ra, 0, RA), ALU.mult)
                nc.vector.tensor_tensor(mix[:, 1], q_t, per_head(use_ra, 1, RA), ALU.mult)
                nc.vector.tensor_tensor(mix[:, 2], q_t, per_head(use_ra, 0, RA), ALU.mult)
                nc.vector.tensor_tensor(mix[:, 3], k_t, per_head(use_ra, 1, RA), ALU.mult).then_inc(mixed, 1)
                dve.wait_ge(mixed, 3)
                nc.vector.tensor_tensor(q_t, mix[:, 0], mix[:, 1], ALU.add)
                nc.vector.tensor_tensor(k_t, mix[:, 2], mix[:, 3], ALU.add).then_inc(mixed, 1)
                dve.wait_ge(s_ready, 2)
                nc.vector.tensor_scalar(q_sr[:, :, :], s_sr[:, :, :], float(HD) ** -0.5, None, ALU.mult).then_inc(s_ready, 1)
                dve.wait_ge(s_ready, 3)
                dve.wait_ge(mixed, 4)
                scale(q_w, q_sr)
                scale(k_w, s_sr)
                u_tails(0)
                for n, buf in enumerate((q_w, k_w, v_w)):
                    dve.wait_ge(w_head_done, n + 1)
                    nc.vector.tensor_tensor(tails[n][:, :, :], buf[:, :, :], heads[n][:, :, :].bitcast(F32),
                                            ALU.subtract).then_inc(w_tail_done, 1)
                rolled(dve, 1, 2, NT, step, tail=1)

            @block.tensor
            def _(pe):
                def step(j, v):
                    t = 2 * j + v
                    first = isinstance(t, int) and t == 0
                    pe.wait_ge(normed, t + 1)
                    if not first:
                        pe.wait_ge(tail_done, NC * t)
                    for c in range(NC):
                        for s in range(NS):
                            last = nc.tensor.transpose(u_ps[:, c, P * s:P * (s + 1)], uh[:, s, P * c:P * (c + 1)], ident[:, :])
                        last.then_inc(transposed, 1)
                    for k in range(NOUT):
                        if first and k % 4 == 0:
                            pe.wait_ge(w_tail_done, k // 4 + 1)
                        if k >= 4:
                            if k < 9:
                                pe.wait_ge(split, 10 * t + k - 3)
                            elif k < 12:
                                pe.wait_ge(split, 10 * t + k - 3)
                        elif not first:
                            if k % 2:
                                pe.wait_ge(split, 10 * (t - 1) + (9 if k == 1 else 10))
                            else:
                                pe.wait_ge(copied, 10 * (t - 1) + (9 if k == 0 else 10))
                        out = o_ps[:, k % 4, :]
                        for c in range(NC):
                            if k == 0:
                                pe.wait_ge(tail_done, NC * t + c + 1)
                            if k < 8:
                                cols, n = slice(P * (k % 4), P * (k % 4 + 1)), k // 4
                                last = products3(nc, out, heads[n][:, c, cols], tails[n][:, c, cols], u_head[:, c, :],
                                                 u_tail[:, c, :], c == 0, c == NC - 1)
                            else:
                                cols = slice(P * (k - 8), P * (k - 7))
                                last = products3(nc, out, u_head[:, c, cols], u_tail[:, c, cols], heads[2][:, c, :],
                                                 tails[2][:, c, :], c == 0, c == NC - 1)
                        last.then_inc(out_ready, 1)

                rolled(pe, 1, 2, NT, step)




def stage5(nc, d, persist):
    G = HEADS // 4
    ITS = BATCH * G
    NB = SEQ // P
    QK = 3 * HD
    HALF = 512
    PARTS = [(0, k) for k in range(NB)] + [(1, k) for k in range(NB // 2)]
    NSTEP = len(PARTS)
    ENDS = [NB, NSTEP]
    LAST = 2
    ADDS = [k for k in range(NSTEP) if PARTS[k][1] and k < ENDS[PARTS[k][0]] - LAST]
    NADD = len(ADDS)
    LATE = [(hh, i, HALF, P * (i + 1) - HALF, NB // 2 + i) for hh in range(4) for i in range(NB // 2, NB)]
    SCORES = LATE + [(hh, i, 0, HALF, i) for hh in range(4) for i in range(NB // 2, NB)]
    NSCORE0 = len(SCORES)
    SCORES += [(hh, i, 0, P * (i + 1), i) for hh in range(4) for i in range(NB // 2)]
    NSCORE = len(SCORES)
    COUNTS = [4, 4, 4, 4, 6, 6, 4, 0, 8, 8, 0, 0]
    MAXIMA_STEPS = [8, 10]
    END_STEP = 10
    ROWS_STEP = 10
    assert sum(COUNTS) == NSCORE and sum(COUNTS[:MAXIMA_STEPS[0]]) == NSCORE0
    MAXIMA_USE = [sum(COUNTS[:k + 1]) + n + 1 for n, k in enumerate(MAXIMA_STEPS)]

    def base(part):
        return HALF * (1 - part)

    def lo(part, blk):
        return max(0, P * blk - base(part))

    def end_columns(k):
        left = ENDS[PARTS[k][0]] - k
        start = P * sum(range(left + 1, LAST + 1))
        return start, start + P * left

    def diagonal(part, blk):
        return P * blk >= base(part)

    def ring_uses(k, v, first, last):
        uses = []
        if not last:
            uses += [("score", s) for s in range(sum(COUNTS[:k]), sum(COUNTS[:k + 1]))]
            if k in MAXIMA_STEPS:
                uses.append(("maxima", MAXIMA_STEPS.index(k)))
        if k == ROWS_STEP and not first and v % G == 0:
            uses += [("rows", i) for i in range(NB)]
        return uses

    USES = NSCORE + 2
    PERIOD = G * USES + NB

    def before(j, v):
        if v == 0:
            return USES
        return 2 * USES + PERIOD * j + USES * (v - 1) + NB * ((v - 1) // G)

    def parity(v):
        return before(0, v) % 2

    def kinds(j, v):
        return isinstance(j, int) and v == 0, isinstance(j, int) and v == ITS - 1

    with ExitStack() as ctx:
        sb = lambda name, shape, dt=F32: ctx.enter_context(nc.sbuf_tensor("s5_" + name, shape, dt))
        ps = lambda name, shape, dt=F32: ctx.enter_context(nc.psum_tensor("s5_" + name, shape, dt))
        sem = lambda name: ctx.enter_context(nc.semaphore("s5_" + name))
        q_st = sb("q_stack", [P, 2, 2, 4, HALF], F32R)
        k_st = sb("k_stack", [P, 2, 4, SEQ], F32R)
        v_in = sb("v_rows", [P, 2, NB, P])
        prob = sb("prob", [P, 2, 4, HALF])
        prob_end = sb("prob_end", [P, 2, 4, P * LAST * (LAST + 1) // 2])
        row_sum = sb("row_sum", [P, 2, 4, HALF])
        y_head = sb("y_head", [P, G, SEQ], F32R)
        y_tail = sb("y_tail", [P, G, SEQ], F32R)
        x_rows = sb("x_rows", [P, NB, DM])
        o_head = sb("o_head", [P, NC, DM], F32R)
        o_tail = sb("o_tail", [P, NC, DM], F32R)
        ones = sb("ones", [P, HD])
        ident = sb("ident", [P, P], BF16)
        mask_q = sb("mask_q", [P, P], BF16)
        mask_k = sb("mask_k", [P, P], BF16)
        mx = sb("mx", [P, 4, 3 * NB // 2])
        nm = sb("nm", [P, 2, 8, 4, NB // 2], F32R)
        nm_t = sb("nm_t", [4 * NB, 2, P], F32R)
        rec = sb("rec", [P, HALF])
        yn = sb("yn", [P, 2, HALF])
        s_ps = ps("s_ps", [P, 2, HALF])
        e_ps = ps("e_ps", [P, 4, HALF])
        y_ps = ps("y_ps", [P, 2, HALF])

        qk_loaded = [[sem(f"qk_loaded{part}{u}") for u in range(2)] for part in range(2)]
        v_loaded = [sem("v_loaded0"), sem("v_loaded1")]
        maxima_loaded = [sem("maxima_loaded0"), sem("maxima_loaded1")]
        w_loaded, w_head_done, w_tail_done, made, ones_rows = (
            sem("w_loaded"), sem("w_head"), sem("w_tail"), sem("made"), sem("ones_rows"))
        x_loaded, stored = sem("x_loaded"), sem("stored")
        ring_ready, ring_free = sem("ring_ready"), sem("ring_free")
        max_done, negated = sem("max"), sem("negated")
        e_ready, exp_done = sem("e_ready"), sem("exp")
        av_done, added = sem("av"), sem("added")
        sum_ready, rec_done = sem("sum_ready"), sem("rec")
        y_out, yn_done, yh_done, yt_done = sem("y_out"), sem("yn"), sem("y_head"), sem("y_tail")

        def probabilities(k, hh):
            part, blk = PARTS[k]
            if blk == 0:
                return row_sum[:, part, hh, :]
            if k in ADDS:
                return prob[:, k % 2, hh, 0:HALF - lo(part, blk)]
            start, end = end_columns(k)
            return prob_end[:, part, hh, start:end]

        with nc.Block() as block:
            @block.sync
            def _(sp):
                def load(j, v, part):
                    b, g, u = j + v // G, v % G, v % 2
                    tok, blocks = slice(base(part), base(part) + HALF), slice(base(part) // P, base(part) // P + NB // 2)
                    stacks = (("q_s", q_st[:, u, part], (0, 1, 0)), ("k_s", k_st[:, u, :, tok], (0, 0, 1)))
                    for name, stack, order in stacks:
                        src = d[name].rearrange("b g a (h e) t -> b g a e h t", h=4)
                        for n, a in enumerate(order):
                            sp.dma_start(stack[HD * n:HD * (n + 1)].bitcast(F32), src[b, g, a, :, :, tok]).then_inc(qk_loaded[part][u], 16)
                    src = d["v_s"].rearrange("(b k p) (g c) -> b g p k c", b=BATCH, p=P, g=G)
                    sp.dma_start(v_in[:, u, blocks], src[b, g, :, blocks]).then_inc(v_loaded[u], 16)

                def maxima(j, v, part, uses):
                    sp.wait_ge(ring_free, uses + MAXIMA_USE[part] + 2)
                    for a in range(2):
                        queries = q_st[QK + a:QK + a + 1, v % 2, part].bitcast(F32)
                        sp.dma_start(queries.rearrange("a h (k t) -> a (h k) t", t=P),
                                     nm_t[2 * NB * a:2 * NB * (a + 1), part, :].bitcast(F32)).then_inc(maxima_loaded[part], 16)

                rows_of = lambda name: d[name].rearrange("(b k p) c -> b p k c", b=BATCH, p=P)
                sp.sem_inc(stored, 16)
                load(0, 0, 0)
                load(0, 0, 1)
                sp.dma_start(x_rows[:, 0:NC, :], d["wp"].rearrange("(c p) m -> p c m", p=P)).then_inc(w_loaded, 16)
                load(0, 1, 0)
                for part in range(2):
                    maxima(0, 0, part, (NSCORE0 + 1, NSCORE + 2)[part] - MAXIMA_USE[part])

                def store(b, uses):
                    sp.wait_ge(ring_free, uses + 2)
                    sp.sem_inc(persist["passed"], 1)
                    sp.dma_start(rows_of("out")[b], x_rows[:, :, :]).then_inc(stored, 16)

                def step(j, v):
                    first, last = kinds(j, v)
                    it, b = G * j + v, j + v // G
                    rows = v % G == 0 and not first
                    if not last:
                        if not first:
                            sp.wait_ge(av_done, NSTEP * it)
                            sp.sem_inc(persist["passed"], 1)
                        load(j, v + 1, 1)
                        maxima(j, v + 1, 0, before(j, v))
                        if not (isinstance(j, int) and v == ITS - 2):
                            sp.wait_ge(av_done, NSTEP * it + ENDS[0])
                            sp.sem_inc(persist["passed"], 1)
                            load(j, v + 2, 0)
                        maxima(j, v + 1, 1, before(j, v))
                    if rows:
                        store(b - 1, before(j, v) + USES + NB)
                    if v % G == G - 1:
                        sp.wait_ge(w_tail_done, 1)
                        sp.wait_ge(stored, 16 * (b + 1))
                        sp.sem_inc(persist["passed"], 1)
                        sp.dma_start(x_rows[:, :, :], rows_of("x1_s")[b]).then_inc(x_loaded, 16)

                rolled(sp, 1, G, ITS, step, tail=1)
                store(BATCH - 1, before(0, ITS - 1) + NB)
                sp.wait_ge(stored, 16 * (BATCH + 1))

            @block.gpsimd
            def _(pool):
                nc.gpsimd.memset(ident[:, :], 0.0).then_inc(made, 1)
                nc.gpsimd.memset(mask_q[:, :], 0.0).then_inc(made, 1)
                nc.gpsimd.memset(mask_k[:, :], 0.0).then_inc(made, 1)
                nc.gpsimd.memset(ones[:, :], 1.0).then_inc(made, 1)
                pool.wait_ge(made, 4)
                nc.gpsimd.affine_select(out=ident[:, :], in_=ident[:, :], compare_op=ALU.not_equal, fill=1.0, base=0,
                                        pattern=[[-1, P]], channel_multiplier=1).then_inc(made, 1)
                nc.gpsimd.affine_select(out=mask_q[:, :], in_=mask_q[:, :], compare_op=ALU.is_ge, fill=-1e30, base=0,
                                        pattern=[[-1, P]], channel_multiplier=1).then_inc(made, 1)
                nc.gpsimd.affine_select(out=mask_k[:, :], in_=mask_k[:, :], compare_op=ALU.is_ge, fill=-1e30, base=0,
                                        pattern=[[1, P]], channel_multiplier=-1).then_inc(made, 1)

                def step(j, v):
                    it = G * j + v
                    for n, k in enumerate(ADDS):
                        part, blk = PARTS[k]
                        pool.wait_ge(exp_done, 4 * (NSTEP * it + k + 1))
                        if blk == 1:
                            pool.wait_ge(av_done, NSTEP * it + k)
                        else:
                            pool.wait_ge(added, NADD * it + n)
                        acc = row_sum[:, part, :, lo(part, blk):HALF]
                        nc.gpsimd.tensor_tensor(acc, acc, prob[:, k % 2, :, 0:HALF - lo(part, blk)], ALU.add).then_inc(added, 1)

                rolled(pool, 1, G, ITS, step, tail=1)

            @block.scalar
            def _(act):
                act.wait_ge(w_loaded, 16)
                nc.scalar.activation(o_head[:, :, :], x_rows[:, 0:NC, :], ACT.Copy).then_inc(w_head_done, 1)

                def bring_out(j, v, part):
                    it = G * j + v
                    first, _ = kinds(j, v)
                    act.wait_ge(av_done, NSTEP * it + ENDS[part])
                    if not first:
                        act.wait_ge(yt_done, 2 * it - 1 + part)
                    nc.scalar.activation(yn[:, part], y_ps[:, part], ACT.Copy).then_inc(y_out, 1)

                def head(j, v, part):
                    act.wait_ge(yn_done, 2 * (G * j + v) + part + 1)
                    nc.scalar.activation(y_head[:, v % G, base(part):base(part) + HALF], yn[:, part], ACT.Copy).then_inc(yh_done, 1)

                def step(j, v):
                    it = G * j + v
                    first, _ = kinds(j, v)
                    for k, (part, blk) in enumerate(PARTS):
                        c = lo(part, blk)
                        if blk == 0:
                            if not first:
                                act.wait_ge(sum_ready, 2 * it - 1 + part)
                        elif k in ADDS:
                            before_k = [m for m in ADDS if m < k and m % 2 == k % 2]
                            if before_k:
                                act.wait_ge(av_done, NSTEP * it + before_k[-1] + 1)
                                act.wait_ge(added, NADD * it + ADDS.index(before_k[-1]) + 1)
                            elif not first:
                                act.wait_ge(av_done, NSTEP * (it - 1) + ADDS[-1] + 1)
                                act.wait_ge(added, NADD * it)
                        for hh in range(4):
                            act.wait_ge(e_ready, 4 * (NSTEP * it + k) + hh + 1)
                            nc.scalar.activation(probabilities(k, hh), e_ps[:, hh, c:HALF], ACT.Exp).then_inc(exp_done, 1)
                        if k == 1 and not first:
                            bring_out(j, v - 1, 1)
                            head(j, v - 1, 0)
                        if k == 8:
                            bring_out(j, v, 0)
                        if k == 9 and not first:
                            head(j, v - 1, 1)

                rolled(act, 1, G, ITS, step, tail=1)
                bring_out(0, ITS - 1, 1)
                head(0, ITS - 1, 0)
                head(0, ITS - 1, 1)

            @block.vector
            def _(dve):
                dve.sem_inc(ring_free, 2)
                nc.vector.memset(nm[:, :, 2:8, :, :].bitcast(F32), 0.0).then_inc(ones_rows, 1)
                nc.vector.memset(k_st[QK:QK + 2, :, :, :].bitcast(F32), 1.0).then_inc(ones_rows, 1)

                def maximum(s, n, bank):
                    hh, blk, key, keys, slot = SCORES[s]
                    dve.wait_ge(ring_ready, n + 1)
                    nc.vector.reduce_max(mx[:, hh, slot:slot + 1], s_ps[:, bank, 0:keys], axis=AX_X).then_inc(ring_free, 1)

                def negate(it, part, n):
                    dve.wait_ge(ring_free, n + 2)
                    if part == 0:
                        late = mx[:, :, NB // 2:NB]
                        nc.vector.tensor_tensor(late, late, mx[:, :, NB:3 * NB // 2], ALU.max).then_inc(max_done, 1)
                        dve.wait_ge(max_done, it + 1)
                    own = mx[:, :, base(part) // P:base(part) // P + NB // 2]
                    nc.vector.tensor_scalar(nm[:, part, 0], own, -1.0, None, ALU.mult).then_inc(negated, 1)
                    dve.wait_ge(negated, 4 * it + 2 * part + 1)
                    nc.vector.scalar_tensor_tensor(nm[:, part, 1], own, -1.0, nm[:, part, 0].bitcast(F32),
                                                   ALU.mult, ALU.subtract).then_inc(negated, 1)

                def copy_maxima(it, part, n, bank):
                    dve.wait_ge(ring_ready, n + 1)
                    if not (isinstance(it, int) and it == 0):
                        dve.wait_ge(maxima_loaded[part], 32 * it)
                    nc.vector.tensor_copy(nm_t[:, part, :], s_ps[0:4 * NB, bank, 0:P]).then_inc(ring_free, 1)

                def reciprocals(j, v, part, cols):
                    it = G * j + v
                    first, _ = kinds(j, v)
                    if cols.start == 0:
                        dve.wait_ge(sum_ready, 2 * it + part + 1)
                        if not (first and part == 0):
                            dve.wait_ge(yn_done, 2 * it + part)
                    last = nc.vector.reciprocal(rec[:, cols], y_ps[:, part, cols])
                    if cols.stop == HALF:
                        last.then_inc(rec_done, 1)

                def normalise(j, v, part):
                    it = G * j + v
                    dve.wait_ge(rec_done, 2 * it + part + 1)
                    dve.wait_ge(y_out, 2 * it + part + 1)
                    nc.vector.tensor_tensor(yn[:, part], yn[:, part], rec[:, :], ALU.mult).then_inc(yn_done, 1)

                def tail(j, v, part):
                    dve.wait_ge(yh_done, 2 * (G * j + v) + part + 1)
                    cols = slice(base(part), base(part) + HALF)
                    nc.vector.tensor_tensor(y_tail[:, v % G, cols], yn[:, part], y_head[:, v % G, cols].bitcast(F32),
                                            ALU.subtract).then_inc(yt_done, 1)

                def add_rows(b, i, n, bank):
                    dve.wait_ge(x_loaded, 16 * (b + 1))
                    dve.wait_ge(ring_ready, n + 1)
                    nc.vector.tensor_tensor(x_rows[:, i, :], x_rows[:, i, :], s_ps[:, bank, :], ALU.add).then_inc(ring_free, 1)

                n = 0
                for part in range(2):
                    for s in (range(NSCORE0) if part == 0 else range(NSCORE0, NSCORE)):
                        maximum(s, n, n % 2)
                        n += 1
                    negate(0, part, n)
                    copy_maxima(0, part, n, n % 2)
                    n += 1
                dve.wait_ge(w_head_done, 1)
                nc.vector.tensor_tensor(o_tail[:, :, :], x_rows[:, 0:NC, :], o_head[:, :, :].bitcast(F32),
                                        ALU.subtract).then_inc(w_tail_done, 1)

                def step(j, v):
                    it, n, bank = G * j + v, before(j, v), parity(v)
                    first, last = kinds(j, v)
                    for k in range(NSTEP):
                        if k == 2 and not first:
                            tail(j, v - 1, 0)
                        if 4 <= k < 8 and not first:
                            reciprocals(j, v - 1, 1, slice(P * (k - 4), P * (k - 3)))
                        if k == 7 and not first:
                            normalise(j, v - 1, 1)
                        if k == END_STEP and not first:
                            tail(j, v - 1, 1)
                        uses = ring_uses(k, v, first, last)
                        for kind, arg in uses:
                            if kind == "rows":
                                add_rows(j + v // G - 1, arg, n, bank)
                            elif kind == "score":
                                if arg == 0:
                                    dve.wait_ge(negated, 4 * it + 4)
                                maximum(arg, n, bank)
                            else:
                                copy_maxima(it + 1, arg, n, bank)
                            n, bank = n + 1, 1 - bank
                        if k + 1 in MAXIMA_STEPS and not last:
                            negate(it + 1, MAXIMA_STEPS.index(k + 1), n)
                        if k == END_STEP:
                            reciprocals(j, v, 0, slice(0, HALF))
                            normalise(j, v, 0)

                rolled(dve, 1, G, ITS, step, tail=1)
                reciprocals(0, ITS - 1, 1, slice(0, HALF))
                normalise(0, ITS - 1, 1)
                tail(0, ITS - 1, 0)
                tail(0, ITS - 1, 1)
                n = before(0, ITS - 1)
                for i in range(NB):
                    add_rows(BATCH - 1, i, n + i, (n + i) % 2)

            @block.tensor
            def _(pe):
                def score(j, v, s, n, bank):
                    hh, blk, key, keys, _ = SCORES[s]
                    u, on_diagonal = v % 2, key + keys == P * (blk + 1)
                    part = 0 if blk >= NB // 2 else 1
                    queries = slice(P * blk - base(part), P * (blk + 1) - base(part))
                    if s in (0, len(LATE)):
                        pe.wait_ge(qk_loaded[1 if s else 0][u], 96 * (2 * j + v // 2 + 1))
                    pe.wait_ge(ring_free, n + 1)
                    last = nc.tensor.matmul(s_ps[:, bank, 0:keys], q_st[0:QK, u, part, hh, queries], k_st[0:QK, u, hh, key:key + keys],
                                            start=True, stop=not on_diagonal)
                    if on_diagonal:
                        last = nc.tensor.matmul(s_ps[:, bank, keys - P:keys], ident[:, :], mask_q[:, :], start=False, stop=True)
                    last.then_inc(ring_ready, 1)

                def turn_maxima(it, part, n, bank):
                    pe.wait_ge(negated, 4 * it + 2 * part + 2)
                    pe.wait_ge(ring_free, n + 1)
                    nc.tensor.transpose(s_ps[:, bank, 0:P], nm[:, part].bitcast(F32).rearrange("p a h k -> p (a h k)"),
                                        persist["ident"][:, :]).then_inc(ring_ready, 1)

                def exponents(j, v, k, hh):
                    it, u, (part, blk) = G * j + v, v % 2, PARTS[k]
                    first, _ = kinds(j, v)
                    c = lo(part, blk)
                    if blk == 0 and hh == 0:
                        pe.wait_ge(maxima_loaded[part], 32 * (it + 1))
                    if not (first and k == 0):
                        pe.wait_ge(exp_done, 4 * (NSTEP * it + k) + hh - 3)
                    last = nc.tensor.matmul(e_ps[:, hh, c:HALF], k_st[0:QK + 2, u, hh, P * blk:P * (blk + 1)],
                                            q_st[0:QK + 2, u, part, hh, c:HALF],
                                            start=True, stop=not diagonal(part, blk))
                    if diagonal(part, blk):
                        last = nc.tensor.matmul(e_ps[:, hh, c:c + P], ident[:, :], mask_k[:, :], start=False, stop=True)
                    last.then_inc(e_ready, 1)

                def weigh(j, v, k):
                    it, u, (part, blk) = G * j + v, v % 2, PARTS[k]
                    first, _ = kinds(j, v)
                    c = lo(part, blk)
                    if k == 0:
                        pe.wait_ge(v_loaded[u], 32 * (2 * j + v // 2 + 1))
                    if blk == 0 and not first:
                        pe.wait_ge(rec_done, 2 * it - 1 + part)
                    pe.wait_ge(exp_done, 4 * (NSTEP * it + k + 1))
                    for hh in range(4):
                        last = nc.tensor.matmul(y_ps[HD * hh:HD * (hh + 1), part, c:HALF], v_in[:, u, blk, HD * hh:HD * (hh + 1)],
                                                probabilities(k, hh), start=blk == 0, stop=k + 1 == ENDS[part])
                    last.then_inc(av_done, 1)

                def total(j, v, part):
                    it = G * j + v
                    pe.wait_ge(added, NADD * it + sum(1 for k in ADDS if k < ENDS[part]))
                    pe.wait_ge(y_out, 2 * it + part + 1)
                    steps = range(ENDS[part] - LAST, ENDS[part])
                    for hh in range(4):
                        nc.tensor.matmul(y_ps[HD * hh:HD * (hh + 1), part, :], ones[:, :], row_sum[:, part, hh, :],
                                         start=True, stop=False)
                    for k in steps:
                        for hh in range(4):
                            last = nc.tensor.matmul(y_ps[HD * hh:HD * (hh + 1), part, lo(*PARTS[k]):HALF], ones[:, :],
                                                    probabilities(k, hh), start=False, stop=k == steps[-1])
                    last.then_inc(sum_ready, 1)

                def out_rows(its, i, n, bank):
                    pe.wait_ge(yt_done, 2 * its - (1 if i >= NB // 2 else 0))
                    pe.wait_ge(w_tail_done, 1)
                    pe.wait_ge(ring_free, n + 1)
                    tokens = slice(P * i, P * (i + 1))
                    for g in range(G):
                        last = products3(nc, s_ps[:, bank, :], y_head[:, g, tokens], y_tail[:, g, tokens], o_head[:, g, :],
                                         o_tail[:, g, :], g == 0, g == G - 1)
                    last.then_inc(ring_ready, 1)

                pe.wait_ge(made, 7)
                pe.wait_ge(ones_rows, 2)
                n = 0
                for part in range(2):
                    for s in (range(NSCORE0) if part == 0 else range(NSCORE0, NSCORE)):
                        score(0, 0, s, n, n % 2)
                        n += 1
                    turn_maxima(0, part, n, n % 2)
                    n += 1

                def step(j, v):
                    it, n, bank = G * j + v, before(j, v), parity(v)
                    first, last = kinds(j, v)
                    for k in range(NSTEP):
                        uses = ring_uses(k, v, first, last)
                        scores = [arg for kind, arg in uses if kind == "score"]
                        for hh in range(4):
                            exponents(j, v, k, hh)
                            for s in scores[len(scores) * hh // 4:len(scores) * (hh + 1) // 4]:
                                score(j, v + 1, s, n, bank)
                                n, bank = n + 1, 1 - bank
                        if k:
                            weigh(j, v, k - 1)
                        elif not first:
                            weigh(j, v - 1, NSTEP - 1)
                        for kind, arg in uses:
                            if kind == "rows":
                                out_rows(it, arg, n, bank)
                            elif kind == "maxima":
                                turn_maxima(it + 1, arg, n, bank)
                            if kind != "score":
                                n, bank = n + 1, 1 - bank
                        if k == 3 and not first:
                            total(j, v - 1, 1)
                        if k == END_STEP - 1:
                            total(j, v, 0)

                rolled(pe, 1, G, ITS, step, tail=1)
                weigh(0, ITS - 1, NSTEP - 1)
                total(0, ITS - 1, 1)
                n = before(0, ITS - 1)
                for i in range(NB):
                    out_rows(ITS, i, n + i, (n + i) % 2)


def build(nc, d):
    scratch = {"z_s": (BATCH, NC, P, SEQ), "x_s": (BATCH, P, SEQ), "B_s": (BATCH, P, SEQ), "C_s": (BATCH, NC, P, SEQ),
               "dt_s": (BATCH, NC, 2, P, SEQ), "dtx_s": (BATCH, NC, 2, P, SEQ), "y_s": (BATCH, NC, P, SEQ),
               "x1_s": (BATCH * SEQ, DM), "q_s": (BATCH, NC, 2, P, SEQ), "k_s": (BATCH, NC, 2, P, SEQ), "v_s": (BATCH * SEQ, DM)}
    for name, shape in scratch.items():
        d[name] = nc.dram_tensor(name, shape, F32).ap()
    with ExitStack() as ctx:
        ident = ctx.enter_context(nc.sbuf_tensor("ident", [P, P], F32))
        mean_all = ctx.enter_context(nc.sbuf_tensor("mean_all", [P, NT * NS], F32))
        rstd_all = ctx.enter_context(nc.sbuf_tensor("rstd_all", [P, NT * NS], F32))
        ident_ready = ctx.enter_context(nc.semaphore("ident_ready"))
        passed = ctx.enter_context(nc.semaphore("passed"))
        persist = dict(passed=passed, ident=ident, mean_all=mean_all, rstd_all=rstd_all, ident_ready=ident_ready)
        with nc.Block() as block:
            @block.gpsimd
            def _(pool):
                nc.gpsimd.memset(ident[:, :], 0.0).then_inc(ident_ready, 1)
                pool.wait_ge(ident_ready, 1)
                nc.gpsimd.affine_select(out=ident[:, :], in_=ident[:, :], compare_op=ALU.not_equal, fill=1.0, base=0,
                                        pattern=[[-1, P]], channel_multiplier=1).then_inc(ident_ready, 1)
        for stage in STAGES:
            stage(nc, d, persist)


STAGES = [stage1, stage2, stage3, stage4, stage5]


def kernel(L0_attn_hidden_states, L0_attn_in_proj_w, L0_attn_dt_proj_w, L0_attn_dt_proj_b, L0_attn_A_log, L0_attn_D_param,
           L0_attn_out_proj_w, L0_attn_gate_w, L0_attn_up_w, L0_attn_down_w, L0_attn_norm1_w, L0_attn_norm2_w, L0_ffn_Wa,
           L0_ffn_Wp, L0_ffn_w_std, L0_ffn_w_rec):
    import concourse.bacc as bacc
    import numpy as np
    from concourse.bass_utils import run_bass_kernel_spmd

    def transposed(w):
        return np.ascontiguousarray(np.asarray(w).T)

    def blocks(w):
        return transposed(np.asarray(w).reshape(NC, P))

    wa, std = np.asarray(L0_ffn_Wa), HD - 8
    ends = np.cumsum([HEADS * std, HEADS * std, DM, HEADS * 8])
    q_std, k_std, v_cols, q_low, k_low = np.split(wa, ends, axis=1)

    def by_head(a, b):
        parts = [a.reshape(DM, HEADS, std), b.reshape(DM, HEADS, 8)]
        return np.ascontiguousarray(np.concatenate(parts, axis=2).reshape(DM, DM))

    arrays = {
        "x": np.ascontiguousarray(np.asarray(L0_attn_hidden_states).reshape(BATCH * SEQ, DM)),
        "in_w": transposed(L0_attn_in_proj_w), "dt_w": transposed(L0_attn_dt_proj_w),
        "norm1": blocks(L0_attn_norm1_w), "norm2": blocks(L0_attn_norm2_w),
        "dt_b": blocks(L0_attn_dt_proj_b), "D": blocks(L0_attn_D_param),
        "A_log": np.ascontiguousarray(np.asarray(L0_attn_A_log).reshape(NC, REP, 8, P).transpose(3, 0, 2, 1).reshape(P, P)),
        "out_w": transposed(L0_attn_out_proj_w), "gate_w": transposed(L0_attn_gate_w),
        "up_w": transposed(L0_attn_up_w), "down_w": transposed(L0_attn_down_w),
        "wq": by_head(q_std, q_low), "wk": by_head(k_std, k_low), "wv": np.ascontiguousarray(v_cols),
        "wp": np.ascontiguousarray(np.asarray(L0_ffn_Wp)),
        "w_std": np.ascontiguousarray(np.asarray(L0_ffn_w_std)), "w_rec": np.ascontiguousarray(np.asarray(L0_ffn_w_rec)),
    }
    nc = bacc.Bacc("TRN2", target_bir_lowering=False, num_devices=1)
    d = {name: nc.dram_tensor(name, a.shape, F32, kind="ExternalInput").ap() for name, a in arrays.items()}
    d["out"] = nc.dram_tensor("out", (BATCH * SEQ, DM), F32, kind="ExternalOutput").ap()
    build(nc, d)
    nc.compile()
    result = run_bass_kernel_spmd(nc, [arrays], core_ids=[0])
    return np.asarray(result.results[0]["out"]).reshape(BATCH, SEQ, DM)
```
